# Optimizing a Trainium2 kernel written in Bass

```python
import numpy as np
import jax
import jax.numpy as jnp

def _softmax(x, axis=-1):
    return jax.nn.softmax(x, axis=axis)

def _gelu(x):
    return jax.nn.gelu(x, approximate=True)

def _silu(x):
    return jax.nn.silu(x)

def _sigmoid(x):
    return jax.nn.sigmoid(x)

def _layernorm(x, axis=-1, eps=1e-05):
    m = jnp.mean(x, axis=axis, keepdims=True)
    v = jnp.var(x, axis=axis, keepdims=True)
    return (x - m) / jnp.sqrt(v + eps)

def _scatter_add(tgt, idx, src, axis=0):
    return tgt.at[idx].add(src)

def _segment_sum(src, seg, n):
    return jax.ops.segment_sum(src, seg, n)
kernel_name = 'mk_adaln_d2_jaxref_r4_db19cf'

def setup_inputs(seed: int=0):
    np.random.seed(seed)
    _w = jnp.asarray

    def _L0_attn_setup():
        import jax, jax.numpy as jnp
        import numpy as np
        B, T, E, H = (8, 512, 256, 256)
        _LN_EPS = 0.001

        def _ln(x, g, b):
            mu = jnp.mean(x, axis=-1, keepdims=True)
            var = jnp.var(x, axis=-1, keepdims=True)
            return (x - mu) * jax.lax.rsqrt(var + _LN_EPS) * g + b

        def _time_shift(x):
            return jnp.pad(x[:, :-1], ((0, 0), (1, 0), (0, 0)))

        def _wkv(k, v, w, u):
            Bk, Tk, Hk = k.shape

            def step(carry, kv_t):
                aa, bb, pp = carry
                kt, vt = kv_t
                ww = u + kt
                q = jnp.maximum(pp, ww)
                e1 = jnp.exp(pp - q)
                e2 = jnp.exp(ww - q)
                out = (e1 * aa + e2 * vt) / (e1 * bb + e2)
                ww2 = pp + w
                q2 = jnp.maximum(ww2, kt)
                e1b = jnp.exp(ww2 - q2)
                e2b = jnp.exp(kt - q2)
                return ((e1b * aa + e2b * vt, e1b * bb + e2b, q2), out)
            init = (jnp.zeros((Bk, Hk), k.dtype), jnp.zeros((Bk, Hk), k.dtype), jnp.full((Bk, Hk), -1e+38, k.dtype))
            kT = jnp.swapaxes(k, 0, 1)
            vT = jnp.swapaxes(v, 0, 1)
            _, outs = jax.lax.scan(step, init, (kT, vT))
            return jnp.swapaxes(outs, 0, 1)
        key = jax.random.key(seed)
        ks = jax.random.split(key, 20)

        def glorot(k, shape):
            lim = np.sqrt(6.0 / (shape[0] + shape[1]))
            return jax.random.uniform(k, shape, jnp.float32, -lim, lim)
        return {'inputs': jax.random.normal(ks[0], (B, T, E), jnp.float32), 'ln1_g': jnp.ones((E,), jnp.float32), 'ln1_b': jnp.zeros((E,), jnp.float32), 'ln2_g': jnp.ones((E,), jnp.float32), 'ln2_b': jnp.zeros((E,), jnp.float32), 'tm_mix_k': jax.random.uniform(ks[1], (E,), jnp.float32, 0.0, 2.0 / E), 'tm_mix_v': jax.random.uniform(ks[2], (E,), jnp.float32, 0.0, 2.0 / E), 'tm_mix_r': jax.random.uniform(ks[3], (E,), jnp.float32, 0.0, (2.0 / E) ** 0.5), 'tm_Wk': glorot(ks[4], (E, H)), 'tm_Wv': glorot(ks[5], (E, H)), 'tm_Wr': glorot(ks[6], (E, H)), 'time_decay': jax.random.uniform(ks[7], (H,), jnp.float32, 0.0, 0.5), 'time_first': jax.random.uniform(ks[8], (H,), jnp.float32, 0.0, 0.05), 'Wo': glorot(ks[9], (H, E)), 'cm_mix_k': jax.random.uniform(ks[10], (E,), jnp.float32, 0.0, 2.0 / E), 'cm_mix_r': jax.random.uniform(ks[11], (E,), jnp.float32, 0.0, 2.0 / E), 'cm_Wk': glorot(ks[12], (E, 4 * H)), 'cm_Wv': glorot(ks[13], (4 * H, E)), 'cm_Wr': glorot(ks[14], (E, E))}
    _L0_attn_in = _L0_attn_setup()

    def _L0_ffn_setup():
        import jax, jax.numpy as jnp
        import numpy as np
        DIM = 256
        DEPTH = 2
        HEADS = 8
        DIM_HEAD = 64
        WINDOW = 128
        INNER = HEADS * DIM_HEAD
        HID = int(DIM * 4 * 2 / 3)
        B, N = (2, 2048)
        QK_SCALE = 8.0

        def shift_token(t):
            t1, t2 = jnp.split(t, 2, axis=-1)
            t2 = jnp.pad(t2, ((0, 0), (1, 0), (0, 0)))[:, :-1]
            return jnp.concatenate([t1, t2], axis=-1)

        def l2norm(t):
            return t / jnp.clip(jnp.linalg.norm(t, axis=-1, keepdims=True), 1e-12)

        def rotate_half(x):
            x1, x2 = jnp.split(x, 2, axis=-1)
            return jnp.concatenate([-x2, x1], axis=-1)

        def rotary_xpos(q, k):
            n = q.shape[-2]
            half_idx = jnp.arange(0, DIM_HEAD, 2, dtype=jnp.float32)
            inv_freq = 1.0 / 10000.0 ** (half_idx / DIM_HEAD)
            t = jnp.arange(n, dtype=jnp.float32)
            freqs = t[:, None] * inv_freq[None, :]
            freqs = jnp.concatenate([freqs, freqs], axis=-1)
            base = (half_idx + 0.4 * DIM_HEAD) / (1.4 * DIM_HEAD)
            power = (t - n // 2) / float(WINDOW // 2)
            scale = base[None, :] ** power[:, None]
            scale = jnp.concatenate([scale, scale], axis=-1)
            cos, sin = (jnp.cos(freqs), jnp.sin(freqs))
            q = q * cos * scale + rotate_half(q) * sin * scale
            k = k * cos / scale + rotate_half(k) * sin / scale
            return (q, k)

        def local_attention(q, k, v):
            b, h, n, d = q.shape
            w = n // WINDOW
            bq = q.reshape(b, h, w, WINDOW, d) * QK_SCALE
            bk = k.reshape(b, h, w, WINDOW, d)
            bv = v.reshape(b, h, w, WINDOW, d)

            def look_around(t):
                p = jnp.pad(t, ((0, 0), (0, 0), (1, 0), (0, 0), (0, 0)))
                return jnp.concatenate([p[:, :, :w], p[:, :, 1:]], axis=3)
            bk, bv = (look_around(bk), look_around(bv))
            bt = jnp.arange(n).reshape(w, WINDOW)
            btp = jnp.pad(bt, ((1, 0), (0, 0)), constant_values=-1)
            btk = jnp.concatenate([btp[:w], btp[1:]], axis=1)
            sim = jnp.einsum('bhwid,bhwjd->bhwij', bq, bk)
            i = bt[:, :, None]
            j = btk[:, None, :]
            mask = (i < j) | (i > j + WINDOW) | (j == -1)
            sim = jnp.where(mask, -jnp.finfo(sim.dtype).max, sim)
            attn = jax.nn.softmax(sim, axis=-1)
            out = jnp.einsum('bhwij,bhwjd->bhwid', attn, bv)
            return out.reshape(b, h, n, d)

        def _layer(x, wqkv, qs, ksc, wo, lg, lb, w1, b1, w2, b2):
            b, n, _ = x.shape
            h = shift_token(x)
            qkv = h @ wqkv
            q, k, v = jnp.split(qkv, 3, axis=-1)
            to_heads = lambda t: t.reshape(b, n, HEADS, DIM_HEAD).transpose(0, 2, 1, 3)
            q, k, v = (to_heads(q), to_heads(k), to_heads(v))
            q = l2norm(q) * qs
            k = l2norm(k) * ksc
            q, k = rotary_xpos(q, k)
            o = local_attention(q, k, v)
            o = o.transpose(0, 2, 1, 3).reshape(b, n, INNER)
            x = x + o @ wo
            h = shift_token(x)
            mu = h.mean(-1, keepdims=True)
            var = h.var(-1, keepdims=True)
            h = (h - mu) / jnp.sqrt(var + 1e-05) * lg + lb
            h = h @ w1 + b1
            a, g = jnp.split(h, 2, axis=-1)
            h = a * jax.nn.gelu(g, approximate=False)
            x = x + h @ w2 + b2
            return x
        key = jax.random.key(seed)
        ks = jax.random.split(key, 6)
        return {'x': jax.random.normal(ks[0], (B, N, DIM), jnp.float32), 'wqkv': jax.random.normal(ks[1], (DEPTH, DIM, 3 * INNER), jnp.float32) * 0.02, 'q_scale': jnp.ones((DEPTH, DIM_HEAD), jnp.float32), 'k_scale': jnp.ones((DEPTH, DIM_HEAD), jnp.float32), 'wo': jax.random.normal(ks[2], (DEPTH, INNER, DIM), jnp.float32) * 0.02, 'ln_g': jnp.ones((DEPTH, DIM), jnp.float32), 'ln_b': jnp.zeros((DEPTH, DIM), jnp.float32), 'w1': jax.random.normal(ks[3], (DEPTH, DIM, 2 * HID), jnp.float32) * 0.02, 'b1': jnp.zeros((DEPTH, 2 * HID), jnp.float32), 'w2': jax.random.normal(ks[4], (DEPTH, HID, DIM), jnp.float32) * 0.02, 'b2': jnp.zeros((DEPTH, DIM), jnp.float32)}
    _L0_ffn_in = _L0_ffn_setup()
    _L0_c = _w((lambda *s: np.random.randn(*s).astype(np.float32) * 0.05)(1, 256))
    _L0_wmod = _w((lambda *s: np.random.randn(*s).astype(np.float32) * 0.05)(256, 6 * 256) * 256 ** (-0.5))

    def _L1_attn_setup():
        import jax, jax.numpy as jnp
        import numpy as np
        NL, H, N, B, L = (4, 256, 32, 8, 256)

        def _layernorm_channels(z, w, b):
            mu = jnp.mean(z, axis=1, keepdims=True)
            var = jnp.mean((z - mu) ** 2, axis=1, keepdims=True)
            zn = (z - mu) * jax.lax.rsqrt(var + 1e-05)
            return zn * w[None, :, None] + b[None, :, None]

        def _s4d_layer(z, log_dt, A_re_log, A_im, C_re, C_im, D_skip, W, bvec):
            Bz, Hh, Lz = z.shape
            dt = jnp.exp(log_dt)
            A = -jnp.exp(A_re_log) + 1j * A_im
            dtA = A * dt[:, None]
            C = (C_re + 1j * C_im) * (jnp.expm1(dtA) / A)
            l = jnp.arange(Lz, dtype=jnp.float32)
            K = 2.0 * jnp.einsum('hn,hnl->hl', C, jnp.exp(dtA[:, :, None] * l)).real
            kf = jnp.fft.rfft(K, n=2 * Lz)
            uf = jnp.fft.rfft(z, n=2 * Lz)
            y = jnp.fft.irfft(uf * kf, n=2 * Lz)[..., :Lz]
            y = y + z * D_skip[:, None]
            y = jax.nn.gelu(y)
            out = jnp.einsum('oh,bhl->bol', W, y) + bvec[None, :, None]
            return out[:, :Hh] * jax.nn.sigmoid(out[:, Hh:])
        key = jax.random.key(seed)
        ks = jax.random.split(key, 10)
        x = jax.random.normal(ks[0], (B, L, H), dtype=jnp.float32)
        ln_w = jnp.ones((NL, H), jnp.float32)
        ln_b = jnp.zeros((NL, H), jnp.float32)
        log_dt = (jax.random.uniform(ks[1], (NL, H)) * (np.log(0.1) - np.log(0.001)) + np.log(0.001)).astype(jnp.float32)
        A_re_log = jnp.full((NL, H, N), np.log(0.5), jnp.float32)
        A_im = jnp.broadcast_to(np.pi * jnp.arange(N, dtype=jnp.float32), (NL, H, N))
        C_re = jax.random.normal(ks[2], (NL, H, N), jnp.float32) * 0.5 ** 0.5
        C_im = jax.random.normal(ks[3], (NL, H, N), jnp.float32) * 0.5 ** 0.5
        D_skip = jax.random.normal(ks[4], (NL, H), jnp.float32)
        W_out = jax.random.normal(ks[5], (NL, 2 * H, H), jnp.float32) * (1.0 / np.sqrt(H))
        b_out = jnp.zeros((NL, 2 * H), jnp.float32)
        return {'x': x, 'ln_w': ln_w, 'ln_b': ln_b, 'log_dt': log_dt, 'A_re_log': A_re_log, 'A_im': A_im, 'C_re': C_re, 'C_im': C_im, 'D_skip': D_skip, 'W_out': W_out, 'b_out': b_out}
    _L1_attn_in = _L1_attn_setup()

    def _L1_ffn_setup():
        import jax, jax.numpy as jnp
        import numpy as np
        D_IN, D_HID = (256, 1024)

        def _ternary(key, shape):
            return jax.random.randint(key, shape, -1, 2).astype(jnp.float32)

        def _tlin(x, w, s):
            return jnp.einsum('bsi,oi->bso', x, w) * s
        key = jax.random.key(seed)
        ks = jax.random.split(key, 12)
        inv = lambda fan: 1.0 / np.sqrt(fan).astype(np.float32)
        return {'x': jax.random.normal(ks[0], (4, 512, D_IN), dtype=jnp.float32), 'w1_w': _ternary(ks[1], (D_HID, D_IN)), 'w1_s': jax.random.uniform(ks[2], (D_HID,), dtype=jnp.float32) * inv(D_IN), 'w2_w': _ternary(ks[3], (D_HID, D_IN)), 'w2_s': jax.random.uniform(ks[4], (D_HID,), dtype=jnp.float32) * inv(D_IN), 'h1_w': _ternary(ks[5], (D_HID, D_HID)), 'h1_s': jax.random.uniform(ks[6], (D_HID,), dtype=jnp.float32) * inv(D_HID), 'h2_w': _ternary(ks[7], (D_HID, D_HID)), 'h2_s': jax.random.uniform(ks[8], (D_HID,), dtype=jnp.float32) * inv(D_HID), 'w3_w': _ternary(ks[9], (D_IN, D_HID)), 'w3_s': jax.random.uniform(ks[10], (D_IN,), dtype=jnp.float32) * inv(D_HID)}
    _L1_ffn_in = _L1_ffn_setup()
    _L1_c = _w((lambda *s: np.random.randn(*s).astype(np.float32) * 0.05)(1, 256))
    _L1_wmod = _w((lambda *s: np.random.randn(*s).astype(np.float32) * 0.05)(256, 6 * 256) * 256 ** (-0.5))
    _d = {'L0_attn_inputs': _L0_attn_in['inputs'], 'L0_attn_ln1_g': _L0_attn_in['ln1_g'], 'L0_attn_ln1_b': _L0_attn_in['ln1_b'], 'L0_attn_ln2_g': _L0_attn_in['ln2_g'], 'L0_attn_ln2_b': _L0_attn_in['ln2_b'], 'L0_attn_tm_mix_k': _L0_attn_in['tm_mix_k'], 'L0_attn_tm_mix_v': _L0_attn_in['tm_mix_v'], 'L0_attn_tm_mix_r': _L0_attn_in['tm_mix_r'], 'L0_attn_tm_Wk': _L0_attn_in['tm_Wk'], 'L0_attn_tm_Wv': _L0_attn_in['tm_Wv'], 'L0_attn_tm_Wr': _L0_attn_in['tm_Wr'], 'L0_attn_time_decay': _L0_attn_in['time_decay'], 'L0_attn_time_first': _L0_attn_in['time_first'], 'L0_attn_Wo': _L0_attn_in['Wo'], 'L0_attn_cm_mix_k': _L0_attn_in['cm_mix_k'], 'L0_attn_cm_mix_r': _L0_attn_in['cm_mix_r'], 'L0_attn_cm_Wk': _L0_attn_in['cm_Wk'], 'L0_attn_cm_Wv': _L0_attn_in['cm_Wv'], 'L0_attn_cm_Wr': _L0_attn_in['cm_Wr'], 'L0_ffn_wqkv': _L0_ffn_in['wqkv'], 'L0_ffn_q_scale': _L0_ffn_in['q_scale'], 'L0_ffn_k_scale': _L0_ffn_in['k_scale'], 'L0_ffn_wo': _L0_ffn_in['wo'], 'L0_ffn_ln_g': _L0_ffn_in['ln_g'], 'L0_ffn_ln_b': _L0_ffn_in['ln_b'], 'L0_ffn_w1': _L0_ffn_in['w1'], 'L0_ffn_b1': _L0_ffn_in['b1'], 'L0_ffn_w2': _L0_ffn_in['w2'], 'L0_ffn_b2': _L0_ffn_in['b2'], 'L0_c': _L0_c, 'L0_wmod': _L0_wmod, 'L1_attn_ln_w': _L1_attn_in['ln_w'], 'L1_attn_ln_b': _L1_attn_in['ln_b'], 'L1_attn_log_dt': _L1_attn_in['log_dt'], 'L1_attn_A_re_log': _L1_attn_in['A_re_log'], 'L1_attn_A_im': _L1_attn_in['A_im'], 'L1_attn_C_re': _L1_attn_in['C_re'], 'L1_attn_C_im': _L1_attn_in['C_im'], 'L1_attn_D_skip': _L1_attn_in['D_skip'], 'L1_attn_W_out': _L1_attn_in['W_out'], 'L1_attn_b_out': _L1_attn_in['b_out'], 'L1_ffn_w1_w': _L1_ffn_in['w1_w'], 'L1_ffn_w1_s': _L1_ffn_in['w1_s'], 'L1_ffn_w2_w': _L1_ffn_in['w2_w'], 'L1_ffn_w2_s': _L1_ffn_in['w2_s'], 'L1_ffn_h1_w': _L1_ffn_in['h1_w'], 'L1_ffn_h1_s': _L1_ffn_in['h1_s'], 'L1_ffn_h2_w': _L1_ffn_in['h2_w'], 'L1_ffn_h2_s': _L1_ffn_in['h2_s'], 'L1_ffn_w3_w': _L1_ffn_in['w3_w'], 'L1_ffn_w3_s': _L1_ffn_in['w3_s'], 'L1_c': _L1_c, 'L1_wmod': _L1_wmod}
    _x0 = _d['L0_attn_inputs']
    _d['L0_attn_inputs'] = jax.random.normal(jax.random.fold_in(jax.random.key(seed), 1), (1, 4096, 256), dtype=_x0.dtype)
    del _x0
    return _d

def reference(L0_attn_inputs, L0_attn_ln1_g, L0_attn_ln1_b, L0_attn_ln2_g, L0_attn_ln2_b, L0_attn_tm_mix_k, L0_attn_tm_mix_v, L0_attn_tm_mix_r, L0_attn_tm_Wk, L0_attn_tm_Wv, L0_attn_tm_Wr, L0_attn_time_decay, L0_attn_time_first, L0_attn_Wo, L0_attn_cm_mix_k, L0_attn_cm_mix_r, L0_attn_cm_Wk, L0_attn_cm_Wv, L0_attn_cm_Wr, L0_ffn_wqkv, L0_ffn_q_scale, L0_ffn_k_scale, L0_ffn_wo, L0_ffn_ln_g, L0_ffn_ln_b, L0_ffn_w1, L0_ffn_b1, L0_ffn_w2, L0_ffn_b2, L0_c, L0_wmod, L1_attn_ln_w, L1_attn_ln_b, L1_attn_log_dt, L1_attn_A_re_log, L1_attn_A_im, L1_attn_C_re, L1_attn_C_im, L1_attn_D_skip, L1_attn_W_out, L1_attn_b_out, L1_ffn_w1_w, L1_ffn_w1_s, L1_ffn_w2_w, L1_ffn_w2_s, L1_ffn_h1_w, L1_ffn_h1_s, L1_ffn_h2_w, L1_ffn_h2_s, L1_ffn_w3_w, L1_ffn_w3_s, L1_c, L1_wmod):

    def _L0_attn_ref(inputs, ln1_g, ln1_b, ln2_g, ln2_b, tm_mix_k, tm_mix_v, tm_mix_r, tm_Wk, tm_Wv, tm_Wr, time_decay, time_first, Wo, cm_mix_k, cm_mix_r, cm_Wk, cm_Wv, cm_Wr):
        import jax, jax.numpy as jnp
        import numpy as np
        B, T, E, H = (8, 512, 256, 256)
        _LN_EPS = 0.001

        def _ln(x, g, b):
            mu = jnp.mean(x, axis=-1, keepdims=True)
            var = jnp.var(x, axis=-1, keepdims=True)
            return (x - mu) * jax.lax.rsqrt(var + _LN_EPS) * g + b

        def _time_shift(x):
            return jnp.pad(x[:, :-1], ((0, 0), (1, 0), (0, 0)))

        def _wkv(k, v, w, u):
            Bk, Tk, Hk = k.shape

            def step(carry, kv_t):
                aa, bb, pp = carry
                kt, vt = kv_t
                ww = u + kt
                q = jnp.maximum(pp, ww)
                e1 = jnp.exp(pp - q)
                e2 = jnp.exp(ww - q)
                out = (e1 * aa + e2 * vt) / (e1 * bb + e2)
                ww2 = pp + w
                q2 = jnp.maximum(ww2, kt)
                e1b = jnp.exp(ww2 - q2)
                e2b = jnp.exp(kt - q2)
                return ((e1b * aa + e2b * vt, e1b * bb + e2b, q2), out)
            init = (jnp.zeros((Bk, Hk), k.dtype), jnp.zeros((Bk, Hk), k.dtype), jnp.full((Bk, Hk), -1e+38, k.dtype))
            kT = jnp.swapaxes(k, 0, 1)
            vT = jnp.swapaxes(v, 0, 1)
            _, outs = jax.lax.scan(step, init, (kT, vT))
            return jnp.swapaxes(outs, 0, 1)
        x = inputs
        h = _ln(x, ln1_g, ln1_b)
        h1 = _time_shift(h)
        xk = h * tm_mix_k + h1 * (1.0 - tm_mix_k)
        xv = h * tm_mix_v + h1 * (1.0 - tm_mix_v)
        xr = h * tm_mix_r + h1 * (1.0 - tm_mix_r)
        k = xk @ tm_Wk
        v = xv @ tm_Wv
        r = xr @ tm_Wr
        wkv = _wkv(k, v, -jnp.exp(time_decay), time_first)
        x = x + jax.nn.sigmoid(r) * wkv @ Wo
        h = _ln(x, ln2_g, ln2_b)
        h1 = _time_shift(h)
        xk = h * cm_mix_k + h1 * (1.0 - cm_mix_k)
        xr = h * cm_mix_r + h1 * (1.0 - cm_mix_r)
        kc = jnp.square(jax.nn.relu(xk @ cm_Wk))
        rc = jax.nn.sigmoid(xr @ cm_Wr)
        x = x + rc * (kc @ cm_Wv)
        return x

    def _L0_ffn_ref(x, wqkv, q_scale, k_scale, wo, ln_g, ln_b, w1, b1, w2, b2):
        import jax, jax.numpy as jnp
        import numpy as np
        DIM = 256
        DEPTH = 2
        HEADS = 8
        DIM_HEAD = 64
        WINDOW = 128
        INNER = HEADS * DIM_HEAD
        HID = int(DIM * 4 * 2 / 3)
        B, N = (2, 2048)
        QK_SCALE = 8.0

        def shift_token(t):
            t1, t2 = jnp.split(t, 2, axis=-1)
            t2 = jnp.pad(t2, ((0, 0), (1, 0), (0, 0)))[:, :-1]
            return jnp.concatenate([t1, t2], axis=-1)

        def l2norm(t):
            return t / jnp.clip(jnp.linalg.norm(t, axis=-1, keepdims=True), 1e-12)

        def rotate_half(x):
            x1, x2 = jnp.split(x, 2, axis=-1)
            return jnp.concatenate([-x2, x1], axis=-1)

        def rotary_xpos(q, k):
            n = q.shape[-2]
            half_idx = jnp.arange(0, DIM_HEAD, 2, dtype=jnp.float32)
            inv_freq = 1.0 / 10000.0 ** (half_idx / DIM_HEAD)
            t = jnp.arange(n, dtype=jnp.float32)
            freqs = t[:, None] * inv_freq[None, :]
            freqs = jnp.concatenate([freqs, freqs], axis=-1)
            base = (half_idx + 0.4 * DIM_HEAD) / (1.4 * DIM_HEAD)
            power = (t - n // 2) / float(WINDOW // 2)
            scale = base[None, :] ** power[:, None]
            scale = jnp.concatenate([scale, scale], axis=-1)
            cos, sin = (jnp.cos(freqs), jnp.sin(freqs))
            q = q * cos * scale + rotate_half(q) * sin * scale
            k = k * cos / scale + rotate_half(k) * sin / scale
            return (q, k)

        def local_attention(q, k, v):
            b, h, n, d = q.shape
            w = n // WINDOW
            bq = q.reshape(b, h, w, WINDOW, d) * QK_SCALE
            bk = k.reshape(b, h, w, WINDOW, d)
            bv = v.reshape(b, h, w, WINDOW, d)

            def look_around(t):
                p = jnp.pad(t, ((0, 0), (0, 0), (1, 0), (0, 0), (0, 0)))
                return jnp.concatenate([p[:, :, :w], p[:, :, 1:]], axis=3)
            bk, bv = (look_around(bk), look_around(bv))
            bt = jnp.arange(n).reshape(w, WINDOW)
            btp = jnp.pad(bt, ((1, 0), (0, 0)), constant_values=-1)
            btk = jnp.concatenate([btp[:w], btp[1:]], axis=1)
            sim = jnp.einsum('bhwid,bhwjd->bhwij', bq, bk)
            i = bt[:, :, None]
            j = btk[:, None, :]
            mask = (i < j) | (i > j + WINDOW) | (j == -1)
            sim = jnp.where(mask, -jnp.finfo(sim.dtype).max, sim)
            attn = jax.nn.softmax(sim, axis=-1)
            out = jnp.einsum('bhwij,bhwjd->bhwid', attn, bv)
            return out.reshape(b, h, n, d)

        def _layer(x, wqkv, qs, ksc, wo, lg, lb, w1, b1, w2, b2):
            b, n, _ = x.shape
            h = shift_token(x)
            qkv = h @ wqkv
            q, k, v = jnp.split(qkv, 3, axis=-1)
            to_heads = lambda t: t.reshape(b, n, HEADS, DIM_HEAD).transpose(0, 2, 1, 3)
            q, k, v = (to_heads(q), to_heads(k), to_heads(v))
            q = l2norm(q) * qs
            k = l2norm(k) * ksc
            q, k = rotary_xpos(q, k)
            o = local_attention(q, k, v)
            o = o.transpose(0, 2, 1, 3).reshape(b, n, INNER)
            x = x + o @ wo
            h = shift_token(x)
            mu = h.mean(-1, keepdims=True)
            var = h.var(-1, keepdims=True)
            h = (h - mu) / jnp.sqrt(var + 1e-05) * lg + lb
            h = h @ w1 + b1
            a, g = jnp.split(h, 2, axis=-1)
            h = a * jax.nn.gelu(g, approximate=False)
            x = x + h @ w2 + b2
            return x
        for l in range(DEPTH):
            x = _layer(x, wqkv[l], q_scale[l], k_scale[l], wo[l], ln_g[l], ln_b[l], w1[l], b1[l], w2[l], b2[l])
        return x

    def _L1_attn_ref(x, ln_w, ln_b, log_dt, A_re_log, A_im, C_re, C_im, D_skip, W_out, b_out):
        import jax, jax.numpy as jnp
        import numpy as np
        NL, H, N, B, L = (4, 256, 32, 8, 256)

        def _layernorm_channels(z, w, b):
            mu = jnp.mean(z, axis=1, keepdims=True)
            var = jnp.mean((z - mu) ** 2, axis=1, keepdims=True)
            zn = (z - mu) * jax.lax.rsqrt(var + 1e-05)
            return zn * w[None, :, None] + b[None, :, None]

        def _s4d_layer(z, log_dt, A_re_log, A_im, C_re, C_im, D_skip, W, bvec):
            Bz, Hh, Lz = z.shape
            dt = jnp.exp(log_dt)
            A = -jnp.exp(A_re_log) + 1j * A_im
            dtA = A * dt[:, None]
            C = (C_re + 1j * C_im) * (jnp.expm1(dtA) / A)
            l = jnp.arange(Lz, dtype=jnp.float32)
            K = 2.0 * jnp.einsum('hn,hnl->hl', C, jnp.exp(dtA[:, :, None] * l)).real
            kf = jnp.fft.rfft(K, n=2 * Lz)
            uf = jnp.fft.rfft(z, n=2 * Lz)
            y = jnp.fft.irfft(uf * kf, n=2 * Lz)[..., :Lz]
            y = y + z * D_skip[:, None]
            y = jax.nn.gelu(y)
            out = jnp.einsum('oh,bhl->bol', W, y) + bvec[None, :, None]
            return out[:, :Hh] * jax.nn.sigmoid(out[:, Hh:])
        h = jnp.transpose(x, (0, 2, 1))
        for i in range(NL):
            z = _layernorm_channels(h, ln_w[i], ln_b[i])
            z = _s4d_layer(z, log_dt[i], A_re_log[i], A_im[i], C_re[i], C_im[i], D_skip[i], W_out[i], b_out[i])
            h = z + h
        return jnp.transpose(h, (0, 2, 1))

    def _L1_ffn_ref(x, w1_w, w1_s, w2_w, w2_s, h1_w, h1_s, h2_w, h2_s, w3_w, w3_s):
        import jax, jax.numpy as jnp
        import numpy as np
        D_IN, D_HID = (256, 1024)

        def _ternary(key, shape):
            return jax.random.randint(key, shape, -1, 2).astype(jnp.float32)

        def _tlin(x, w, s):
            return jnp.einsum('bsi,oi->bso', x, w) * s
        h = jax.nn.silu(_tlin(x, w1_w, w1_s)) * _tlin(x, w2_w, w2_s)
        h = jax.nn.gelu(_tlin(h, h1_w, h1_s), approximate=False)
        h = jax.nn.gelu(_tlin(h, h2_w, h2_s), approximate=False)
        return _tlin(h, w3_w, w3_s)
    x = L0_attn_inputs
    mod = (_silu(L0_c) @ L0_wmod).reshape(L0_c.shape[0], 6, 1, -1)
    sa, ca, ga, sb, cb, gb = (mod[:, 0], mod[:, 1], mod[:, 2], mod[:, 3], mod[:, 4], mod[:, 5])
    ga = (2 * (ga >= 0) - 1) * jnp.maximum(jnp.abs(ga), 0.25)
    gb = (2 * (gb >= 0) - 1) * jnp.maximum(jnp.abs(gb), 0.25)
    h = _layernorm(x, axis=-1) * (1 + ca) + sa
    x = x + ga * _L0_attn_ref(h, L0_attn_ln1_g, L0_attn_ln1_b, L0_attn_ln2_g, L0_attn_ln2_b, L0_attn_tm_mix_k, L0_attn_tm_mix_v, L0_attn_tm_mix_r, L0_attn_tm_Wk, L0_attn_tm_Wv, L0_attn_tm_Wr, L0_attn_time_decay, L0_attn_time_first, L0_attn_Wo, L0_attn_cm_mix_k, L0_attn_cm_mix_r, L0_attn_cm_Wk, L0_attn_cm_Wv, L0_attn_cm_Wr)
    h = _layernorm(x, axis=-1) * (1 + cb) + sb
    x = x + gb * _L0_ffn_ref(h, L0_ffn_wqkv, L0_ffn_q_scale, L0_ffn_k_scale, L0_ffn_wo, L0_ffn_ln_g, L0_ffn_ln_b, L0_ffn_w1, L0_ffn_b1, L0_ffn_w2, L0_ffn_b2)
    mod = (_silu(L1_c) @ L1_wmod).reshape(L1_c.shape[0], 6, 1, -1)
    sa, ca, ga, sb, cb, gb = (mod[:, 0], mod[:, 1], mod[:, 2], mod[:, 3], mod[:, 4], mod[:, 5])
    ga = (2 * (ga >= 0) - 1) * jnp.maximum(jnp.abs(ga), 0.25)
    gb = (2 * (gb >= 0) - 1) * jnp.maximum(jnp.abs(gb), 0.25)
    h = _layernorm(x, axis=-1) * (1 + ca) + sa
    x = x + ga * _L1_attn_ref(h, L1_attn_ln_w, L1_attn_ln_b, L1_attn_log_dt, L1_attn_A_re_log, L1_attn_A_im, L1_attn_C_re, L1_attn_C_im, L1_attn_D_skip, L1_attn_W_out, L1_attn_b_out)
    h = _layernorm(x, axis=-1) * (1 + cb) + sb
    x = x + gb * _L1_ffn_ref(h, L1_ffn_w1_w, L1_ffn_w1_s, L1_ffn_w2_w, L1_ffn_w2_s, L1_ffn_h1_w, L1_ffn_h1_s, L1_ffn_h2_w, L1_ffn_h2_s, L1_ffn_w3_w, L1_ffn_w3_s)
    return x

_drawn_inputs = setup_inputs


def setup_inputs(seed=0):
    import zlib

    import numpy as np

    out = dict(_drawn_inputs(seed))
    spreads = {'L0_attn_ln1_g': (1.0, 0.2),
     'L0_attn_ln1_b': (0.0, 0.1),
     'L0_attn_ln2_g': (1.0, 0.2),
     'L0_attn_ln2_b': (0.0, 0.1),
     'L0_ffn_q_scale': (1.0, 0.2),
     'L0_ffn_k_scale': (1.0, 0.2),
     'L0_ffn_ln_g': (1.0, 0.2),
     'L0_ffn_ln_b': (0.0, 0.1),
     'L0_ffn_b1': (0.0, 0.1),
     'L0_ffn_b2': (0.0, 0.1),
     'L1_attn_ln_w': (1.0, 0.2),
     'L1_attn_ln_b': (0.0, 0.1),
     'L1_attn_A_re_log': (-0.6931471824645996, 0.2),
     'L1_attn_b_out': (0.0, 0.1)}
    factors = {}
    for name, (base, spread) in spreads.items():
        noise = np.random.default_rng([zlib.crc32(name.encode()), seed]).standard_normal(out[name].shape)
        drawn = base * np.exp(spread * noise) if base else spread * noise
        out[name] = jnp.asarray(drawn.astype(out[name].dtype))
    for name, factor in factors.items():
        out[name] = (out[name] * factor).astype(out[name].dtype)
    return out
```

```python
from contextlib import ExitStack

import concourse.bass as bass
from concourse import mybir

F32 = mybir.dt.float32
BF16 = mybir.dt.bfloat16
ALU = mybir.AluOpType
ACT = mybir.ActivationFunctionType
AX = mybir.AxisListType

P = 128
D = 256
KD = D // P
N = 4096
TT = 512
NT = N // TT
W = 128
NW = N // W
HEADS, DH = 8, 64
INNER = HEADS * DH
DEPTH = 2
HID = 682
HK = -(-HID // P)
HLAST = HID - (HK - 1) * P
CM = 4 * D
FF = 1024
NL = 4
SN = 32
Q4 = 4
HQ = D // Q4
C = 128
NC = N // C
GQ = 4
GC = GQ * Q4
NG = HQ // GQ
MAGIC = 1.5 * 2.0 ** 23
TWO_PI = 6.2831850
PI = TWO_PI / 2

COLS = {}


def _cols():
    at = 0
    for name, n in ([(k, KD) for k in (
            "ln1_g", "ln1_b", "ln2_g", "ln2_b", "tm_mix_k", "tm_mix_v", "tm_mix_r",
            "time_decay", "time_first", "cm_mix_k", "cm_mix_r", "c0", "c1")]
            + [(f"f_ln_g{l}", KD) for l in range(DEPTH)] + [(f"f_ln_b{l}", KD) for l in range(DEPTH)]
            + [(f"f_b1a{l}", HK) for l in range(DEPTH)] + [(f"f_b1g{l}", HK) for l in range(DEPTH)]
            + [(f"f_b2{l}", KD) for l in range(DEPTH)]
            + [(f"s_ln_w{l}", KD) for l in range(NL)] + [(f"s_ln_b{l}", KD) for l in range(NL)]
            + [(f"s_b{l}", 2 * KD) for l in range(NL)]
            + [("w1_s", FF // P), ("w2_s", FF // P), ("h1_s", FF // P), ("h2_s", FF // P), ("w3_s", KD)]):
        COLS[name] = (at, n)
        at += n
    return at


NCOLS = _cols()
SA, CA, GA, SB, CB, GB = (KD * j for j in range(6))


class Shared:
    pass


def known(t):
    return isinstance(t, int)


def past(t, k):
    return not known(t) or t >= k


def run(eng, n, steps, width=2):
    deepest = max(lag for lag, _ in steps)
    head = -(-(deepest + width) // width) * width
    loops = (n - head) // width
    if n < 24:
        head, loops = n, 0

    def straight(s):
        for lag, f in steps:
            if 0 <= s - lag < n:
                f(s - lag, (s - lag) % width)

    for s in range(head):
        straight(s)
    if loops:
        with eng.Fori(head // width, head // width + loops) as turn:
            for j in range(width):
                for lag, f in steps:
                    f(turn * width + (j - lag), (j - lag) % width)
    for s in range(head + loops * width, n + deepest):
        straight(s)


def open_pass(nc, G, ctx):
    G.passes += 1
    sems, mark = [], f"_{G.passes}"

    def sb(name, shape, dt=F32):
        return ctx.enter_context(nc.sbuf_tensor(name + mark, shape, dt))

    def sem(name):
        s = nc.alloc_semaphore(name + mark)
        sems.append(s)
        return s

    def close():
        nc.clear_and_free_semaphores(sems)
        nc.all_engine_barrier()

    return sb, sem, close


def chain(eng, sem):
    count = [0]

    def link(ins):
        count[0] += 1
        ins.then_inc(sem, 1)
        eng.wait_ge(sem, count[0])

    return link


def tok(t, shift=0, size=TT):
    return bass.ds(t * size + shift, size)


def setup_pass(nc, G, tag):
    with ExitStack() as ctx:
        sb, sem, close = open_pass(nc, G, ctx)
        wmod = sb("wmod", [P, 2, KD, 6 * D])
        silu_c = sb("silu_c", [P, 2, KD])
        sign = sb("sign", [P, 2, 12])
        mag = sb("mag", [P, 2, 12])
        loaded, wloaded = sem("loaded"), sem("wloaded")
        silu_ready, mod_ready, link_s = sem("silu_ready"), sem("mod_ready"), sem("link_s")
        with nc.Block() as block:
            @block.sync
            def _(sp):
                sp.dma_start(G.cols[:, :], G.io["cols"]).then_inc(loaded, 16)
                sp.dma_start(G.ident[:, :], G.io["ident"]).then_inc(loaded, 16)
                for l in range(2):
                    sp.dma_start(wmod[:, l], G.io[f"wmod{l}"].rearrange("(k p) n -> p k n", p=P)).then_inc(wloaded, 16)
                sp.wait_ge(loaded, 32)

            @block.scalar
            def _(act):
                act.wait_ge(loaded, 32)
                for l in range(2):
                    act.activation(silu_c[:, l], G.col(f"c{l}"), ACT.Silu).then_inc(silu_ready, 1)

            @block.tensor
            def _(pe):
                pe.wait_ge(silu_ready, 2)
                pe.wait_ge(wloaded, 32)
                for l in range(2):
                    for m in range(12):
                        for k in range(KD):
                            mm = pe.matmul(G.bank[l][:, m:m + 1], wmod[:, l, k, m * P:(m + 1) * P],
                                           silu_c[:, l, k:k + 1], start=(k == 0), stop=(k == KD - 1))
                    mm.then_inc(mod_ready, 1)

            @block.vector
            def _(dve):
                link = chain(dve, link_s)
                dve.memset(G.mean_w[:, :], 1.0 / D)
                dve.memset(G.eps3[:, :], 1e-3)
                dve.memset(G.half_pi[:, :], TWO_PI / 4)
                dve.memset(G.eps5[:, :], 1e-5)
                dve.wait_ge(mod_ready, 2)
                for l in range(2):
                    M = G.mod[:, l, :]
                    link(dve.tensor_copy(M, G.bank[l][:, 0:12]))
                    link(dve.tensor_scalar(sign[:, l], M, 0.0, 2.0, ALU.is_ge, ALU.mult))
                    link(dve.tensor_scalar(sign[:, l], sign[:, l], -1.0, None, ALU.add))
                    link(dve.tensor_tensor(mag[:, l], sign[:, l], M, ALU.mult))
                    link(dve.tensor_scalar(mag[:, l], mag[:, l], 0.25, None, ALU.max))
                    for at in (CA, CB):
                        link(dve.tensor_scalar(M[:, at:at + KD], M[:, at:at + KD], 1.0, None, ALU.add))
                    for at in (GA, GB):
                        link(dve.tensor_tensor(M[:, at:at + KD], mag[:, l, at:at + KD], sign[:, l, at:at + KD], ALU.mult))
        close()


def ln_pass(nc, G, tag, src, dst, eps, gain, bias, load=None):
    with ExitStack() as ctx:
        sb, sem, close = open_pass(nc, G, ctx)
        xc = sb("ln_xc", [P, 2, KD, TT])
        sq = sb("ln_sq", [P, 2, KD, TT])
        std = sb("ln_std", [P, 2, TT])
        inv = sb("ln_inv", [P, 2, TT])
        src_loaded = [sem(f"src_loaded{t}") for t in range(NT)] if load is not None else []
        mean_ready, centered = sem("mean_ready"), sem("centered")
        squared, var_ready, std_ready = sem("squared"), sem("var_ready"), sem("std_ready")
        inv_ready, normed, affined = sem("inv_ready"), sem("normed"), sem("affined")
        mean_bank, var_bank = G.bank[0:2], G.bank[2:4]
        with nc.Block() as block:
            if load is not None:
                @block.sync
                def _(sp):
                    load(sp, src_loaded)

            @block.tensor
            def _(pe):
                def mean(t, p):
                    if load is not None:
                        pe.wait_ge(src_loaded[t], 16)
                    if past(t, 2):
                        pe.wait_ge(centered, t - 1)
                    for k in range(KD):
                        mm = pe.matmul(mean_bank[p][:, :], G.mean_w[:, :], src(k, t), start=(k == 0), stop=(k == KD - 1))
                    mm.then_inc(mean_ready, 1)

                def var(t, p):
                    pe.wait_ge(squared, t + 1)
                    if past(t, 2):
                        pe.wait_ge(std_ready, t - 1)
                    for k in range(KD):
                        mm = pe.matmul(var_bank[p][:, :], G.mean_w[:, :], sq[:, p, k], start=(k == 0), stop=(k == KD - 1))
                    mm.then_inc(var_ready, 1)

                run(pe, NT, [(1, var), (0, mean)])

            @block.vector
            def _(dve):
                def center(t, p):
                    dve.wait_ge(mean_ready, t + 1)
                    if past(t, 2):
                        dve.wait_ge(affined, t - 1)
                    for k in range(KD):
                        i = dve.tensor_tensor(xc[:, p, k], src(k, t), mean_bank[p][:, :], ALU.subtract)
                    i.then_inc(centered, 1)

                def norm(t, p):
                    dve.wait_ge(std_ready, t + 1)
                    dve.reciprocal(inv[:, p], std[:, p]).then_inc(inv_ready, 1)
                    dve.wait_ge(inv_ready, t + 1)
                    for k in range(KD):
                        i = dve.tensor_tensor(xc[:, p, k], xc[:, p, k], inv[:, p], ALU.mult)
                    i.then_inc(normed, 1)

                run(dve, NT, [(1, norm), (0, center)])

            @block.scalar
            def _(act):
                def square(t, p):
                    act.wait_ge(centered, t + 1)
                    if past(t, 2):
                        act.wait_ge(var_ready, t - 1)
                    act.activation(sq[:, p], xc[:, p], ACT.Square).then_inc(squared, 1)

                def root(t, p):
                    act.wait_ge(var_ready, t + 1)
                    if past(t, 2):
                        act.wait_ge(inv_ready, t - 1)
                    act.activation(std[:, p], var_bank[p][:, :], ACT.Sqrt, bias=eps).then_inc(std_ready, 1)

                def affine(t, p):
                    act.wait_ge(normed, t + 1)
                    for k in range(KD):
                        out = dst(k, t)
                        x = xc[:, p, k] if len(out.shape) == 2 else xc[:, p, k].rearrange("p (c j) -> p c j", j=out.shape[2])
                        i = act.activation(out, x, ACT.Identity, scale=gain[:, k:k + 1], bias=bias[:, k:k + 1])
                    i.then_inc(affined, 1)

                run(act, NT, [(2, affine), (1, root), (0, square)])
        close()


def load_x(G, name, X):
    def load(sp, done):
        for t in range(NT):
            sp.dma_start(X[:, :, t * TT:(t + 1) * TT],
                         G.io[name].rearrange("(k p) n -> p k n", p=P)[:, :, t * TT:(t + 1) * TT]).then_inc(done[t], 16)
    return load


def time_mix_pass(nc, G, H, S):
    with ExitStack() as ctx:
        sb, sem, close = open_pass(nc, G, ctx)
        wkvr = sb("tm_w", [P, 3, KD, D])
        wo = sb("tm_wo", [P, KD, D])
        decay = sb("decay", [P, KD, TT])
        wdec = sb("wdec", [P, KD])
        d = sb("tm_d", [P, 2, KD, TT])
        mix = sb("tm_mix", [P, 3, KD, TT])
        mixr = sb("tm_mixr", [P, KD, TT])
        kvr = sb("tm_kvr", [P, 2, 3, KD, TT])
        pp = sb("tm_pp", [P, 2, KD, 1 + TT])
        ab = sb("tm_ab", [P, 1, 2, KD, 1 + TT])
        ex = sb("tm_ex", [P, 2, 4, KD, TT])
        ev = sb("tm_ev", [P, 1, 2, KD, TT])
        rw = sb("tm_rw", [P, 1, KD, TT])
        names = ("weights", "dif", "mixk", "mixv", "mixr_h", "mixr", "proj", "evac", "args", "exps", "evs", "out", "wod", "res", "dec", "l")
        weights, dif, mixk, mixv, mixr_h, mixr_s, proj, evac, args, exps, evs, out, wod, res, dec, link_s = (sem("tm_" + n) for n in names)
        kvr_bank, wo_bank = G.bank[0:6], G.bank[6:8]
        cols = [G.col(n) for n in ("tm_mix_k", "tm_mix_v", "tm_mix_r")]
        u = G.col("time_first")
        with nc.Block() as block:
            @block.sync
            def _(sp):
                for j, n in enumerate(("tm_Wk", "tm_Wv", "tm_Wr")):
                    sp.dma_start(wkvr[:, j], G.io[n].rearrange("(k p) n -> p k n", p=P)).then_inc(weights, 16)
                sp.dma_start(wo[:, :, :], G.io["Wo"].rearrange("(k p) n -> p k n", p=P)).then_inc(weights, 16)

            @block.gpsimd
            def _(pool):
                for t in range(NT):
                    p = t % 2
                    if t >= 2:
                        pool.wait_ge(mixv, t - 1)
                        pool.wait_ge(mixr_s, t - 1)
                    pool.tensor_tensor(d[:, p], S[:, :, tok(t, 1)], S[:, :, tok(t)], ALU.subtract).then_inc(dif, 1)
                    pool.wait_ge(dif, t + 1)
                    if t >= 1:
                        pool.wait_ge(proj, t)
                    for k in range(KD):
                        i = pool.tensor_scalar(mixr[:, k], d[:, p, k], cols[2][:, k:k + 1], None, ALU.mult)
                    i.then_inc(mixr_h, 1)
                    pool.wait_ge(mixr_h, t + 1)
                    pool.tensor_tensor(mix[:, 2], mixr[:, :], S[:, :, tok(t)], ALU.add).then_inc(mixr_s, 1)
                    if t >= 1:
                        q = 1 - p
                        pool.wait_ge(exps, t)
                        if t >= 2:
                            pool.wait_ge(out, t - 1)
                        pool.tensor_tensor(ev[:, 0, 0], ex[:, q, 1], kvr[:, q, 1], ALU.mult)
                        pool.tensor_tensor(ev[:, 0, 1], ex[:, q, 3], kvr[:, q, 1], ALU.mult).then_inc(evs, 1)
                q = (NT - 1) % 2
                pool.wait_ge(exps, NT)
                pool.wait_ge(out, NT - 1)
                pool.tensor_tensor(ev[:, 0, 0], ex[:, q, 1], kvr[:, q, 1], ALU.mult)
                pool.tensor_tensor(ev[:, 0, 1], ex[:, q, 3], kvr[:, q, 1], ALU.mult).then_inc(evs, 1)

            @block.tensor
            def _(pe):
                def project(t, p):
                    if t == 0:
                        pe.wait_ge(weights, 64)
                    pe.wait_ge(mixk, t + 1)
                    pe.wait_ge(mixv, t + 1)
                    pe.wait_ge(mixr_s, t + 1)
                    if t >= 1:
                        pe.wait_ge(evac, t)
                    for j in range(3):
                        for m in range(KD):
                            for k in range(KD):
                                mm = pe.matmul(kvr_bank[2 * j + m][:, :], wkvr[:, j, k, m * P:(m + 1) * P], mix[:, j, k],
                                               start=(k == 0), stop=(k == KD - 1))
                    mm.then_inc(proj, 1)

                def outproj(t, p):
                    pe.wait_ge(out, t + 1)
                    if t >= 1:
                        pe.wait_ge(res, t)
                    for m in range(KD):
                        for k in range(KD):
                            mm = pe.matmul(wo_bank[m][:, :], wo[:, k, m * P:(m + 1) * P], rw[:, 0, k], start=(k == 0), stop=(k == KD - 1))
                    mm.then_inc(wod, 1)

                run(pe, NT, [(0, project), (2, outproj)])

            @block.scalar
            def _(act):
                act.activation(wdec[:, :], G.col("time_decay"), ACT.Exp).then_inc(dec, 1)

                def evacuate(t, p):
                    act.wait_ge(proj, t + 1)
                    if t >= 2:
                        act.wait_ge(out, t - 1)
                    for j in range(3):
                        for m in range(KD):
                            i = act.activation(kvr[:, p, j, m], kvr_bank[2 * j + m][:, :], ACT.Tanh if j == 2 else ACT.Copy,
                                               scale=0.5 if j == 2 else 1.0)
                    i.then_inc(evac, 1)

                def exponents(t, p):
                    act.wait_ge(args, t + 1)
                    act.activation(ex[:, p], ex[:, p], ACT.Exp).then_inc(exps, 1)

                run(act, NT, [(0, evacuate), (1, exponents)])

            @block.vector
            def _(dve):
                link = chain(dve, link_s)
                dve.wait_ge(dec, 1)
                link(dve.tensor_scalar(wdec[:, :], wdec[:, :], -1.0, None, ALU.mult))
                link(dve.memset(decay[:, :, :], 0.0))
                for k in range(KD):
                    link(dve.tensor_scalar(decay[:, k], decay[:, k], wdec[:, k:k + 1], None, ALU.add))
                dve.memset(pp[:, 0, :, 0:1], -1e38)
                link(dve.memset(ab[:, 0, :, :, 0:1], 0.0))

                def mixes(t, p):
                    dve.wait_ge(dif, t + 1)
                    if t >= 1:
                        dve.wait_ge(proj, t)
                    for j, s in ((0, mixk), (1, mixv)):
                        for k in range(KD):
                            i = dve.scalar_tensor_tensor(mix[:, j, k], d[:, p, k], cols[j][:, k:k + 1], S[:, k, tok(t)], ALU.mult, ALU.add)
                        i.then_inc(s, 1)

                def arguments(t, p):
                    dve.wait_ge(evac, t + 1)
                    if t >= 1:
                        link(dve.tensor_copy(pp[:, p, :, 0:1], pp[:, 1 - p, :, TT:TT + 1]))
                    K = kvr[:, p, 0]
                    for h in range(KD):
                        link(dve.tensor_tensor_scan(pp[:, p, h, 1:1 + TT], decay[:, h], K[:, h], pp[:, p, h, 0:1], ALU.add, ALU.max))
                    prev, cur = pp[:, p, :, 0:TT], pp[:, p, :, 1:1 + TT]
                    for h in range(KD):
                        dve.scalar_tensor_tensor(ex[:, p, 0, h], prev[:, h], wdec[:, h:h + 1], cur[:, h], ALU.add, ALU.subtract)
                        link(dve.scalar_tensor_tensor(ex[:, p, 2, h], K[:, h], u[:, h:h + 1], prev[:, h], ALU.add, ALU.max))
                    dve.tensor_tensor(ex[:, p, 1], K, cur, ALU.subtract)
                    for h in range(KD):
                        link(dve.scalar_tensor_tensor(ex[:, p, 3, h], K[:, h], u[:, h:h + 1], ex[:, p, 2, h], ALU.add, ALU.subtract))
                    dve.tensor_tensor(ex[:, p, 2], prev, ex[:, p, 2], ALU.subtract).then_inc(args, 1)

                def wkv(t, p):
                    dve.wait_ge(evs, t + 1)
                    if t >= 1:
                        link(dve.tensor_copy(ab[:, 0, :, :, 0:1], ab[:, 0, :, :, TT:TT + 1]))
                    for h in range(KD):
                        dve.tensor_tensor_scan(ab[:, 0, 0, h, 1:1 + TT], ex[:, p, 0, h], ev[:, 0, 0, h], ab[:, 0, 0, h, 0:1], ALU.mult, ALU.add)
                        link(dve.tensor_tensor_scan(ab[:, 0, 1, h, 1:1 + TT], ex[:, p, 0, h], ex[:, p, 1, h], ab[:, 0, 1, h, 0:1], ALU.mult, ALU.add))
                    num, den = ex[:, p, 0], ex[:, p, 1]
                    dve.tensor_tensor(den, ex[:, p, 2], ab[:, 0, 1, :, 0:TT], ALU.mult)
                    link(dve.tensor_tensor(num, ex[:, p, 2], ab[:, 0, 0, :, 0:TT], ALU.mult))
                    dve.tensor_tensor(den, den, ex[:, p, 3], ALU.add)
                    link(dve.tensor_tensor(num, num, ev[:, 0, 1], ALU.add))
                    link(dve.reciprocal(den, den))
                    link(dve.tensor_tensor(num, num, den, ALU.mult))
                    if t >= 1:
                        dve.wait_ge(wod, t)
                    dve.scalar_tensor_tensor(rw[:, 0], kvr[:, p, 2], 1.0, num, ALU.add, ALU.mult).then_inc(out, 1)

                def residual(t, p):
                    dve.wait_ge(wod, t + 1)
                    for h in range(KD):
                        i = dve.scalar_tensor_tensor(H[:, h, tok(t)], wo_bank[h][:, :], 0.5, H[:, h, tok(t)], ALU.mult, ALU.add)
                    i.then_inc(res, 1)

                run(dve, NT, [(3, residual), (0, mixes), (2, wkv), (1, arguments)])
        close()


def channel_mix_pass(nc, G, H, S, src, dst):
    MF = CM // P
    with ExitStack() as ctx:
        sb, sem, close = open_pass(nc, G, ctx)
        wk = sb("cm_wk", [P, KD, CM])
        wv = sb("cm_wv", [P, MF, D])
        wr = sb("cm_wr", [P, KD, D])
        d = sb("cm_d", [P, KD, TT])
        mix = sb("cm_mix", [P, 2, 2, KD, TT])
        kc = sb("cm_kc", [P, 2, MF, TT])
        th = sb("cm_th", [P, KD, TT])
        xin = sb("cm_x", [P, 2, KD, TT])
        weights, dif, mixed, krdy, kev, ksq, rrdy, tanhed, vrdy, res, xload, stored, link_s = (
            sem("cm_" + n) for n in ("weights", "dif", "mixed", "krdy", "kev", "ksq", "rrdy", "tanhed", "vrdy", "res", "xload", "stored", "l"))
        xld = [xload, sem("cm_xload1")]
        k_bank, r_bank, v_bank = G.bank[0:4], G.bank[4:6], G.bank[6:8]
        mk, mr = G.col("cm_mix_k"), G.col("cm_mix_r")
        gate = G.mod[:, 0, GA:GA + KD]
        xs = G.io[src].rearrange("(k p) n -> p k n", p=P)
        xd = G.io[dst].rearrange("(k p) n -> p k n", p=P)
        with nc.Block() as block:
            @block.sync
            def _(sp):
                sp.dma_start(wr[:, :, :], G.io["cm_Wr"].rearrange("(k p) n -> p k n", p=P)).then_inc(weights, 16)
                sp.dma_start(wk[:, :, :], G.io["cm_Wk"].rearrange("(k p) n -> p k n", p=P)).then_inc(weights, 16)
                sp.dma_start(wv[:, :, :], G.io["cm_Wv"].rearrange("(k p) n -> p k n", p=P)).then_inc(weights, 16)
                for t in range(NT):
                    if t >= 2:
                        sp.wait_ge(res, t - 1)
                        sp.dma_start(xd[:, :, tok(t - 2)], xin[:, t % 2]).then_inc(stored, 16)
                        sp.wait_ge(stored, 16 * (t - 1))
                    sp.dma_start(xin[:, t % 2], xs[:, :, tok(t)]).then_inc(xld[t % 2], 16)
                for t in range(NT, NT + 2):
                    sp.wait_ge(res, t - 1)
                    sp.dma_start(xd[:, :, tok(t - 2)], xin[:, t % 2]).then_inc(stored, 16)
                sp.wait_ge(stored, 16 * NT)

            @block.gpsimd
            def _(pool):
                def mixes(t, p):
                    if t >= 1:
                        pool.wait_ge(mixed, t)
                    pool.tensor_tensor(d[:, :], S[:, :, tok(t, 1)], S[:, :, tok(t)], ALU.subtract).then_inc(dif, 1)
                run(pool, NT, [(0, mixes)])

            @block.tensor
            def _(pe):
                def front(t, p):
                    if t == 0:
                        pe.wait_ge(weights, 48)
                    pe.wait_ge(mixed, t + 1)
                    if t >= 1:
                        pe.wait_ge(tanhed, t)
                    for m in range(KD):
                        for k in range(KD):
                            mm = pe.matmul(r_bank[m][:, :], wr[:, k, m * P:(m + 1) * P], mix[:, p, 1, k], start=(k == 0), stop=(k == KD - 1))
                    mm.then_inc(rrdy, 1)
                    for m in range(MF):
                        n = t * MF + m
                        if n >= 4:
                            pe.wait_ge(kev, n - 3)
                        for k in range(KD):
                            mm = pe.matmul(k_bank[m % 4][:, :], wk[:, k, m * P:(m + 1) * P], mix[:, p, 0, k], start=(k == 0), stop=(k == KD - 1))
                        mm.then_inc(krdy, 1)

                def back(t, p):
                    if t >= 1:
                        pe.wait_ge(res, t)
                    for m in range(KD):
                        for k in range(MF):
                            if m == 0:
                                pe.wait_ge(ksq, t * MF + k + 1)
                            mm = pe.matmul(v_bank[m][:, :], wv[:, k, m * P:(m + 1) * P], kc[:, p, k], start=(k == 0), stop=(k == MF - 1))
                    mm.then_inc(vrdy, 1)

                run(pe, NT, [(0, front), (1, back)])

            @block.scalar
            def _(act):
                def front(t, p):
                    act.wait_ge(rrdy, t + 1)
                    if t >= 1:
                        act.wait_ge(res, t)
                    for m in range(KD):
                        i = act.activation(th[:, m], r_bank[m][:, :], ACT.Tanh, scale=0.5)
                    i.then_inc(tanhed, 1)

                def relu(t, p):
                    if t >= 2:
                        act.wait_ge(vrdy, t - 1)
                    for m in range(MF):
                        act.wait_ge(krdy, t * MF + m + 1)
                        act.activation(kc[:, p, m], k_bank[m % 4][:, :], ACT.Relu).then_inc(kev, 1)

                for s in range(NT):
                    relu(s, s % 2)
                    front(s, s % 2)

            @block.vector
            def _(dve):
                link = chain(dve, link_s)

                def mixes(t, p):
                    dve.wait_ge(dif, t + 1)
                    if t >= 2:
                        dve.wait_ge(krdy, (t - 1) * MF)
                    for j, col in ((0, mk), (1, mr)):
                        for k in range(KD):
                            i = dve.scalar_tensor_tensor(mix[:, p, j, k], d[:, k], col[:, k:k + 1], S[:, k, tok(t)], ALU.mult, ALU.add)
                    i.then_inc(mixed, 1)

                def square(t, p):
                    for m in range(MF):
                        dve.wait_ge(kev, t * MF + m + 1)
                        dve.tensor_tensor(kc[:, p, m], kc[:, p, m], kc[:, p, m], ALU.mult).then_inc(ksq, 1)

                def residual(t, p):
                    dve.wait_ge(tanhed, t + 1)
                    dve.wait_ge(vrdy, t + 1)
                    dve.wait_ge(xld[p], 16 * (t // 2 + 1))
                    for h in range(KD):
                        link(dve.scalar_tensor_tensor(th[:, h], th[:, h], 1.0, v_bank[h][:, :], ALU.add, ALU.mult))
                    for h in range(KD):
                        link(dve.scalar_tensor_tensor(H[:, h, tok(t)], th[:, h], 0.5, H[:, h, tok(t)], ALU.mult, ALU.add))
                    for h in range(KD):
                        i = dve.scalar_tensor_tensor(xin[:, p, h], H[:, h, tok(t)], gate[:, h:h + 1], xin[:, p, h], ALU.mult, ALU.add)
                    i.then_inc(res, 1)

                run(dve, NT, [(0, mixes), (1, residual), (0, square)])
        close()


def zero_column(nc, G, tag, bufs):
    with nc.Block() as block:
        @block.vector
        def _(dve):
            for b in bufs:
                dve.memset(b[:, :, 0:1], 0.0)


def rwkv_stage(nc, G, src, dst):
    with ExitStack() as ctx:
        H = ctx.enter_context(nc.sbuf_tensor("rw_h", [P, KD, N], F32))
        S = ctx.enter_context(nc.sbuf_tensor("rw_s", [P, KD, 1 + N], F32))
        Sv = lambda k, t: S[:, k, tok(t, 1)]
        Hv = lambda k, t: H[:, k, tok(t)]
        zero_column(nc, G, "", [S])
        ln_pass(nc, G, "", Hv, Hv, G.eps5[:, :], G.mod[:, 0, CA:CA + KD], G.mod[:, 0, SA:SA + KD], load=load_x(G, src, H))
        ln_pass(nc, G, "", Hv, Sv, G.eps3[:, :], G.col("ln1_g"), G.col("ln1_b"))
        time_mix_pass(nc, G, H, S)
        ln_pass(nc, G, "", Hv, Sv, G.eps3[:, :], G.col("ln2_g"), G.col("ln2_b"))
        channel_mix_pass(nc, G, H, S, src, dst)


def attention_pass(nc, G, l, X, Y):
    with ExitStack() as ctx:
        sb, sem, close = open_pass(nc, G, ctx)
        wqkv = sb("wqkv", [P, KD, 3 * INNER])
        wo = sb("wo", [P, INNER // P, D])
        masks = sb("masks", [P, 3, 2 * W], BF16)
        masks32 = sb("masks32", [P, 3, 2 * W])
        identb = sb("identb", [P, P], BF16)
        scales = sb("scales", [P, 4, DH])
        rot = [sb(f"rot{i}", [P, 4, DH]) for i in range(2)]
        rots = [sb(f"rots{i}", [P, 4, DH]) for i in range(2)]
        hs = [sb(f"hs{i}", [P, KD, W]) for i in range(2)]
        qk = [sb(f"qk{i}", [P, 2, HEADS, DH]) for i in range(2)]
        v = [sb(f"v{i}", [P, INNER]) for i in range(4)]
        sq = sb("sq", [P, 2, HEADS, DH])
        ss = [sb(f"ss{i}", [P, 2, HEADS]) for i in range(2)]
        rn = [sb(f"rn{i}", [P, 2, HEADS]) for i in range(2)]
        half = sb("half", [P, 2, HEADS])
        ra = sb("ra", [P, 2, HEADS, DH])
        rb = sb("rb", [P, 2, HEADS, DH])
        qkr = [sb(f"qkr{i}", [P, 2, INNER]) for i in range(2)]
        qT = [sb(f"qT{i}", [P, HEADS // 2, W]) for i in range(2)]
        kT = sb("kT", [P, HEADS // 2, 2, W])
        nmax = [sb(f"nmax{i}", [P, HEADS]) for i in range(2)]
        rsum = [sb(f"rsum{i}", [P, HEADS]) for i in range(2)]
        rinv = [sb(f"rinv{i}", [P, HEADS]) for i in range(2)]
        pr = [sb(f"pr{i}", [P, HEADS, 2, W]) for i in range(2)]
        pT = sb("pT", [P, HEADS, 2, W])
        o = [sb(f"o{i}", [P, INNER]) for i in range(2)]
        oT = sb("oT", [P, INNER // P, W])
        names = ("weights", "consts", "scal", "rotld0", "rotld1", "rotsc", "hsr", "projq", "projk", "projv", "qev", "kev", "vev",
                 "sqd", "ssd", "rnh", "rnd", "ram", "rbm", "rsumd", "qkrd", "trq", "trk", "qTd", "kTd", "sc", "mx", "ex",
                 "pt", "ptA", "ptV", "pv", "rid", "od", "otr", "oTd", "wod", "res", "zeroed")
        (weights, consts, scal, rotld0, rotld1, rotsc, hsr, projq, projk, projv, qev, kev, vev,
         sqd, ssd, rnh, rnd, ram, rbm, rsumd, qkrd, trq, trk, qTd, kTd, sc, mx, ex,
         pt, ptA, ptV, pv, rid, od, otr, oTd, wod, res, zeroed) = (sem("a_" + n) for n in names)
        rotld = (rotld0, rotld1)
        proj_bank, turn_bank, score_bank, value_bank = G.bank[0:2], G.bank[2:4], G.bank[4:7], G.bank[7]
        QUAD = ((0, 2), (1, 3), (4, 6), (5, 7))
        qs, ks = G.io["q_scale"], G.io["k_scale"]
        with nc.Block() as block:
            @block.sync
            def _(sp):
                sp.dma_start(wqkv[:, :, :], G.io["wqkv"][l].rearrange("(k p) n -> p k n", p=P)).then_inc(weights, 16)
                sp.dma_start(wo[:, :, :], G.io["wo"][l].rearrange("(k p) n -> p k n", p=P)).then_inc(weights, 16)
                sp.dma_start(masks32[:, :, :], G.io["masks"]).then_inc(consts, 16)
                for j, s in ((0, qs), (2, ks)):
                    row = s[l:l + 1, :]
                    sp.dma_start(scales[:, j], row.to_broadcast([P, DH])).then_inc(consts, 16)
                    for a in (0, DH // 2):
                        b = DH // 2 - a
                        sp.dma_start(scales[:, j + 1, a:a + DH // 2], row[:, b:b + DH // 2].to_broadcast([P, DH // 2])).then_inc(consts, 16)

                def table(t, p):
                    if past(t, 2):
                        sp.wait_ge(rotsc, t - 1)
                    sp.dma_start(rot[p % 2][:, :, :], G.io["rotary"][t] if known(t) else G.io["rotary"][bass.ds(t, 1)].rearrange("a p j d -> p (a j) d")).then_inc(rotld[p % 2], 16)
                run(sp, NW, [(0, table)], 4)

            @block.gpsimd
            def _(pool):
                pool.wait_ge(consts, 16 * 7)

                def shift(t, p):
                    if past(t, 2):
                        pool.wait_ge(projv, t - 1)
                    pool.tensor_copy(hs[p % 2][:, 0], X[:, 0, tok(t, 1, W)])
                    pool.tensor_copy(hs[p % 2][:, 1], X[:, 1, tok(t, 0, W)]).then_inc(hsr, 1)
                    pool.wait_ge(rotld[p % 2], 16 * (t // 2 + 1) if known(t) else (t - p % 2) * 8 + 16)
                    if past(t, 2):
                        pool.wait_ge(rbm, t - 1)
                    pool.tensor_tensor(rots[p % 2][:, :, :], rot[p % 2][:, :, :], scales[:, :, :], ALU.mult).then_inc(rotsc, 1)

                def norms(t, p):
                    pool.wait_ge(ssd, t + 1)
                    if past(t, 2):
                        pool.wait_ge(qkrd, t - 1)
                    pool.tensor_tensor(rn[p % 2][:, :, :], ss[p % 2][:, :, :], half[:, :, :], ALU.pow).then_inc(rnd, 1)

                def add(t, p):
                    pool.wait_ge(ram, t + 1)
                    pool.wait_ge(rbm, t + 1)
                    pool.tensor_tensor(ra[:, :, :, :], ra[:, :, :, :], rb[:, :, :, :], ALU.add).then_inc(rsumd, 1)

                pool.wait_ge(zeroed, 1)
                run(pool, NW, [(0, shift), (0, norms), (0, add)], 4)

            @block.tensor
            def _(pe):
                pe.wait_ge(weights, 32)
                pe.wait_ge(zeroed, 1)

                def project(t, p):
                    pe.wait_ge(hsr, t + 1)
                    for j, bank, done in ((0, 0, projq), (1, 1, projk), (2, 0, projv)):
                        if j == 0 and past(t, 1):
                            pe.wait_ge(vev, t)
                        if j == 1 and past(t, 1):
                            pe.wait_ge(kev, t)
                        if j == 2:
                            pe.wait_ge(qev, t + 1)
                        for k in range(KD):
                            mm = pe.matmul(proj_bank[bank][:, :], hs[p % 2][:, k], wqkv[:, k, j * INNER:(j + 1) * INNER],
                                           start=(k == 0), stop=(k == KD - 1))
                        mm.then_inc(done, 1)

                def turn_qk(t, p):
                    pe.wait_ge(qkrd, t + 1)
                    if past(t, 3):
                        pe.wait_ge(oTd, t - 2)
                        pe.wait_ge(res, t - 2)
                    elif t == 2:
                        pe.wait_ge(ptA, 2 * (t - 1))
                        pe.wait_ge(ptV, 2 * (t - 1))
                    elif t == 1:
                        pe.wait_ge(qTd, t)
                        pe.wait_ge(kTd, t)
                    for j, done in ((0, trq), (1, trk)):
                        for c in range(HEADS // 2):
                            mm = pe.transpose(turn_bank[j][:, c * W:(c + 1) * W], qkr[p % 2][:, j, c * P:(c + 1) * P], G.ident[:, :])
                        mm.then_inc(done, 1)

                def scores(t, p):
                    pe.wait_ge(qTd, t + 1)
                    pe.wait_ge(kTd, t + 1)
                    which = 2 if known(t) and t == 0 else p % 2
                    for i, heads in enumerate(QUAD):
                        bank = i % 3
                        if i == 3:
                            pe.wait_ge(ex, 4 * t + 1)
                        elif past(t, 1):
                            pe.wait_ge(ex, 4 * t - 2 + i if i else 4 * t)
                        for a, h in enumerate(heads):
                            r = slice(DH * (h % 2), DH * (h % 2) + DH)
                            out = score_bank[bank][:, a * 2 * W:(a + 1) * 2 * W]
                            pe.matmul(out, qT[p % 2][r, h // 2], kT[r, h // 2].rearrange("p s w -> p (s w)"), start=True, stop=False)
                            mm = pe.matmul(out, identb[:, :], masks[:, which], start=False, stop=True)
                        mm.then_inc(sc, 1)

                def turn_p(t, p):
                    pe.wait_ge(ex, 4 * t + 4)
                    for i in range(4):
                        if i < 2:
                            n = min(t + 2, NW) if known(t) else t + 2
                            pe.wait_ge((qTd, kTd)[i], n)
                            if known(t) and t + 1 >= NW:
                                pe.wait_ge((oTd, res)[i], t - 1)
                        else:
                            pe.wait_ge((ptA, ptV)[i % 2], 2 * t + 1)
                        for a in range(4):
                            h, s = 2 * i + a // 2, a % 2
                            mm = pe.transpose(turn_bank[i % 2][:, a * W:(a + 1) * W], pr[p % 2][:, h, s], G.ident[:, :])
                        mm.then_inc(pt, 1)

                def values(t, p):
                    pe.wait_ge(ptA, 2 * t + 2)
                    pe.wait_ge(ptV, 2 * t + 2)
                    pe.wait_ge(vev, t + 1)
                    if past(t, 1):
                        pe.wait_ge(od, t)
                    for h in range(HEADS):
                        for s in range(2):
                            vw = v[p] if s == p % 2 else v[(p - 1) % 4]
                            mm = pe.matmul(value_bank[:, h * DH:(h + 1) * DH], pT[:, h, s], vw[:, h * DH:(h + 1) * DH], start=(s == 0), stop=(s == 1))
                    mm.then_inc(pv, 1)

                def turn_o(t, p):
                    pe.wait_ge(od, t + 1)
                    pe.wait_ge(ptA, min(2 * t + 4, 2 * NW) if known(t) else 2 * t + 4)
                    for c in range(INNER // P):
                        mm = pe.transpose(turn_bank[0][:, c * W:(c + 1) * W], o[p % 2][:, c * P:(c + 1) * P], G.ident[:, :])
                    mm.then_inc(otr, 1)

                def outproj(t, p):
                    pe.wait_ge(oTd, t + 1)
                    pe.wait_ge(ptV, min(2 * t + 4, 2 * NW) if known(t) else 2 * t + 4)
                    for m in range(KD):
                        for k in range(INNER // P):
                            mm = pe.matmul(turn_bank[1][:, m * W:(m + 1) * W], wo[:, k, m * P:(m + 1) * P], oT[:, k], start=(k == 0), stop=(k == INNER // P - 1))
                    mm.then_inc(wod, 1)

                run(pe, NW, [(3, turn_p), (4, turn_o), (2, scores), (4, outproj), (3, values), (1, turn_qk), (0, project)], 4)

            @block.scalar
            def _(act):
                def turned_p(t, p):
                    if past(t, 1):
                        act.wait_ge(pv, t)
                    for i in (0, 2):
                        act.wait_ge(pt, 4 * t + i + 1)
                        act.activation(pT[:, 2 * i:2 * i + 2].rearrange("p h s w -> p (h s w)"), turn_bank[0][:, :], ACT.Copy).then_inc(ptA, 1)

                def exponentials(t, p):
                    if past(t, 2):
                        act.wait_ge(pt, 4 * (t - 1))
                        act.wait_ge(rid, t - 1)
                    for i, heads in enumerate(QUAD):
                        act.wait_ge(mx, 4 * t + i + 1)
                        for a, h in enumerate(heads):
                            e = act.activation(pr[p % 2][:, h].rearrange("p s w -> p (s w)"), score_bank[i % 3][:, a * 2 * W:(a + 1) * 2 * W],
                                               ACT.Exp, bias=nmax[p % 2][:, h:h + 1], accum_out=rsum[p % 2][:, h:h + 1])
                        e.then_inc(ex, 1)

                def turned_o(t, p):
                    act.wait_ge(otr, t + 1)
                    if past(t, 1):
                        act.wait_ge(wod, t)
                    act.activation(oT[:, :, :].rearrange("p k w -> p (k w)"), turn_bank[0][:, :], ACT.Copy).then_inc(oTd, 1)

                def turned_q(t, p):
                    act.wait_ge(trq, t + 1)
                    if past(t, 2):
                        act.wait_ge(sc, 4 * (t - 1))
                    act.activation(qT[p % 2][:, :, :].rearrange("p c w -> p (c w)"), turn_bank[0][:, :], ACT.Copy).then_inc(qTd, 1)

                def projected(t, p):
                    if past(t, 2):
                        act.wait_ge(rbm, t - 1)
                        act.wait_ge(ram, t - 1)
                    for j, bank, ready, done in ((0, 0, projq, qev), (1, 1, projk, kev)):
                        act.wait_ge(ready, t + 1)
                        act.activation(qk[p % 2][:, j].rearrange("p h d -> p (h d)"), proj_bank[bank][:, :], ACT.Copy).then_inc(done, 1)
                    act.wait_ge(kev, t + 1)
                    if past(t, 1):
                        act.wait_ge(rnh, t)
                    act.activation(sq[:, :, :, :], qk[p % 2][:, :, :, :], ACT.Square).then_inc(sqd, 1)
                    act.wait_ge(projv, t + 1)
                    if past(t, 4):
                        act.wait_ge(pv, t - 2)
                    act.activation(v[p][:, :], proj_bank[0][:, :], ACT.Copy).then_inc(vev, 1)

                act.wait_ge(zeroed, 1)
                run(act, NW, [(3, turned_p), (4, turned_o), (2, exponentials), (1, turned_q), (0, projected)], 4)

            @block.vector
            def _(dve):
                dve.wait_ge(consts, 16 * 7)
                dve.tensor_copy(masks[:, :, :], masks32[:, :, :])
                dve.tensor_copy(identb[:, :], G.ident[:, :])
                dve.memset(half[:, :, :], -0.5)
                dve.memset(kT[:, :, :, :], 0.0)
                dve.memset(v[3][:, :], 0.0)
                dve.memset(Y[:, :, 0:1], 0.0).then_inc(zeroed, 1)

                def turned_p(t, p):
                    if past(t, 1):
                        dve.wait_ge(pv, t)
                    for i in (1, 3):
                        dve.wait_ge(pt, 4 * t + i + 1)
                        dve.tensor_copy(pT[:, 2 * i:2 * i + 2].rearrange("p h s w -> p (h s w)"), turn_bank[1][:, :]).then_inc(ptV, 1)

                def maxima(t, p):
                    for i, heads in enumerate(QUAD):
                        dve.wait_ge(sc, 4 * t + i + 1)
                        dve.tensor_reduce(nmax[p % 2][:, heads[0]:heads[1] + 1:2], score_bank[i % 3][:, :].rearrange("p (h k) -> p h k", h=2),
                                          AX.X, ALU.max, negate=True).then_inc(mx, 1)

                def inverse(t, p):
                    dve.wait_ge(ex, 4 * t + 4)
                    if past(t, 2):
                        dve.wait_ge(od, t - 1)
                    dve.reciprocal(rinv[p % 2][:, :], rsum[p % 2][:, :]).then_inc(rid, 1)

                def normalise(t, p):
                    dve.wait_ge(pv, t + 1)
                    dve.wait_ge(rid, t + 1)
                    if past(t, 2):
                        dve.wait_ge(otr, t - 1)
                    dve.tensor_tensor(o[p % 2][:, :].rearrange("p (h d) -> p h d", h=HEADS), value_bank[:, :].rearrange("p (h d) -> p h d", h=HEADS),
                                      rinv[p % 2][:, :].unsqueeze(2).to_broadcast([P, HEADS, DH]), ALU.mult).then_inc(od, 1)

                def residual(t, p):
                    dve.wait_ge(wod, t + 1)
                    dve.tensor_tensor(Y[:, :, tok(t, 1, W)], turn_bank[1][:, 0:KD * W].rearrange("p (k w) -> p k w", k=KD),
                                      X[:, :, tok(t, 1, W)], ALU.add).then_inc(res, 1)

                def turned_k(t, p):
                    dve.wait_ge(trk, t + 1)
                    if past(t, 1):
                        dve.wait_ge(sc, 4 * t)
                    dve.tensor_copy(kT[:, :, p % 2], turn_bank[1][:, :].rearrange("p (c w) -> p c w", w=W)).then_inc(kTd, 1)

                def squares(t, p):
                    dve.wait_ge(sqd, t + 1)
                    if past(t, 2):
                        dve.wait_ge(rnd, t - 1)
                    dve.tensor_reduce(ss[p % 2][:, :, :], sq[:, :, :, :], AX.X, ALU.add).then_inc(rnh, 1)

                def clip(t, p):
                    dve.wait_ge(rnh, t + 1)
                    dve.tensor_scalar(ss[p % 2][:, :, :], ss[p % 2][:, :, :], 1e-24, None, ALU.max).then_inc(ssd, 1)

                def rotate(t, p):
                    q = qk[p % 2]
                    tab = rots[p % 2]
                    dve.wait_ge(kev, t + 1)
                    dve.wait_ge(rotsc, t + 1)
                    for j in range(2):
                        cos = tab[:, 2 * j].unsqueeze(1).to_broadcast([P, HEADS, DH])
                        i = dve.tensor_tensor(ra[:, j], q[:, j], cos, ALU.mult)
                    i.then_inc(ram, 1)
                    H2 = DH // 2
                    for j in range(2):
                        for a in (0, H2):
                            b = H2 - a
                            sin = tab[:, 2 * j + 1, a:a + H2].unsqueeze(1).to_broadcast([P, HEADS, H2])
                            i = dve.tensor_tensor(rb[:, j, :, a:a + H2], q[:, j, :, b:b + H2], sin, ALU.mult)
                    i.then_inc(rbm, 1)

                def scale(t, p):
                    dve.wait_ge(rsumd, t + 1)
                    dve.wait_ge(rnd, t + 1)
                    if past(t, 2):
                        dve.wait_ge(trk, t - 1)
                    dve.tensor_tensor(qkr[p % 2][:, :, :].rearrange("p j (h d) -> p (j h) d", h=HEADS), ra[:, :, :, :].rearrange("p j h d -> p (j h) d"),
                                      rn[p % 2][:, :, :].rearrange("p j h -> p (j h)").unsqueeze(2).to_broadcast([P, 2 * HEADS, DH]), ALU.mult).then_inc(qkrd, 1)

                run(dve, NW, [(3, turned_p), (2, maxima), (4, residual), (2, inverse), (3, normalise), (1, turned_k), (0, squares), (0, rotate), (0, clip), (0, scale)], 4)
        close()


def gated_mlp_pass(nc, G, l, S, X, finish=None):
    with ExitStack() as ctx:
        sb, sem, close = open_pass(nc, G, ctx)
        w1 = sb("mlp_w1", [P, KD, 2 * HID])
        w2 = sb("mlp_w2", [P, HK, D])
        gel = sb("mlp_gel", [P, 2, TT])
        hid = sb("mlp_hid", [P, 2, HK, TT])
        xin = sb("mlp_x", [P, 2, KD, TT])
        weights, ad, gd, geld, hidd, w2d, res, xl0, xl1, stored, link_s = (
            sem("m_" + n) for n in ("weights", "ad", "gd", "geld", "hidd", "w2d", "res", "xl0", "xl1", "stored", "l"))
        xl = (xl0, xl1)
        up_bank, out_bank = G.bank[0:6], G.bank[6:8]
        b1a, b1g, b2 = G.col(f"f_b1a{l}"), G.col(f"f_b1g{l}"), G.col(f"f_b2{l}")
        size = [P] * (HK - 1) + [HLAST]
        if finish:
            xs, xd = (G.io[n].rearrange("(k p) n -> p k n", p=P) for n in finish[0:2])
        with nc.Block() as block:
            @block.sync
            def _(sp):
                sp.dma_start(w1[:, :, :], G.io["w1"][l].rearrange("(k p) n -> p k n", p=P)).then_inc(weights, 16)
                sp.dma_start(w2[:, 0:HK - 1], G.io["w2"][l, 0:(HK - 1) * P].rearrange("(k p) n -> p k n", p=P)).then_inc(weights, 16)
                sp.dma_start(w2[0:HLAST, HK - 1], G.io["w2"][l, (HK - 1) * P:HID]).then_inc(weights, 16)
                if finish:
                    for t in range(NT + 2):
                        if t >= 2:
                            sp.wait_ge(res, t - 1)
                            sp.dma_start(xd[:, :, tok(t - 2)], xin[:, t % 2]).then_inc(stored, 16)
                            sp.wait_ge(stored, 16 * (t - 1))
                        if t < NT:
                            sp.dma_start(xin[:, t % 2], xs[:, :, tok(t)]).then_inc(xl[t % 2], 16)

            @block.tensor
            def _(pe):
                def up(t, p):
                    if t == 0:
                        pe.wait_ge(weights, 48)
                    for m in range(HK):
                        n = t * HK + m
                        M = size[m]
                        if past(n, 3):
                            pe.wait_ge(hidd, n - 2)
                        for j, done in ((1, gd), (0, ad)):
                            for k in range(KD):
                                mm = pe.matmul(up_bank[2 * (m % 3) + j][0:M, :], w1[:, k, j * HID + m * P:j * HID + m * P + M], S(k, t),
                                               start=(k == 0), stop=(k == KD - 1))
                            mm.then_inc(done, 1)

                def down(t, p):
                    pe.wait_ge(hidd, (t + 1) * HK)
                    if past(t, 1):
                        pe.wait_ge(res, t)
                    for m in range(KD):
                        for k in range(HK):
                            mm = pe.matmul(out_bank[m][:, :], w2[0:size[k], k, m * P:(m + 1) * P], hid[0:size[k], p, k], start=(k == 0), stop=(k == HK - 1))
                    mm.then_inc(w2d, 1)
                run(pe, NT, [(0, up), (1, down)])

            @block.scalar
            def _(act):
                def gelu(t, p):
                    for m in range(HK):
                        n, M = t * HK + m, size[m]
                        act.wait_ge(gd, n + 1)
                        if past(n, 2):
                            act.wait_ge(hidd, n - 1)
                        act.activation(gel[0:M, m % 2], up_bank[2 * (m % 3) + 1][0:M, :], ACT.Gelu, bias=b1g[0:M, m:m + 1]).then_inc(geld, 1)
                run(act, NT, [(0, gelu)])

            @block.vector
            def _(dve):
                link = chain(dve, link_s)

                def gate(t, p):
                    if past(t, 2):
                        dve.wait_ge(w2d, t - 1)
                    for m in range(HK):
                        n, M = t * HK + m, size[m]
                        dve.wait_ge(ad, n + 1)
                        dve.wait_ge(geld, n + 1)
                        dve.scalar_tensor_tensor(hid[0:M, p, m], up_bank[2 * (m % 3)][0:M, :], b1a[0:M, m:m + 1], gel[0:M, m % 2], ALU.add, ALU.mult).then_inc(hidd, 1)

                def residual(t, p):
                    dve.wait_ge(w2d, t + 1)
                    for h in range(KD):
                        i = dve.scalar_tensor_tensor(X(h, t), out_bank[h][:, :], b2[:, h:h + 1], X(h, t), ALU.add, ALU.add)
                        if finish:
                            link(i)
                    if finish:
                        dve.wait_ge(xl[p], 16 * (t // 2 + 1))
                        for h in range(KD):
                            i = dve.scalar_tensor_tensor(xin[:, p, h], X(h, t), finish[2][:, h:h + 1], xin[:, p, h], ALU.mult, ALU.add)
                    i.then_inc(res, 1)
                run(dve, NT, [(0, gate), (1, residual)])
        close()


def local_attention_stage(nc, G, src, dst):
    def plain(Z):
        return lambda k, t: Z[:, k, tok(t, 1)]

    def shifted(Z):
        return lambda k, t: Z[:, k, tok(t, 1 - k)]

    with ExitStack() as ctx:
        A, B = (ctx.enter_context(nc.sbuf_tensor(f"la_{n}", [P, KD, 1 + N], F32)) for n in "ab")
        zero_column(nc, G, "", [A])
        ln_pass(nc, G, "", plain(A), plain(A), G.eps5[:, :], G.mod[:, 0, CB:CB + KD], G.mod[:, 0, SB:SB + KD],
                load=load_x(G, src, A[:, :, 1:1 + N]))
        for l in range(DEPTH):
            attention_pass(nc, G, l, A, B)
            ln_pass(nc, G, "", shifted(B), plain(A), G.eps5[:, :], G.col(f"f_ln_g{l}"), G.col(f"f_ln_b{l}"))
            gated_mlp_pass(nc, G, l, plain(A), plain(B), (src, dst, G.mod[:, 0, GB:GB + KD]) if l == DEPTH - 1 else None)
            A, B = B, A


def s4d_params_pass(nc, G, prm):
    K = NL * HQ
    with ExitStack() as ctx:
        sb, sem, close = open_pass(nc, G, ctx)
        dt, ar, ai, cr, ci = (sb(n, [P, K]) for n in ("dt", "ar", "ai", "cr", "ci"))
        e1, s, c, a, b, q, r, den = (sb(n, [P, K]) for n in ("e1", "s", "c", "a", "b", "q", "r", "den"))
        zeros = sb("zeros", [Q4, HQ, C])
        loaded, cleared, stored, dv, ac = sem("p_loaded"), sem("p_cleared"), sem("p_stored"), sem("p_dv"), sem("p_ac")
        turns, rate, cre, cim, ncre = (x[:, :] for x in prm)
        with nc.Block() as block:
            @block.sync
            def _(sp):
                for n, t in (("s_log_dt", dt), ("s_A_re_log", ar), ("s_A_im", ai), ("s_C_re", cr), ("s_C_im", ci)):
                    sp.dma_start(t[:, :], G.io[n].rearrange("p l q -> p (l q)")).then_inc(loaded, 16)
                sp.wait_ge(cleared, 1)
                sp.dma_start(G.io["taps"][:, :, 0:C].rearrange("q a j -> a q j"), zeros[:, :, :]).then_inc(stored, 16)
                sp.wait_ge(stored, 16)

            @block.scalar
            def _(act):
                act.wait_ge(loaded, 80)
                act.activation(dt[:, :], dt[:, :], ACT.Exp).then_inc(ac, 1)
                act.activation(ar[:, :], ar[:, :], ACT.Exp).then_inc(ac, 1)
                act.wait_ge(dv, 4)
                act.activation(e1[:, :], rate, ACT.Tanh, scale=0.5).then_inc(ac, 1)
                act.wait_ge(dv, 8)
                act.activation(s[:, :], turns, ACT.Sin, scale=PI).then_inc(ac, 1)
                act.activation(c[:, :], a[:, :], ACT.Sin, scale=-PI, bias=G.half_pi[:, :]).then_inc(ac, 1)

            @block.vector
            def _(dve):
                link = chain(dve, dv)
                dve.wait_ge(ac, 2)
                link(dve.tensor_scalar(ar[:, :], ar[:, :], -1.0, None, ALU.mult))
                link(dve.tensor_tensor(rate, ar[:, :], dt[:, :], ALU.mult))
                link(dve.tensor_tensor(b[:, :], ai[:, :], dt[:, :], ALU.mult))
                link(dve.tensor_scalar(b[:, :], b[:, :], 1.0 / 6.283185307179586, None, ALU.mult))
                link(dve.tensor_scalar(q[:, :], b[:, :], MAGIC, None, ALU.add))
                link(dve.tensor_scalar(q[:, :], q[:, :], MAGIC, None, ALU.subtract))
                link(dve.tensor_tensor(turns, b[:, :], q[:, :], ALU.subtract))
                link(dve.scalar_tensor_tensor(a[:, :], turns, -1.0, turns, ALU.mult, ALU.max))
                dve.wait_ge(ac, 3)
                link(dve.tensor_scalar(q[:, :], e1[:, :], -1.0, 1.0, ALU.mult, ALU.add))
                link(dve.reciprocal(q[:, :], q[:, :]))
                link(dve.scalar_tensor_tensor(e1[:, :], e1[:, :], 2.0, q[:, :], ALU.mult, ALU.mult))
                dve.wait_ge(ac, 5)
                link(dve.scalar_tensor_tensor(a[:, :], s[:, :], 2.0, s[:, :], ALU.mult, ALU.mult))
                link(dve.scalar_tensor_tensor(b[:, :], s[:, :], 2.0, c[:, :], ALU.mult, ALU.mult))
                link(dve.tensor_tensor(q[:, :], e1[:, :], a[:, :], ALU.mult))
                link(dve.tensor_tensor(q[:, :], e1[:, :], q[:, :], ALU.subtract))
                link(dve.tensor_tensor(q[:, :], q[:, :], a[:, :], ALU.subtract))
                link(dve.scalar_tensor_tensor(r[:, :], e1[:, :], 1.0, b[:, :], ALU.add, ALU.mult))
                link(dve.tensor_tensor(a[:, :], ar[:, :], ar[:, :], ALU.mult))
                link(dve.tensor_tensor(b[:, :], ai[:, :], ai[:, :], ALU.mult))
                link(dve.tensor_tensor(den[:, :], a[:, :], b[:, :], ALU.add))
                link(dve.reciprocal(den[:, :], den[:, :]))
                link(dve.tensor_tensor(a[:, :], q[:, :], ar[:, :], ALU.mult))
                link(dve.tensor_tensor(b[:, :], r[:, :], ai[:, :], ALU.mult))
                link(dve.tensor_tensor(a[:, :], a[:, :], b[:, :], ALU.add))
                link(dve.tensor_tensor(b[:, :], r[:, :], ar[:, :], ALU.mult))
                link(dve.tensor_tensor(q[:, :], q[:, :], ai[:, :], ALU.mult))
                link(dve.tensor_tensor(b[:, :], b[:, :], q[:, :], ALU.subtract))
                link(dve.scalar_tensor_tensor(a[:, :], a[:, :], 2.0, den[:, :], ALU.mult, ALU.mult))
                link(dve.scalar_tensor_tensor(b[:, :], b[:, :], 2.0, den[:, :], ALU.mult, ALU.mult))
                link(dve.tensor_tensor(q[:, :], cr[:, :], a[:, :], ALU.mult))
                link(dve.tensor_tensor(r[:, :], ci[:, :], b[:, :], ALU.mult))
                link(dve.tensor_tensor(cre, q[:, :], r[:, :], ALU.subtract))
                link(dve.tensor_tensor(q[:, :], cr[:, :], b[:, :], ALU.mult))
                link(dve.tensor_tensor(r[:, :], ci[:, :], a[:, :], ALU.mult))
                link(dve.tensor_tensor(cim, q[:, :], r[:, :], ALU.add))
                link(dve.tensor_scalar(ncre, cre, -1.0, None, ALU.mult))

            @block.gpsimd
            def _(pool):
                pool.memset(zeros[:, :, :], 0.0).then_inc(cleared, 1)
        close()


def to_chunks_pass(nc, G, Z, Zr):
    with ExitStack() as ctx:
        sb, sem, close = open_pass(nc, G, ctx)
        turned, evA, evV = sem("turned"), sem("evA"), sem("evV")
        with nc.Block() as block:
            @block.tensor
            def _(pe):
                for n in range(NC // 2):
                    if n >= 4:
                        pe.wait_ge((evA, evV)[n % 2], (n - 4) // 2 + 1)
                    for a in range(2):
                        for h in range(KD):
                            t0 = (2 * n + a) * C
                            mm = pe.transpose(G.bank[n % 4][:, (KD * a + h) * P:(KD * a + h + 1) * P], Z[:, h, t0:t0 + C], G.ident[:, :])
                    mm.then_inc(turned, 1)

            def evacuate(eng, copy, first, done):
                for n in range(first, NC // 2, 2):
                    eng.wait_ge(turned, n + 1)
                    copy(Zr[:, :, 2 * n:2 * n + 2], G.bank[n % 4][:, :].rearrange("p (c h) -> p h c", c=2)).then_inc(done, 1)

            @block.scalar
            def _(act):
                evacuate(act, lambda o, i: act.activation(o, i, ACT.Copy), 0, evA)

            @block.vector
            def _(dve):
                evacuate(dve, dve.tensor_copy, 1, evV)
        close()


def convolution_pass(nc, G, l, prm, Zr, Yt):
    TW = C + 1 + NC
    S = GQ * NC
    with ExitStack() as ctx:
        sb, sem, close = open_pass(nc, G, ctx)
        ramp, quads = sb("ramp", [P, C + 1]), sb("quads", [P, Q4])
        skip = sb("skip", [Q4, HQ])
        ph, rd = sb("ph", [P, GQ, TW]), sb("rd", [P, GQ, TW])
        g128 = sb("g128", [P, HQ])
        g128r = sb("g128r", [P, HQ])
        r128 = sb("r128", [P, HQ])
        ex, sn, cs = ([sb(f"{n}{i}", [P, GQ, TW]) for i in range(3)] for n in ("ex", "sn", "cs"))
        er = sb("er", [P, 2, GQ, C + 1])
        tv = sb("tv", [P, 2, GQ, C])
        tp = sb("tp", [P, 2, GQ, C])
        gm = [sb(f"gm{i}", [P, 2, GQ, C]) for i in range(3)]
        bt = [sb(f"bt{i}", [P, 2, GQ, P]) for i in range(2)]
        krow = [sb(f"krow{i}", [Q4, GQ, C]) for i in range(2)]
        toep = [sb(f"toep{i}", [P, GC, C]) for i in range(2)]
        w = sb("w", [P, 4, GQ, NC])
        uh = sb("uh", [P, 2, GQ, NC])
        sh = sb("sh", [P, 2, GQ, NC])
        sw = sb("sw", [P, 4, GQ, NC])
        st = [sb(f"st{i}", [P, 2, GQ, Q4, NC]) for i in range(2)]
        names = ("consts", "phd", "exh", "trig", "erd", "gmV", "gmP", "taps", "kr", "ks0", "ks1", "tl0", "tl1", "btr", "btA", "btV",
                 "ud", "uread", "scand", "stV", "stP", "yd", "gel", "lv", "lp", "decd")
        (consts, phd, exh, trig, erd, gmV, gmP, taps, kr, ks0, ks1, tl0, tl1, btr, btA, btV,
         ud, uread, scand, stV, stP, yd, gel, lv, lp, decd) = (sem("c_" + n) for n in names)
        ks, tl = (ks0, ks1), (tl0, tl1)
        turns, rate, cre, cim, ncre = (x[:, l * HQ:(l + 1) * HQ] for x in prm)
        taps_bank, b_bank, u_bank, y_bank = G.bank[0], G.bank[1:3], G.bank[3:5], G.bank[5:7]
        tap_rows = G.io["taps"]
        qs = lambda g: slice(g * GQ, (g + 1) * GQ)
        bc = lambda v, g, n: v[:, qs(g)].unsqueeze(2).to_broadcast([P, GQ, n])
        rc = lambda v, n: v.unsqueeze(1).to_broadcast([P, GQ, n])
        with nc.Block() as block:
            @block.sync
            def _(sp):
                sp.dma_start(ramp[:, :], G.io["ramp"]).then_inc(consts, 16)
                sp.dma_start(quads[:, :], G.io["quads"]).then_inc(consts, 16)
                sp.dma_start(skip[:, :], G.io["s_D"][:, l, :]).then_inc(consts, 16)

                def store(g, p):
                    sp.wait_ge(kr, g + 1)
                    sp.dma_start(tap_rows[qs(g), :, C:2 * C].rearrange("q a j -> a q j"), krow[g % 2][:, :, :]).then_inc(ks[g % 2], 16)

                def load(g, p):
                    sp.wait_ge(ks[g % 2], 16 * (g // 2 + 1))
                    if past(g, 2):
                        sp.wait_ge(yd, g - 1)
                    at = tap_rows[g * GQ:g * GQ + 1, 0:1, 1:2]
                    src = bass.AP(tensor=at.tensor, offset=at.offset, ap=[[1, P], [2 * C, GC], [1, C]])
                    sp.dma_start(toep[g % 2][:, :, :], src).then_inc(tl[g % 2], 16)
                run(sp, NG, [(0, store), (0, load)], 2)

            @block.gpsimd
            def _(pool):
                link = chain(pool, lp)
                pool.wait_ge(consts, 48)
                pool.wait_ge(decd, 1)

                def exponents(g, p):
                    r = g % 3
                    if past(g, 3):
                        pool.wait_ge(stV, g - 2)
                        pool.wait_ge(stP, g - 2)
                    pool.tensor_tensor(ex[r][:, :, 0:C + 1], bc(rate, g, C + 1), rc(ramp[:, :], C + 1), ALU.mult)
                    pool.tensor_copy(ex[r][:, :, C + 1:TW], bc(r128, g, NC)).then_inc(exh, 1)

                def imaginary(g, p):
                    if past(g, 3):
                        pool.wait_ge(yd, g - 2)
                    pool.wait_ge(erd, g + 1)
                    pool.tensor_tensor(tp[:, 0], er[:, 1, :, 0:C], bc(ncre, g, C), ALU.mult)
                    link(pool.tensor_tensor(tp[:, 1], er[:, 0, :, 0:C], bc(cim, g, C), ALU.mult))
                    pool.tensor_tensor(gm[g % 3][:, 1], tp[:, 0], tp[:, 1], ALU.subtract).then_inc(gmP, 1)

                def state_im(g, p):
                    pool.wait_ge(scand, g + 1)
                    if past(g, 2):
                        pool.wait_ge(yd, g - 1)
                    R = slice(C + 1, TW)
                    pool.tensor_tensor(sw[:, 2], cs[g % 3][:, :, R], sh[:, 1], ALU.mult)
                    link(pool.tensor_tensor(sw[:, 3], sn[g % 3][:, :, R], sh[:, 0], ALU.mult))
                    link(pool.tensor_tensor(sw[:, 2], sw[:, 2], sw[:, 3], ALU.add))
                    pool.tensor_tensor(st[g % 2][:, 1], sw[:, 2].unsqueeze(2).to_broadcast([P, GQ, Q4, NC]),
                                       quads[:, :].unsqueeze(1).unsqueeze(3).to_broadcast([P, GQ, Q4, NC]), ALU.mult).then_inc(stP, 1)

                run(pool, NG, [(2, state_im), (0, exponents), (1, imaginary)], 2)

            @block.scalar
            def _(act):
                def trigonometry(g, p):
                    r = g % 3
                    act.wait_ge(phd, g + 1)
                    act.activation(sn[r][:, :, :], sn[r][:, :, :], ACT.Sin, scale=TWO_PI)
                    act.activation(cs[r][:, :, :], cs[r][:, :, :], ACT.Sin, scale=-TWO_PI, bias=G.half_pi[:, :])
                    act.wait_ge(exh, g + 1)
                    act.activation(ex[r][:, :, :], ex[r][:, :, :], ACT.Exp).then_inc(trig, 1)

                def inputs(g, p):
                    act.wait_ge(btr, 2 * g + 1)
                    if past(g, 2):
                        act.wait_ge(ud, g - 1)
                    act.activation(bt[g % 2][:, 0].rearrange("p q m -> p (q m)"), b_bank[0][:, :], ACT.Copy).then_inc(btA, 1)

                def gelu(g, p):
                    act.wait_ge(yd, g + 1)
                    act.activation(Yt[:, :, g * GC:(g + 1) * GC], y_bank[g % 2][:, :].rearrange("p (h c) -> p c h", h=GC), ACT.Gelu_apprx_tanh).then_inc(gel, 1)

                run(act, NG, [(1, inputs), (0, trigonometry), (3, gelu)], 2)

            @block.vector
            def _(dve):
                link = chain(dve, lv)
                dve.wait_ge(consts, 48)
                link(dve.tensor_scalar(g128[:, :], turns, float(C), None, ALU.mult))
                link(dve.tensor_scalar(g128r[:, :], g128[:, :], MAGIC, None, ALU.add))
                link(dve.tensor_scalar(g128r[:, :], g128r[:, :], MAGIC, None, ALU.subtract))
                link(dve.tensor_tensor(g128[:, :], g128[:, :], g128r[:, :], ALU.subtract))
                for x in st:
                    dve.memset(x[:, :, :, :, :], 0.0)
                link(dve.memset(uh[:, :, :, 0:1], 0.0))
                dve.tensor_scalar(r128[:, :], rate, float(C), None, ALU.mult).then_inc(decd, 1)

                def phases(g, p):
                    r = g % 3
                    dve.tensor_tensor(ph[:, :, 0:C + 1], bc(turns, g, C + 1), rc(ramp[:, :], C + 1), ALU.mult)
                    link(dve.tensor_tensor(ph[:, :, C + 1:TW], bc(g128, g, NC), rc(ramp[:, 0:NC], NC), ALU.mult))
                    link(dve.tensor_scalar(rd[:, :, :], ph[:, :, :], MAGIC, None, ALU.add))
                    link(dve.tensor_scalar(rd[:, :, :], rd[:, :, :], MAGIC, None, ALU.subtract))
                    if past(g, 3):
                        dve.wait_ge(stP, g - 2)
                    link(dve.tensor_tensor(sn[r][:, :, :], ph[:, :, :], rd[:, :, :], ALU.subtract))
                    dve.scalar_tensor_tensor(cs[r][:, :, :], sn[r][:, :, :], -1.0, sn[r][:, :, :], ALU.mult, ALU.max).then_inc(phd, 1)

                def bases(g, p):
                    r = g % 3
                    dve.wait_ge(trig, g + 1)
                    if past(g, 1):
                        dve.wait_ge(gmP, g)
                        dve.wait_ge(btr, 2 * g)
                    link(dve.memset(ex[r][:, :, C + 1:C + 2], 0.0))
                    dve.tensor_tensor(er[:, 0], ex[r][:, :, 0:C + 1], cs[r][:, :, 0:C + 1], ALU.mult)
                    dve.tensor_tensor(er[:, 1], ex[r][:, :, 0:C + 1], sn[r][:, :, 0:C + 1], ALU.mult).then_inc(erd, 1)
                    dve.wait_ge(erd, g + 1)
                    if past(g, 3):
                        dve.wait_ge(yd, g - 2)
                    dve.tensor_tensor(tv[:, 0], er[:, 0, :, 0:C], bc(cre, g, C), ALU.mult)
                    link(dve.tensor_tensor(tv[:, 1], er[:, 1, :, 0:C], bc(cim, g, C), ALU.mult))
                    dve.tensor_tensor(gm[g % 3][:, 0], tv[:, 0], tv[:, 1], ALU.subtract).then_inc(gmV, 1)

                def tap_row(g, p):
                    dve.wait_ge(taps, g + 1)
                    if past(g, 2):
                        dve.wait_ge(ks[g % 2], 16 * (g // 2))
                    link(dve.tensor_copy(krow[g % 2][:, :, :].rearrange("p q j -> p (q j)"), taps_bank[0:Q4, :]))
                    dve.tensor_tensor(krow[g % 2][:, :, 0], krow[g % 2][:, :, 0], skip[:, qs(g)], ALU.add).then_inc(kr, 1)
                    dve.wait_ge(btr, 2 * g + 2)
                    if past(g, 2):
                        dve.wait_ge(ud, g - 1)
                    dve.tensor_copy(bt[g % 2][:, 1].rearrange("p q m -> p (q m)"), b_bank[1][:, :]).then_inc(btV, 1)

                def scan(g, p):
                    r = g % 3
                    dve.wait_ge(ud, g + 1)
                    u = u_bank[g % 2][:, 0:2 * S].rearrange("p (r q c) -> p r q c", r=2, q=GQ)
                    R1, R = slice(C + 2, TW), slice(C + 1, TW)
                    for j, (tab, part) in enumerate(((cs, 0), (sn, 1), (cs, 1), (sn, 0))):
                        i = dve.tensor_tensor(w[:, j, :, 1:NC], tab[r][:, :, R1], u[:, part, :, 0:NC - 1], ALU.mult)
                    i.then_inc(uread, 1)
                    dve.wait_ge(uread, g + 1)
                    dve.tensor_tensor(uh[:, 0, :, 1:NC], w[:, 0, :, 1:NC], w[:, 1, :, 1:NC], ALU.add)
                    link(dve.tensor_tensor(uh[:, 1, :, 1:NC], w[:, 2, :, 1:NC], w[:, 3, :, 1:NC], ALU.subtract))
                    if past(g, 1):
                        dve.wait_ge(stP, g)
                    link(dve.tensor_copy(w[:, 0], ex[r][:, :, R]))
                    for part in range(2):
                        i = dve.tensor_tensor_scan(sh[:, part].rearrange("p q c -> p (q c)"), w[:, 0].rearrange("p q c -> p (q c)"),
                                                   uh[:, part].rearrange("p q c -> p (q c)"), 0.0, ALU.mult, ALU.add)
                    i.then_inc(scand, 1)
                    dve.wait_ge(scand, g + 1)
                    if past(g, 2):
                        dve.wait_ge(yd, g - 1)
                    dve.tensor_tensor(sw[:, 0], cs[r][:, :, R], sh[:, 0], ALU.mult)
                    link(dve.tensor_tensor(sw[:, 1], sn[r][:, :, R], sh[:, 1], ALU.mult))
                    for a in range(Q4):
                        R = slice(SN * a, SN * (a + 1))
                        i = dve.tensor_tensor(st[g % 2][R, 0, :, a], sw[R, 0], sw[R, 1], ALU.subtract)
                    i.then_inc(stV, 1)

                run(dve, NG, [(1, bases), (2, scan), (1, tap_row), (0, phases)], 2)

            @block.tensor
            def _(pe):
                pe.wait_ge(consts, 48)

                def tables(g, p):
                    pe.wait_ge(gmV, g + 1)
                    if past(g, 1):
                        pe.wait_ge(kr, g)
                    pe.matmul(taps_bank[0:Q4, :], quads[:, :], gm[g % 3][:, 0].rearrange("p q j -> p (q j)"), start=True, stop=True).then_inc(taps, 1)
                    for part, ev in ((0, btA), (1, btV)):
                        if past(g, 1):
                            pe.wait_ge(ev, g)
                        for q in range(GQ):
                            mm = pe.transpose(b_bank[part][:, q * P:(q + 1) * P], er[:, part, q, 1:C + 1], G.ident[:, :])
                        mm.then_inc(btr, 1)

                def inputs(g, p):
                    pe.wait_ge(btA, g + 1)
                    pe.wait_ge(btV, g + 1)
                    if past(g, 2):
                        pe.wait_ge(uread, g - 1)
                    for q in range(GQ):
                        for a in range(Q4):
                            for part in range(2):
                                mm = pe.matmul(u_bank[g % 2][SN * a:SN * (a + 1), (part * GQ + q) * NC:(part * GQ + q + 1) * NC],
                                               bt[g % 2][:, part, q, SN * a:SN * (a + 1)], Zr[:, (g * GQ + q) * Q4 + a], start=True, stop=True)
                    mm.then_inc(ud, 1)

                def outputs(g, p):
                    pe.wait_ge(tl[g % 2], 16 * (g // 2 + 1))
                    pe.wait_ge(gmP, g + 1)
                    pe.wait_ge(stV, g + 1)
                    pe.wait_ge(stP, g + 1)
                    if past(g, 2):
                        pe.wait_ge(gel, g - 1)
                    for q in range(GQ):
                        four = y_bank[g % 2][:, q * Q4 * NC:(q + 1) * Q4 * NC]
                        for part in range(2):
                            pe.matmul(four, gm[g % 3][:, part, q], st[g % 2][:, part, q].rearrange("p a c -> p (a c)"),
                                      start=(part == 0), stop=False)
                        for a in range(Q4):
                            mm = pe.matmul(y_bank[g % 2][:, (q * Q4 + a) * NC:(q * Q4 + a + 1) * NC], toep[g % 2][:, q * Q4 + a],
                                           Zr[:, (g * GQ + q) * Q4 + a], start=False, stop=(a == Q4 - 1))
                    mm.then_inc(yd, 1)

                run(pe, NG, [(2, inputs), (1, tables), (3, outputs)], 2)
        close()


def s4d_out_pass(nc, G, l, Yt, H, finish=None):
    CT = TT // C
    with ExitStack() as ctx:
        sb, sem, close = open_pass(nc, G, ctx)
        wt = sb("so_w", [P, KD, 2 * D])
        y = sb("so_y", [P, 2, KD, TT])
        th = sb("so_th", [P, 2, KD, TT])
        hb = sb("so_hb", [P, KD])
        xin = sb("so_x", [P, 2, KD, TT])
        weights, tr, yA, yV, od, thd, res, o1r, hbd, xl0, xl1, stored, link_s = (
            sem("so_" + n) for n in ("weights", "tr", "yA", "yV", "od", "thd", "res", "o1r", "hbd", "xl0", "xl1", "stored", "l"))
        xl = (xl0, xl1)
        tr_bank, o_bank = G.bank[0:4], G.bank[4:8]
        b = G.col(f"s_b{l}")
        if finish:
            xs, xd = (G.io[n].rearrange("(k p) n -> p k n", p=P) for n in finish[0:2])
        with nc.Block() as block:
            @block.sync
            def _(sp):
                sp.dma_start(wt[:, :, :], G.io["s_W"][l].rearrange("(k p) n -> p k n", p=P)).then_inc(weights, 16)
                if finish:
                    for t in range(NT + 2):
                        if t >= 2:
                            sp.wait_ge(res, t - 1)
                            sp.dma_start(xd[:, :, tok(t - 2)], xin[:, t % 2]).then_inc(stored, 16)
                            sp.wait_ge(stored, 16 * (t - 1))
                        if t < NT:
                            sp.dma_start(xin[:, t % 2], xs[:, :, tok(t)]).then_inc(xl[t % 2], 16)

            @block.tensor
            def _(pe):
                def turn(t, p):
                    for h, ev in ((0, yA), (1, yV)):
                        if past(t, 2):
                            pe.wait_ge(ev, t - 1)
                        for c in range(CT):
                            mm = pe.transpose(tr_bank[2 * p + h][:, c * C:(c + 1) * C], Yt[:, t * CT + c, h * P:(h + 1) * P], G.ident[:, :])
                        mm.then_inc(tr, 1)

                def project(t, p):
                    if t == 0:
                        pe.wait_ge(weights, 16)
                    pe.wait_ge(yA, t + 1)
                    pe.wait_ge(yV, t + 1)
                    for m in (2, 3, 0, 1):
                        if past(t, 1):
                            pe.wait_ge(thd if m >= 2 else o1r, t)
                        for k in range(KD):
                            mm = pe.matmul(o_bank[m][:, :], wt[:, k, m * P:(m + 1) * P], y[:, p, k], start=(k == 0), stop=(k == KD - 1))
                        if m in (3, 1):
                            mm.then_inc(od, 1)
                run(pe, NT, [(0, turn), (1, project)])

            @block.scalar
            def _(act):
                def evacuate(t, p):
                    act.wait_ge(tr, 2 * t + 1)
                    if past(t, 2):
                        act.wait_ge(od, 2 * (t - 1))
                    act.activation(y[:, p, 0], tr_bank[2 * p][:, :], ACT.Copy).then_inc(yA, 1)

                def sigmoid(t, p):
                    if t == 0:
                        act.wait_ge(hbd, 1)
                    act.wait_ge(od, 2 * t + 1)
                    if past(t, 2):
                        act.wait_ge(res, t - 1)
                    for h in range(KD):
                        i = act.activation(th[:, p, h], o_bank[2 + h][:, :], ACT.Tanh, scale=0.5, bias=hb[:, h:h + 1])
                    i.then_inc(thd, 1)
                run(act, NT, [(0, evacuate), (1, sigmoid)])

            @block.vector
            def _(dve):
                link = chain(dve, link_s)
                dve.tensor_scalar(hb[:, :], b[:, KD:2 * KD], 0.5, None, ALU.mult).then_inc(hbd, 1)

                def evacuate(t, p):
                    dve.wait_ge(tr, 2 * t + 2)
                    if past(t, 2):
                        dve.wait_ge(od, 2 * (t - 1))
                    dve.tensor_copy(y[:, p, 1], tr_bank[2 * p + 1][:, :]).then_inc(yV, 1)

                def residual(t, p):
                    dve.wait_ge(thd, t + 1)
                    link(dve.tensor_scalar(th[:, p], th[:, p], 1.0, 0.5, ALU.add, ALU.mult))
                    dve.wait_ge(od, 2 * t + 2)
                    for h in range(KD):
                        i = dve.scalar_tensor_tensor(th[:, p, h], o_bank[h][:, :], b[:, h:h + 1], th[:, p, h], ALU.add, ALU.mult)
                    i.then_inc(o1r, 1)
                    dve.wait_ge(o1r, t + 1)
                    i = dve.tensor_tensor(H[:, :, tok(t)], H[:, :, tok(t)], th[:, p], ALU.add)
                    if finish:
                        link(i)
                        dve.wait_ge(xl[p], 16 * (t // 2 + 1))
                        for h in range(KD):
                            i = dve.scalar_tensor_tensor(xin[:, p, h], H[:, h, tok(t)], finish[2][:, h:h + 1], xin[:, p, h], ALU.mult, ALU.add)
                    i.then_inc(res, 1)
                run(dve, NT, [(0, evacuate), (1, residual)])
        close()


def s4d_stage(nc, G, src, dst):
    with ExitStack() as ctx:
        sb = lambda n, s: ctx.enter_context(nc.sbuf_tensor(n, s, F32))
        prm = [sb("s_" + n, [P, NL * HQ]) for n in ("turns", "rate", "cre", "cim", "ncre")]
        H = sb("s_h", [P, KD, N])
        Z = sb("s_z", [P, KD, N])
        Zr = sb("s_zr", [P, D, NC])
        Yt = Z[:, :, :].rearrange("p k n -> p (k n)").rearrange("p (c h) -> p c h", h=D)
        Hv = lambda k, t: H[:, k, tok(t)]
        Zv = lambda k, t: Z[:, k, tok(t)].rearrange("p (c j) -> p c j", j=C)[:, :, ::-1]
        s4d_params_pass(nc, G, prm)
        ln_pass(nc, G, "", Hv, Hv, G.eps5[:, :], G.mod[:, 1, CA:CA + KD], G.mod[:, 1, SA:SA + KD], load=load_x(G, src, H))
        for l in range(NL):
            ln_pass(nc, G, "", Hv, Zv, G.eps5[:, :], G.col(f"s_ln_w{l}"), G.col(f"s_ln_b{l}"))
            to_chunks_pass(nc, G, Z, Zr)
            convolution_pass(nc, G, l, prm, Zr, Yt)
            s4d_out_pass(nc, G, l, Yt, H, (src, dst, G.mod[:, 1, GA:GA + KD]) if l == NL - 1 else None)


def ffn_pass(nc, G, S, src, dst):
    MF = FF // P
    with ExitStack() as ctx:
        sb, sem, close = open_pass(nc, G, ctx)
        w1, w2 = sb("w1", [P, KD, FF]), sb("w2", [P, KD, FF])
        h1, h2 = sb("h1", [P, MF, FF]), sb("h2", [P, MF, FF])
        w3 = sb("w3", [P, MF, D])
        u = sb("u", [P, MF, TT])
        v = sb("v", [P, MF, TT])
        gated = sb("gated", [P, 2, TT])
        xin = sb("xin", [P, KD, TT])
        out_scale = sb("out_scale", [P, KD])
        weights = [sem(f"w{i}") for i in range(5)]
        w1d, w2d, silud, w2ev, ud, h1d, vd, h2d, zd, w3d, res, xload, stored, scaled = (
            sem(n) for n in ("w1d", "w2d", "silud", "w2ev", "ud", "h1d", "vd", "h2d", "zd", "w3d", "res", "xload", "stored", "scaled"))
        ring = G.bank[0:6]
        out_bank = G.bank[6:8]
        gate = G.mod[:, 1, GB:GB + KD]
        s1, s2, sh1, sh2, s3 = (G.col(n) for n in ("w1_s", "w2_s", "h1_s", "h2_s", "w3_s"))
        xs = G.io[src].rearrange("(k p) n -> p k n", p=P)
        xd = G.io[dst].rearrange("(k p) n -> p k n", p=P)
        with nc.Block() as block:
            @block.sync
            def _(sp):
                for i, (n, b) in enumerate((("g_w1", w1), ("g_w2", w2), ("g_h1", h1), ("g_h2", h2), ("g_w3", w3))):
                    sp.dma_start(b[:, :, :], G.io[n].rearrange("(k p) n -> p k n", p=P)).then_inc(weights[i], 16)

                def load(t, p):
                    if past(t, 1):
                        sp.wait_ge(stored, 16 * t)
                    sp.dma_start(xin[:, :, :], xs[:, :, tok(t)]).then_inc(xload, 16)
                    sp.wait_ge(res, t + 1)
                    sp.dma_start(xd[:, :, tok(t)], xin[:, :, :]).then_inc(stored, 16)
                run(sp, NT, [(0, load)])
                sp.wait_ge(stored, 16 * NT)

            @block.tensor
            def _(pe):
                def tile(t, p):
                    if t == 0:
                        pe.wait_ge(weights[0], 16)
                        pe.wait_ge(weights[1], 16)
                    for m in range(MF):
                        n = t * MF + m
                        if past(n, 2):
                            pe.wait_ge(ud, n - 1)
                        for j, w, s in ((0, w1, w1d), (1, w2, w2d)):
                            for k in range(KD):
                                mm = pe.matmul(ring[2 * (m % 2) + j][:, :], w[:, k, m * P:(m + 1) * P], S[:, k, tok(t)],
                                               start=(k == 0), stop=(k == KD - 1))
                            mm.then_inc(s, 1)
                    for w, wait, ready, done, freed, src_buf in ((h1, weights[2], ud, h1d, vd, u), (h2, weights[3], vd, h2d, zd, v)):
                        if t == 0:
                            pe.wait_ge(wait, 16)
                        for m in range(MF):
                            n = t * MF + m
                            if m >= 2:
                                pe.wait_ge(freed, n - 1)
                            elif w is h2:
                                pe.wait_ge(vd, n + MF - 1)
                            elif past(t, 1):
                                pe.wait_ge(zd, n - 1)
                            for k in range(MF):
                                if m == 0:
                                    pe.wait_ge(ready, t * MF + k + 1)
                                mm = pe.matmul(ring[4 + m % 2][:, :], w[:, k, m * P:(m + 1) * P], src_buf[:, k], start=(k == 0), stop=(k == MF - 1))
                            mm.then_inc(done, 1)
                    if t == 0:
                        pe.wait_ge(weights[4], 16)
                    if past(t, 1):
                        pe.wait_ge(res, t)
                    for m in range(KD):
                        for k in range(MF):
                            if m == 0:
                                pe.wait_ge(zd, t * MF + k + 1)
                            mm = pe.matmul(out_bank[m][:, :], w3[:, k, m * P:(m + 1) * P], u[:, k], start=(k == 0), stop=(k == MF - 1))
                    mm.then_inc(w3d, 1)
                run(pe, NT, [(0, tile)])

            @block.scalar
            def _(act):
                def tile(t, p):
                    if past(t, 1):
                        act.wait_ge(w3d, t)
                    for m in range(MF):
                        n = t * MF + m
                        act.wait_ge(w1d, n + 1)
                        if past(n, 2):
                            act.wait_ge(ud, n - 1)
                        act.activation(gated[:, m % 2], ring[2 * (m % 2)][:, :], ACT.Silu, scale=s1[:, m:m + 1]).then_inc(silud, 1)
                    for m in range(MF):
                        act.wait_ge(h1d, t * MF + m + 1)
                        act.activation(v[:, m], ring[4 + m % 2][:, :], ACT.Gelu, scale=sh1[:, m:m + 1]).then_inc(vd, 1)
                    for m in range(MF):
                        act.wait_ge(h2d, t * MF + m + 1)
                        act.activation(u[:, m], ring[4 + m % 2][:, :], ACT.Gelu, scale=sh2[:, m:m + 1]).then_inc(zd, 1)
                run(act, NT, [(0, tile)])

            @block.vector
            def _(dve):
                dve.tensor_tensor(out_scale[:, :], gate, s3, ALU.mult).then_inc(scaled, 1)
                dve.wait_ge(scaled, 1)

                def tile(t, p):
                    if past(t, 1):
                        dve.wait_ge(w3d, t)
                    for m in range(MF):
                        n = t * MF + m
                        dve.wait_ge(silud, n + 1)
                        dve.wait_ge(w2d, n + 1)
                        dve.scalar_tensor_tensor(u[:, m], ring[2 * (m % 2) + 1][:, :], s2[:, m:m + 1], gated[:, m % 2], ALU.mult, ALU.mult).then_inc(ud, 1)
                    dve.wait_ge(w3d, t + 1)
                    dve.wait_ge(xload, 16 * (t + 1))
                    for h in range(KD):
                        i = dve.scalar_tensor_tensor(xin[:, h], out_bank[h][:, :], out_scale[:, h:h + 1], xin[:, h], ALU.mult, ALU.add)
                    i.then_inc(res, 1)
                run(dve, NT, [(0, tile)])
        close()


def ffn_stage(nc, G, src, dst):
    with ExitStack() as ctx:
        S = ctx.enter_context(nc.sbuf_tensor("ff_s", [P, KD, N], F32))
        Sv = lambda k, t: S[:, k, tok(t)]
        ln_pass(nc, G, "", Sv, Sv, G.eps5[:, :], G.mod[:, 1, CB:CB + KD], G.mod[:, 1, SB:SB + KD], load=load_x(G, src, S))
        ffn_pass(nc, G, S, src, dst)


def program(nc, io, stages="0123"):
    G = Shared()
    G.io, G.passes = io, 0
    with ExitStack() as ctx:
        sb = lambda name, shape, dt=F32: ctx.enter_context(nc.sbuf_tensor(name, shape, dt))
        G.cols = sb("cols", [P, NCOLS])
        G.ident = sb("ident", [P, P])
        G.mean_w = sb("mean_w", [P, P])
        G.mod = sb("mod", [P, 2, 12])
        G.eps3, G.eps5, G.half_pi = sb("eps3", [P, 1]), sb("eps5", [P, 1]), sb("half_pi", [P, 1])
        G.bank = [ctx.enter_context(nc.psum_tensor(f"bank{i}", [P, TT], F32)) for i in range(8)]
        G.col = lambda name: G.cols[:, COLS[name][0]:COLS[name][0] + COLS[name][1]]
        setup_pass(nc, G, "")
        for s, stage in (("0", rwkv_stage), ("1", local_attention_stage), ("2", s4d_stage), ("3", ffn_stage)):
            if s in stages:
                stage(nc, G, f"x{s}", f"x{int(s) + 1}")


def constants():
    import numpy as np
    c = {"ident": np.eye(P, dtype=np.float32)}
    i, j = np.arange(W)[:, None], np.arange(W)[None, :]
    now, before, never = (np.where(m, 0.0, -1e30) for m in (j <= i, j >= i, np.zeros((W, W), bool)))
    c["masks"] = np.stack([np.concatenate(m, 1) for m in ((now, before), (before, now), (now, never))], 1).astype(np.float32)
    half = np.arange(0, DH, 2, dtype=np.float32)
    inv = (1.0 / np.power(np.float32(10000.0), half / np.float32(DH))).astype(np.float32)
    t = np.arange(N, dtype=np.float32)
    fr = np.tile((t[:, None] * inv[None, :]).astype(np.float32), (1, 2)).astype(np.float64)
    base = (half + 0.4 * DH) / (1.4 * DH)
    sc = np.tile(base[None, :] ** ((t - N // 2) / float(W // 2))[:, None], (1, 2)).astype(np.float64)
    sign = np.where(np.arange(DH) < DH // 2, -1.0, 1.0)[None, :]
    rot = np.stack([np.cos(fr) * sc * 8.0, np.sin(fr) * sc * 8.0 * sign, np.cos(fr) / sc, np.sin(fr) / sc * sign], 1)
    c["rotary"] = np.ascontiguousarray(rot.astype(np.float32).reshape(NW, W, 4, DH))
    c["ramp"] = np.ascontiguousarray(np.broadcast_to(np.arange(C + 1, dtype=np.float32), (P, C + 1)))
    c["quads"] = np.ascontiguousarray((np.arange(P)[:, None] // SN == np.arange(Q4)[None, :]).astype(np.float32))
    return c


def lay_out(inp):
    import numpy as np
    a = {}

    def per_feature(v, n):
        v = np.asarray(v)
        full = np.zeros((n * P,), v.dtype)
        full[:v.shape[0]] = v
        return full.reshape(n, P).T

    vec = {}
    for k in ("ln1_g", "ln1_b", "ln2_g", "ln2_b", "tm_mix_k", "tm_mix_v", "tm_mix_r", "time_decay", "time_first", "cm_mix_k", "cm_mix_r"):
        vec[k] = inp["L0_attn_" + k]
    vec["c0"], vec["c1"] = inp["L0_c"][0], inp["L1_c"][0]
    for l in range(DEPTH):
        vec[f"f_ln_g{l}"], vec[f"f_ln_b{l}"] = inp["L0_ffn_ln_g"][l], inp["L0_ffn_ln_b"][l]
        vec[f"f_b1a{l}"], vec[f"f_b1g{l}"] = inp["L0_ffn_b1"][l][:HID], inp["L0_ffn_b1"][l][HID:]
        vec[f"f_b2{l}"] = inp["L0_ffn_b2"][l]
    for l in range(NL):
        vec[f"s_ln_w{l}"], vec[f"s_ln_b{l}"] = inp["L1_attn_ln_w"][l], inp["L1_attn_ln_b"][l]
        vec[f"s_b{l}"] = inp["L1_attn_b_out"][l]
    for k in ("w1_s", "w2_s", "h1_s", "h2_s", "w3_s"):
        vec[k] = inp["L1_ffn_" + k]
    a["cols"] = np.ascontiguousarray(np.concatenate([per_feature(vec[k], COLS[k][1]) for k in COLS], axis=1))
    a["wmod0"], a["wmod1"] = inp["L0_wmod"], inp["L1_wmod"]
    for k in ("tm_Wk", "tm_Wv", "tm_Wr", "Wo", "cm_Wk", "cm_Wv", "cm_Wr"):
        a[k] = inp["L0_attn_" + k]
    for k in ("wqkv", "q_scale", "k_scale", "wo", "w1", "w2"):
        a[k] = inp["L0_ffn_" + k]

    def by_quads(v, axis_n=True):
        v = np.asarray(v)
        if not axis_n:
            v = np.broadcast_to(v[:, :, None], (NL, D, SN))
        return np.ascontiguousarray(v.reshape(NL, HQ, Q4, SN).transpose(2, 3, 0, 1).reshape(P, NL, HQ))

    a["s_log_dt"] = by_quads(inp["L1_attn_log_dt"], False)
    for k in ("A_re_log", "A_im", "C_re", "C_im"):
        a["s_" + k] = by_quads(inp["L1_attn_" + k])
    a["s_D"] = np.ascontiguousarray(np.asarray(inp["L1_attn_D_skip"]).reshape(NL, HQ, Q4).transpose(2, 0, 1))
    a["s_W"] = np.ascontiguousarray(np.asarray(inp["L1_attn_W_out"]).transpose(0, 2, 1))
    for k in ("w1", "w2", "h1", "h2", "w3"):
        a["g_" + k] = np.ascontiguousarray(np.asarray(inp[f"L1_ffn_{k}_w"]).T)
    a.update(constants())
    return {k: np.ascontiguousarray(v) for k, v in a.items()}


def kernel(**inputs):
    import numpy as np
    import concourse.bacc as bacc
    from concourse.bass_utils import run_bass_kernel_spmd

    nc = bacc.Bacc("TRN2", target_bir_lowering=False, num_devices=1)
    arrays = {"in_" + k: v for k, v in lay_out({k: np.asarray(v) for k, v in inputs.items()}).items()}
    arrays["in_x0"] = np.ascontiguousarray(np.asarray(inputs["L0_attn_inputs"])[0].T)
    io = {k[3:]: nc.dram_tensor(k, v.shape, mybir.dt.from_np(v.dtype), kind="ExternalInput").ap() for k, v in arrays.items()}
    for s in (1, 2, 3):
        io[f"x{s}"] = nc.dram_tensor(f"x{s}", [D, N], F32, kind="Internal").ap()
    io["taps"] = nc.dram_tensor("taps", [HQ, Q4, 2 * C], F32, kind="Internal").ap()
    io["x4"] = nc.dram_tensor("out_x", [D, N], F32, kind="ExternalOutput").ap()
    program(nc, io)
    r = run_bass_kernel_spmd(nc, [arrays], core_ids=[0])
    return np.ascontiguousarray(r.results[0]["out_x"].T)[None]
```

```python
from contextlib import ExitStack

import concourse.bass as bass
from concourse import mybir

F32 = mybir.dt.float32
F32R = mybir.dt.float32r
I32 = mybir.dt.int32
BF16 = mybir.dt.bfloat16
ALU = mybir.AluOpType
ACT = mybir.ActivationFunctionType
AX = mybir.AxisListType

P = 128
D = 256
KD = D // P
N = 4096
TT = 512
NT = N // TT
W = 128
NW = N // W
HEADS, DH = 8, 64
INNER = HEADS * DH
DEPTH = 2
HID = 682
HK = -(-HID // P)
HLAST = HID - (HK - 1) * P
CM = 4 * D
FF = 1024
NL = 4
SN = 32
Q4 = 4
HQ = D // Q4
C = 128
NC = N // C
GQ = 4
GC = GQ * Q4
NG = HQ // GQ
MAGIC = 1.5 * 2.0 ** 23
TWO_PI = 6.2831850
PI = TWO_PI / 2

COLS = {}


def _cols():
    at = 0
    for name, n in ([(k, KD) for k in (
            "ln1_g", "ln1_b", "ln2_g", "ln2_b", "tm_mix_k", "tm_mix_v", "tm_mix_r",
            "time_decay", "time_first", "cm_mix_k", "cm_mix_r", "c0", "c1")]
            + [(f"f_ln_g{l}", KD) for l in range(DEPTH)] + [(f"f_ln_b{l}", KD) for l in range(DEPTH)]
            + [(f"f_b1a{l}", HK) for l in range(DEPTH)] + [(f"f_b1g{l}", HK) for l in range(DEPTH)]
            + [(f"f_b2{l}", KD) for l in range(DEPTH)]
            + [(f"s_ln_w{l}", KD) for l in range(NL)] + [(f"s_ln_b{l}", KD) for l in range(NL)]
            + [(f"s_b{l}", 2 * KD) for l in range(NL)]
            + [("w1_s", FF // P), ("w2_s", FF // P), ("h1_s", FF // P), ("h2_s", FF // P), ("w3_s", KD)]):
        COLS[name] = (at, n)
        at += n
    return at


NCOLS = _cols()
SA, CA, GA, SB, CB, GB = (KD * j for j in range(6))


class Shared:
    pass


def known(t):
    return isinstance(t, int)


def past(t, k):
    return not known(t) or t >= k


def run(eng, n, steps, width=2):
    deepest = max(lag for lag, _ in steps)
    head = -(-(deepest + width) // width) * width
    loops = (n - head) // width
    if n < 24:
        head, loops = n, 0

    def straight(s):
        for lag, f in steps:
            if 0 <= s - lag < n:
                f(s - lag, (s - lag) % width)

    for s in range(head):
        straight(s)
    if loops:
        with eng.Fori(head // width, head // width + loops) as turn:
            for j in range(width):
                for lag, f in steps:
                    f(turn * width + (j - lag), (j - lag) % width)
    for s in range(head + loops * width, n + deepest):
        straight(s)


def open_pass(nc, G, ctx):
    G.passes += 1
    sems, mark = [], f"_{G.passes}"

    def sb(name, shape, dt=F32):
        return ctx.enter_context(nc.sbuf_tensor(name + mark, shape, dt))

    def sem(name):
        s = nc.alloc_semaphore(name + mark)
        sems.append(s)
        return s

    def close():
        nc.clear_and_free_semaphores(sems)
        nc.all_engine_barrier()

    return sb, sem, close


def chain(eng, sem):
    count = [0]

    def link(ins):
        count[0] += 1
        ins.then_inc(sem, 1)
        eng.wait_ge(sem, count[0])

    return link


def tok(t, shift=0, size=TT):
    return bass.ds(t * size + shift, size)


def setup_pass(nc, G, tag):
    with ExitStack() as ctx:
        sb, sem, close = open_pass(nc, G, ctx)
        wmod = sb("wmod", [P, 2, KD, 6 * D])
        silu_c = sb("silu_c", [P, 2, KD])
        sign = sb("sign", [P, 2, 12])
        mag = sb("mag", [P, 2, 12])
        loaded, wloaded = sem("loaded"), sem("wloaded")
        silu_ready, mod_ready, link_s = sem("silu_ready"), sem("mod_ready"), sem("link_s")
        with nc.Block() as block:
            @block.sync
            def _(sp):
                sp.dma_start(G.cols[:, :], G.io["cols"]).then_inc(loaded, 16)
                sp.dma_start(G.ident[:, :], G.io["ident"]).then_inc(loaded, 16)
                for l in range(2):
                    sp.dma_start(wmod[:, l], G.io[f"wmod{l}"].rearrange("(k p) n -> p k n", p=P)).then_inc(wloaded, 16)
                sp.wait_ge(loaded, 32)

            @block.scalar
            def _(act):
                act.wait_ge(loaded, 32)
                for l in range(2):
                    act.activation(silu_c[:, l], G.col(f"c{l}"), ACT.Silu).then_inc(silu_ready, 1)

            @block.tensor
            def _(pe):
                pe.wait_ge(silu_ready, 2)
                pe.wait_ge(wloaded, 32)
                for l in range(2):
                    for m in range(12):
                        for k in range(KD):
                            mm = pe.matmul(G.bank[l][:, m:m + 1], wmod[:, l, k, m * P:(m + 1) * P],
                                           silu_c[:, l, k:k + 1], start=(k == 0), stop=(k == KD - 1))
                    mm.then_inc(mod_ready, 1)

            @block.vector
            def _(dve):
                link = chain(dve, link_s)
                dve.memset(G.mean_w[:, :], 1.0 / D)
                dve.memset(G.eps3[:, :], 1e-3)
                dve.memset(G.half_pi[:, :], TWO_PI / 4)
                dve.memset(G.eps5[:, :], 1e-5)
                dve.wait_ge(mod_ready, 2)
                for l in range(2):
                    M = G.mod[:, l, :]
                    link(dve.tensor_copy(M, G.bank[l][:, 0:12]))
                    link(dve.tensor_scalar(sign[:, l], M, 0.0, 2.0, ALU.is_ge, ALU.mult))
                    link(dve.tensor_scalar(sign[:, l], sign[:, l], -1.0, None, ALU.add))
                    link(dve.tensor_tensor(mag[:, l], sign[:, l], M, ALU.mult))
                    link(dve.tensor_scalar(mag[:, l], mag[:, l], 0.25, None, ALU.max))
                    for at in (CA, CB):
                        link(dve.tensor_scalar(M[:, at:at + KD], M[:, at:at + KD], 1.0, None, ALU.add))
                    for at in (GA, GB):
                        link(dve.tensor_tensor(M[:, at:at + KD], mag[:, l, at:at + KD], sign[:, l, at:at + KD], ALU.mult))
        close()


def ln_pass(nc, G, tag, src, dst, eps, gain, bias, load=None, also=None, store=None):
    with ExitStack() as ctx:
        sb, sem, close = open_pass(nc, G, ctx)
        xc = sb("ln_xc", [P, 3, KD, TT])
        sq = sb("ln_sq", [P, 2, KD, TT])
        inv = sb("ln_inv", [P, 2, TT])
        src_loaded = [sem(f"src_loaded{t}") for t in range(NT)] if load is not None else []
        mean_ready, centered = sem("mean_ready"), sem("centered")
        squared, var_ready, log_ready = sem("squared"), sem("var_ready"), sem("log_ready")
        inv_ready, normed, affined = sem("inv_ready"), sem("normed"), sem("affined")
        mean_bank, var_bank = G.bank[0:2], G.bank[2:4]
        if also:
            also.open(sb, sem)
            stored = sem("stored")
        with nc.Block() as block:
            if load is not None:
                @block.sync
                def _(sp):
                    load(sp, src_loaded)
                    if also:
                        def store_tile(t, p):
                            sp.wait_ge(affined, t + 1)
                            sp.dma_start(G.io[store[1]].rearrange("(k p) n -> p k n", p=P)[:, :, tok(t)], store[0][:, :, tok(t)]).then_inc(stored, 16)
                        run(sp, NT, [(0, lambda t, p: also.load(sp, t)), (3, store_tile)])
                        sp.wait_ge(stored, 16 * NT)

            if also:
                @block.gpsimd
                def _(pool):
                    run(pool, NT, [(0, lambda t, p: also.subtract(pool, t))])

            @block.tensor
            def _(pe):
                def mean(t, p):
                    if load is not None:
                        pe.wait_ge(src_loaded[t], 16)
                    if past(t, 2):
                        pe.wait_ge(centered, t - 1)
                    for k in range(KD):
                        mm = pe.matmul(mean_bank[p][:, :], G.mean_w[:, :], src(k, t), start=(k == 0), stop=(k == KD - 1))
                    mm.then_inc(mean_ready, 1)

                def var(t, p):
                    pe.wait_ge(squared, t + 1)
                    if past(t, 2):
                        pe.wait_ge(log_ready, t - 1)
                    for k in range(KD):
                        mm = pe.matmul(var_bank[p][:, :], G.mean_w[:, :], sq[:, p, k], start=(k == 0), stop=(k == KD - 1))
                    mm.then_inc(var_ready, 1)

                run(pe, NT, [(0, mean), (1, var)])
                if also:
                    also.count(pe)

            @block.vector
            def _(dve):
                def center(t, p):
                    dve.wait_ge(mean_ready, t + 1)
                    if past(t, 3):
                        dve.wait_ge(affined, t - 2)
                    for k in range(KD):
                        i = dve.tensor_tensor(xc[:, t % 3, k], src(k, t), mean_bank[p][:, :], ALU.subtract)
                    i.then_inc(centered, 1)

                def norm(t, p):
                    dve.wait_ge(inv_ready, t + 1)
                    for k in range(KD):
                        i = dve.tensor_tensor(xc[:, t % 3, k], xc[:, t % 3, k], inv[:, p], ALU.mult)
                    i.then_inc(normed, 1)

                def affine(t, p):
                    dve.wait_ge(normed, t + 1)
                    for k in range(KD):
                        out = dst(k, t)
                        x = xc[:, t % 3, k] if len(out.shape) == 2 else xc[:, t % 3, k].rearrange("p (c j) -> p c j", j=out.shape[2])
                        i = dve.tensor_scalar(out, x, gain[:, k:k + 1], bias[:, k:k + 1], ALU.mult, ALU.add)
                    i.then_inc(affined, 1)

                run(dve, NT, [(0, center), (2, affine), (1, norm)])
                if also:
                    also.decide(dve)

            @block.scalar
            def _(act):
                def square(t, p):
                    act.wait_ge(centered, t + 1)
                    if past(t, 2):
                        act.wait_ge(var_ready, t - 1)
                    act.activation(sq[:, p], xc[:, t % 3], ACT.Square).then_inc(squared, 1)

                def root(t, p):
                    act.wait_ge(var_ready, t + 1)
                    if past(t, 2):
                        act.wait_ge(normed, t - 1)
                    act.activation(inv[:, p], var_bank[p][:, :], ACT.Ln, bias=eps).then_inc(log_ready, 1)
                    act.wait_ge(log_ready, t + 1)
                    act.activation(inv[:, p], inv[:, p], ACT.Exp, scale=-0.5).then_inc(inv_ready, 1)

                act.preload_act_table_set("natural_log_exp_and_others")
                weights = [(0, lambda t, p: also.round(act, t)), (1, lambda t, p: also.sum_rests(act, t))] if also else []
                run(act, NT, [(0, square), (1, root)] + weights)
        close()


def load_x(G, name, X):
    def load(sp, done):
        for t in range(NT):
            sp.dma_start(X[:, :, t * TT:(t + 1) * TT],
                         G.io[name].rearrange("(k p) n -> p k n", p=P)[:, :, t * TT:(t + 1) * TT]).then_inc(done[t], 16)
    return load


def time_mix_pass(nc, G, H, S):
    with ExitStack() as ctx:
        sb, sem, close = open_pass(nc, G, ctx)
        wkvr = sb("tm_w", [P, 3, KD, D])
        wo = sb("tm_wo", [P, KD, D])
        decay = sb("decay", [P, KD, TT])
        wdec = sb("wdec", [P, KD])
        d = sb("tm_d", [P, 2, KD, TT])
        mix = sb("tm_mix", [P, 3, KD, TT])
        mixr = sb("tm_mixr", [P, KD, TT])
        kvr = sb("tm_kvr", [P, 2, 3, KD, TT])
        pp = sb("tm_pp", [P, 2, KD, 1 + TT])
        ab = sb("tm_ab", [P, 1, 2, KD, 1 + TT])
        ex = sb("tm_ex", [P, 2, 4, KD, TT])
        ev = sb("tm_ev", [P, 1, 2, KD, TT])
        rw = sb("tm_rw", [P, 1, KD, TT])
        names = ("weights", "dif", "mixk", "mixv", "mixr_h", "mixr", "proj", "evac", "args", "exps", "evs", "out", "wod", "res", "dec", "l")
        weights, dif, mixk, mixv, mixr_h, mixr_s, proj, evac, args, exps, evs, out, wod, res, dec, link_s = (sem("tm_" + n) for n in names)
        kvr_bank, wo_bank = G.bank[0:6], G.bank[6:8]
        cols = [G.col(n) for n in ("tm_mix_k", "tm_mix_v", "tm_mix_r")]
        u = G.col("time_first")
        with nc.Block() as block:
            @block.sync
            def _(sp):
                for j, n in enumerate(("tm_Wk", "tm_Wv", "tm_Wr")):
                    sp.dma_start(wkvr[:, j], G.io[n].rearrange("(k p) n -> p k n", p=P)).then_inc(weights, 16)
                sp.dma_start(wo[:, :, :], G.io["Wo"].rearrange("(k p) n -> p k n", p=P)).then_inc(weights, 16)

            @block.gpsimd
            def _(pool):
                def mixes(t, p):
                    if past(t, 2):
                        pool.wait_ge(mixv, t - 1)
                        pool.wait_ge(mixr_s, t - 1)
                    pool.tensor_tensor(d[:, p], S[:, :, tok(t, 1)], S[:, :, tok(t)], ALU.subtract).then_inc(dif, 1)
                    pool.wait_ge(dif, t + 1)
                    if past(t, 1):
                        pool.wait_ge(proj, t)
                        pool.wait_ge(mixr_s, t)
                    for k in range(KD):
                        i = pool.tensor_scalar(mixr[:, k], d[:, p, k], cols[2][:, k:k + 1], None, ALU.mult)
                    i.then_inc(mixr_h, 1)
                    pool.wait_ge(mixr_h, t + 1)
                    pool.tensor_tensor(mix[:, 2], mixr[:, :], S[:, :, tok(t)], ALU.add).then_inc(mixr_s, 1)

                def weighted(t, p):
                    pool.wait_ge(exps, t + 1)
                    if past(t, 1):
                        pool.wait_ge(out, t)
                    pool.tensor_tensor(ev[:, 0, 0], ex[:, p, 1], kvr[:, p, 1], ALU.mult)
                    pool.tensor_tensor(ev[:, 0, 1], ex[:, p, 3], kvr[:, p, 1], ALU.mult).then_inc(evs, 1)

                run(pool, NT, [(2, weighted), (0, mixes)])

            @block.tensor
            def _(pe):
                def project(t, p):
                    if t == 0:
                        pe.wait_ge(weights, 64)
                    pe.wait_ge(mixk, t + 1)
                    pe.wait_ge(mixv, t + 1)
                    pe.wait_ge(mixr_s, t + 1)
                    if t >= 1:
                        pe.wait_ge(evac, t)
                    for j in range(3):
                        for m in range(KD):
                            for k in range(KD):
                                mm = pe.matmul(kvr_bank[2 * j + m][:, :], wkvr[:, j, k, m * P:(m + 1) * P], mix[:, j, k],
                                               start=(k == 0), stop=(k == KD - 1))
                    mm.then_inc(proj, 1)

                def outproj(t, p):
                    pe.wait_ge(out, t + 1)
                    if t >= 1:
                        pe.wait_ge(res, t)
                    for m in range(KD):
                        for k in range(KD):
                            mm = pe.matmul(wo_bank[m][:, :], wo[:, k, m * P:(m + 1) * P], rw[:, 0, k], start=(k == 0), stop=(k == KD - 1))
                    mm.then_inc(wod, 1)

                run(pe, NT, [(0, project), (2, outproj)])

            @block.scalar
            def _(act):
                act.activation(wdec[:, :], G.col("time_decay"), ACT.Exp).then_inc(dec, 1)

                def evacuate(t, p):
                    act.wait_ge(proj, t + 1)
                    if t >= 2:
                        act.wait_ge(out, t - 1)
                    for j in range(3):
                        for m in range(KD):
                            i = act.activation(kvr[:, p, j, m], kvr_bank[2 * j + m][:, :], ACT.Tanh if j == 2 else ACT.Copy,
                                               scale=0.5 if j == 2 else 1.0)
                    i.then_inc(evac, 1)

                def exponents(t, p):
                    act.wait_ge(args, t + 1)
                    act.activation(ex[:, p], ex[:, p], ACT.Exp).then_inc(exps, 1)

                run(act, NT, [(0, evacuate), (1, exponents)])

            @block.vector
            def _(dve):
                link = chain(dve, link_s)
                dve.wait_ge(dec, 1)
                link(dve.tensor_scalar(wdec[:, :], wdec[:, :], -1.0, None, ALU.mult))
                link(dve.memset(decay[:, :, :], 0.0))
                for k in range(KD):
                    link(dve.tensor_scalar(decay[:, k], decay[:, k], wdec[:, k:k + 1], None, ALU.add))
                dve.memset(pp[:, 0, :, 0:1], -1e38)
                link(dve.memset(ab[:, 0, :, :, 0:1], 0.0))

                def mixes(t, p):
                    dve.wait_ge(dif, t + 1)
                    if t >= 1:
                        dve.wait_ge(proj, t)
                    for j, s in ((0, mixk), (1, mixv)):
                        for k in range(KD):
                            i = dve.scalar_tensor_tensor(mix[:, j, k], d[:, p, k], cols[j][:, k:k + 1], S[:, k, tok(t)], ALU.mult, ALU.add)
                        i.then_inc(s, 1)

                def arguments(t, p):
                    dve.wait_ge(evac, t + 1)
                    if t >= 1:
                        link(dve.tensor_copy(pp[:, p, :, 0:1], pp[:, 1 - p, :, TT:TT + 1]))
                    K = kvr[:, p, 0]
                    for h in range(KD):
                        link(dve.tensor_tensor_scan(pp[:, p, h, 1:1 + TT], decay[:, h], K[:, h], pp[:, p, h, 0:1], ALU.add, ALU.max))
                    prev, cur = pp[:, p, :, 0:TT], pp[:, p, :, 1:1 + TT]
                    for h in range(KD):
                        dve.scalar_tensor_tensor(ex[:, p, 0, h], prev[:, h], wdec[:, h:h + 1], cur[:, h], ALU.add, ALU.subtract)
                        link(dve.scalar_tensor_tensor(ex[:, p, 2, h], K[:, h], u[:, h:h + 1], prev[:, h], ALU.add, ALU.max))
                    dve.tensor_tensor(ex[:, p, 1], K, cur, ALU.subtract)
                    for h in range(KD):
                        link(dve.scalar_tensor_tensor(ex[:, p, 3, h], K[:, h], u[:, h:h + 1], ex[:, p, 2, h], ALU.add, ALU.subtract))
                    dve.tensor_tensor(ex[:, p, 2], prev, ex[:, p, 2], ALU.subtract).then_inc(args, 1)

                def wkv(t, p):
                    dve.wait_ge(evs, t + 1)
                    if t >= 1:
                        link(dve.tensor_copy(ab[:, 0, :, :, 0:1], ab[:, 0, :, :, TT:TT + 1]))
                    for h in range(KD):
                        dve.tensor_tensor_scan(ab[:, 0, 0, h, 1:1 + TT], ex[:, p, 0, h], ev[:, 0, 0, h], ab[:, 0, 0, h, 0:1], ALU.mult, ALU.add)
                        link(dve.tensor_tensor_scan(ab[:, 0, 1, h, 1:1 + TT], ex[:, p, 0, h], ex[:, p, 1, h], ab[:, 0, 1, h, 0:1], ALU.mult, ALU.add))
                    num, den = ex[:, p, 0], ex[:, p, 1]
                    dve.tensor_tensor(den, ex[:, p, 2], ab[:, 0, 1, :, 0:TT], ALU.mult)
                    link(dve.tensor_tensor(num, ex[:, p, 2], ab[:, 0, 0, :, 0:TT], ALU.mult))
                    dve.tensor_tensor(den, den, ex[:, p, 3], ALU.add)
                    link(dve.tensor_tensor(num, num, ev[:, 0, 1], ALU.add))
                    link(dve.reciprocal(den, den))
                    link(dve.tensor_tensor(num, num, den, ALU.mult))
                    if t >= 1:
                        dve.wait_ge(wod, t)
                    dve.scalar_tensor_tensor(rw[:, 0], kvr[:, p, 2], 1.0, num, ALU.add, ALU.mult).then_inc(out, 1)

                def residual(t, p):
                    dve.wait_ge(wod, t + 1)
                    for h in range(KD):
                        i = dve.scalar_tensor_tensor(H[:, h, tok(t)], wo_bank[h][:, :], 0.5, H[:, h, tok(t)], ALU.mult, ALU.add)
                    i.then_inc(res, 1)

                run(dve, NT, [(0, mixes), (2, wkv), (1, arguments), (3, residual)])
        close()


def channel_mix_pass(nc, G, H, S, src, dst):
    MF = CM // P
    with ExitStack() as ctx:
        sb, sem, close = open_pass(nc, G, ctx)
        wk = sb("cm_wk", [P, KD, CM])
        wv = sb("cm_wv", [P, MF, D])
        wr = sb("cm_wr", [P, KD, D])
        d = sb("cm_d", [P, KD, TT])
        mix = sb("cm_mix", [P, 2, 2, KD, TT])
        kc = sb("cm_kc", [P, 2, MF, TT])
        th = sb("cm_th", [P, 2, KD, TT])
        xin = sb("cm_x", [P, 2, KD, TT])
        weights, dif, mixed, krdy, kev, ksq, rrdy, tanhed, vrdy, res, xload, stored, link_s = (
            sem("cm_" + n) for n in ("weights", "dif", "mixed", "krdy", "kev", "ksq", "rrdy", "tanhed", "vrdy", "res", "xload", "stored", "l"))
        xld = [xload, sem("cm_xload1")]
        k_bank, r_bank, v_bank = G.bank[0:4], G.bank[4:6], G.bank[6:8]
        mk, mr = G.col("cm_mix_k"), G.col("cm_mix_r")
        gate = G.mod[:, 0, GA:GA + KD]
        xs = G.io[src].rearrange("(k p) n -> p k n", p=P)
        xd = G.io[dst].rearrange("(k p) n -> p k n", p=P)
        with nc.Block() as block:
            @block.sync
            def _(sp):
                sp.dma_start(wr[:, :, :], G.io["cm_Wr"].rearrange("(k p) n -> p k n", p=P)).then_inc(weights, 16)
                sp.dma_start(wk[:, :, :], G.io["cm_Wk"].rearrange("(k p) n -> p k n", p=P)).then_inc(weights, 16)
                sp.dma_start(wv[:, :, :], G.io["cm_Wv"].rearrange("(k p) n -> p k n", p=P)).then_inc(weights, 16)
                for t in range(NT):
                    if t >= 2:
                        sp.wait_ge(res, t - 1)
                        sp.dma_start(xd[:, :, tok(t - 2)], xin[:, t % 2]).then_inc(stored, 16)
                        sp.wait_ge(stored, 16 * (t - 1))
                    sp.dma_start(xin[:, t % 2], xs[:, :, tok(t)]).then_inc(xld[t % 2], 16)
                for t in range(NT, NT + 2):
                    sp.wait_ge(res, t - 1)
                    sp.dma_start(xd[:, :, tok(t - 2)], xin[:, t % 2]).then_inc(stored, 16)
                sp.wait_ge(stored, 16 * NT)

            @block.gpsimd
            def _(pool):
                def mixes(t, p):
                    if t >= 1:
                        pool.wait_ge(mixed, t)
                    pool.tensor_tensor(d[:, :], S[:, :, tok(t, 1)], S[:, :, tok(t)], ALU.subtract).then_inc(dif, 1)
                run(pool, NT, [(0, mixes)])

            @block.tensor
            def _(pe):
                def front(t, p):
                    if t == 0:
                        pe.wait_ge(weights, 48)
                    pe.wait_ge(mixed, t + 1)
                    if t >= 1:
                        pe.wait_ge(tanhed, t)
                    for m in range(KD):
                        for k in range(KD):
                            mm = pe.matmul(r_bank[m][:, :], wr[:, k, m * P:(m + 1) * P], mix[:, p, 1, k], start=(k == 0), stop=(k == KD - 1))
                    mm.then_inc(rrdy, 1)
                    for m in range(MF):
                        n = t * MF + m
                        if n >= 4:
                            pe.wait_ge(kev, n - 3)
                        for k in range(KD):
                            mm = pe.matmul(k_bank[m % 4][:, :], wk[:, k, m * P:(m + 1) * P], mix[:, p, 0, k], start=(k == 0), stop=(k == KD - 1))
                        mm.then_inc(krdy, 1)

                def back(t, p):
                    if t >= 1:
                        pe.wait_ge(res, t)
                    for m in range(KD):
                        for k in range(MF):
                            if m == 0:
                                pe.wait_ge(ksq, t * MF + k + 1)
                            mm = pe.matmul(v_bank[m][:, :], wv[:, k, m * P:(m + 1) * P], kc[:, p, k], start=(k == 0), stop=(k == MF - 1))
                    mm.then_inc(vrdy, 1)

                run(pe, NT, [(1, front), (2, back)])

            @block.scalar
            def _(act):
                def front(t, p):
                    act.wait_ge(rrdy, t + 1)
                    if t >= 2:
                        act.wait_ge(res, t - 1)
                    for m in range(KD):
                        i = act.activation(th[:, p, m], r_bank[m][:, :], ACT.Tanh, scale=0.5)
                    i.then_inc(tanhed, 1)

                def relu(t, p):
                    if t >= 2:
                        act.wait_ge(vrdy, t - 1)
                    for m in range(MF):
                        act.wait_ge(krdy, t * MF + m + 1)
                        act.activation(kc[:, p, m], k_bank[m % 4][:, :], ACT.Relu).then_inc(kev, 1)

                for s in range(NT):
                    relu(s, s % 2)
                    front(s, s % 2)

            @block.vector
            def _(dve):
                link = chain(dve, link_s)

                def mixes(t, p):
                    dve.wait_ge(dif, t + 1)
                    if t >= 2:
                        dve.wait_ge(krdy, (t - 1) * MF)
                    for j, col in ((0, mk), (1, mr)):
                        for k in range(KD):
                            i = dve.scalar_tensor_tensor(mix[:, p, j, k], d[:, k], col[:, k:k + 1], S[:, k, tok(t)], ALU.mult, ALU.add)
                    i.then_inc(mixed, 1)

                def square(t, p):
                    for m in range(MF):
                        dve.wait_ge(kev, t * MF + m + 1)
                        dve.tensor_tensor(kc[:, p, m], kc[:, p, m], kc[:, p, m], ALU.mult).then_inc(ksq, 1)

                def residual(t, p):
                    dve.wait_ge(tanhed, t + 1)
                    dve.wait_ge(vrdy, t + 1)
                    dve.wait_ge(xld[p], 16 * (t // 2 + 1))
                    for h in range(KD):
                        link(dve.scalar_tensor_tensor(th[:, p, h], th[:, p, h], 1.0, v_bank[h][:, :], ALU.add, ALU.mult))
                    for h in range(KD):
                        link(dve.scalar_tensor_tensor(H[:, h, tok(t)], th[:, p, h], 0.5, H[:, h, tok(t)], ALU.mult, ALU.add))
                    for h in range(KD):
                        i = dve.scalar_tensor_tensor(xin[:, p, h], H[:, h, tok(t)], gate[:, h:h + 1], xin[:, p, h], ALU.mult, ALU.add)
                    i.then_inc(res, 1)

                run(dve, NT, [(0, mixes), (1, square), (2, residual)])
        close()


def zero_column(nc, G, tag, bufs):
    with nc.Block() as block:
        @block.vector
        def _(dve):
            for b in bufs:
                dve.memset(b[:, :, 0:1], 0.0)


def rwkv_stage(nc, G, src, dst):
    with ExitStack() as ctx:
        H = ctx.enter_context(nc.sbuf_tensor("rw_h", [P, KD, N], F32))
        S = ctx.enter_context(nc.sbuf_tensor("rw_s", [P, KD, 1 + N], F32))
        Sv = lambda k, t: S[:, k, tok(t, 1)]
        Hv = lambda k, t: H[:, k, tok(t)]
        zero_column(nc, G, "", [S])
        ln_pass(nc, G, "", Hv, Hv, G.eps5[:, :], G.mod[:, 0, CA:CA + KD], G.mod[:, 0, SA:SA + KD], load=load_x(G, src, H))
        ln_pass(nc, G, "", Hv, Sv, G.eps3[:, :], G.col("ln1_g"), G.col("ln1_b"))
        time_mix_pass(nc, G, H, S)
        ln_pass(nc, G, "", Hv, Sv, G.eps3[:, :], G.col("ln2_g"), G.col("ln2_b"))
        channel_mix_pass(nc, G, H, S, src, dst)


def attention_pass(nc, G, l, X, Y):
    with ExitStack() as ctx:
        sb, sem, close = open_pass(nc, G, ctx)
        wqkv = sb("wqkv", [P, KD, 3 * INNER])
        wo = sb("wo", [P, INNER // P, D])
        masks = sb("masks", [P, 3, 2 * W], BF16)
        masks32 = sb("masks32", [P, 3, 2 * W])
        identb = sb("identb", [P, P], BF16)
        scales = sb("scales", [P, 4, DH])
        rot = [sb(f"rot{i}", [P, 4, DH]) for i in range(2)]
        rots = [sb(f"rots{i}", [P, 4, DH]) for i in range(2)]
        hs = [sb(f"hs{i}", [P, KD, W]) for i in range(4)]
        qk = [sb(f"qk{i}", [P, 2, HEADS, DH]) for i in range(2)]
        v = [sb(f"v{i}", [P, INNER]) for i in range(4)]
        sq = sb("sq", [P, 2, HEADS, DH])
        ss = [sb(f"ss{i}", [P, 2, HEADS]) for i in range(2)]
        rn = [sb(f"rn{i}", [P, 2, HEADS]) for i in range(2)]
        half = sb("half", [P, 2, HEADS])
        ra = sb("ra", [P, 2, HEADS, DH])
        rb = sb("rb", [P, 2, HEADS, DH])
        qkr = [sb(f"qkr{i}", [P, 2, INNER]) for i in range(2)]
        qT = [sb(f"qT{i}", [P, HEADS // 2, W]) for i in range(2)]
        kT = sb("kT", [P, HEADS // 2, 2, W])
        nmax = [sb(f"nmax{i}", [P, HEADS]) for i in range(2)]
        rsum = [sb(f"rsum{i}", [P, HEADS]) for i in range(2)]
        rinv = [sb(f"rinv{i}", [P, HEADS]) for i in range(2)]
        pr = [sb(f"pr{i}", [P, HEADS, 2, W]) for i in range(2)]
        pT = sb("pT", [P, HEADS, 2, W])
        o = [sb(f"o{i}", [P, INNER]) for i in range(2)]
        oT = sb("oT", [P, INNER // P, W])
        names = ("weights", "consts", "scal", "rotld0", "rotld1", "rotsc", "hsr", "projq", "projk", "projv", "qev", "kev", "vev",
                 "sqd", "ssd", "rnh", "rnd", "ram", "rbm", "rsumd", "qkrd", "trq", "trk", "qTd", "kTd", "sc", "mx", "ex",
                 "pt", "ptA", "ptV", "pv", "rid", "od", "otr", "oTd", "wod", "res", "zeroed")
        (weights, consts, scal, rotld0, rotld1, rotsc, hsr, projq, projk, projv, qev, kev, vev,
         sqd, ssd, rnh, rnd, ram, rbm, rsumd, qkrd, trq, trk, qTd, kTd, sc, mx, ex,
         pt, ptA, ptV, pv, rid, od, otr, oTd, wod, res, zeroed) = (sem("a_" + n) for n in names)
        rotld = (rotld0, rotld1)
        proj_bank, turn_bank, score_bank, value_bank = G.bank[0:2], G.bank[2:4], G.bank[4:7], G.bank[7]
        QUAD = ((0, 2), (1, 3), (4, 6), (5, 7))
        qs, ks = G.io["q_scale"], G.io["k_scale"]
        with nc.Block() as block:
            @block.sync
            def _(sp):
                sp.dma_start(wqkv[:, :, :], G.io["wqkv"][l].rearrange("(k p) n -> p k n", p=P)).then_inc(weights, 16)
                sp.dma_start(wo[:, :, :], G.io["wo"][l].rearrange("(k p) n -> p k n", p=P)).then_inc(weights, 16)
                sp.dma_start(masks32[:, :, :], G.io["masks"]).then_inc(consts, 16)
                for j, s in ((0, qs), (2, ks)):
                    row = s[l:l + 1, :]
                    sp.dma_start(scales[:, j], row.to_broadcast([P, DH])).then_inc(consts, 16)
                    for a in (0, DH // 2):
                        b = DH // 2 - a
                        sp.dma_start(scales[:, j + 1, a:a + DH // 2], row[:, b:b + DH // 2].to_broadcast([P, DH // 2])).then_inc(consts, 16)

                def table(t, p):
                    if past(t, 2):
                        sp.wait_ge(rotsc, t - 1)
                    sp.dma_start(rot[p % 2][:, :, :], G.io["rotary"][t] if known(t) else G.io["rotary"][bass.ds(t, 1)].rearrange("a p j d -> p (a j) d")).then_inc(rotld[p % 2], 16)
                run(sp, NW, [(0, table)], 4)

            @block.gpsimd
            def _(pool):
                pool.wait_ge(consts, 16 * 7)

                def shift(t, p):
                    if past(t, 4):
                        pool.wait_ge(projv, t - 3)
                    pool.tensor_copy(hs[p][:, 0], X[:, 0, tok(t, 1, W)])
                    pool.tensor_copy(hs[p][:, 1], X[:, 1, tok(t, 0, W)]).then_inc(hsr, 1)
                    pool.wait_ge(rotld[p % 2], 16 * (t // 2 + 1) if known(t) else (t - p % 2) * 8 + 16)
                    if past(t, 2):
                        pool.wait_ge(rbm, t - 1)
                    pool.tensor_tensor(rots[p % 2][:, :, :], rot[p % 2][:, :, :], scales[:, :, :], ALU.mult).then_inc(rotsc, 1)

                def norms(t, p):
                    pool.wait_ge(ssd, t + 1)
                    if past(t, 2):
                        pool.wait_ge(qkrd, t - 1)
                    pool.tensor_tensor(rn[p % 2][:, :, :], ss[p % 2][:, :, :], half[:, :, :], ALU.pow).then_inc(rnd, 1)

                def add(t, p):
                    pool.wait_ge(ram, t + 1)
                    pool.wait_ge(rbm, t + 1)
                    pool.tensor_tensor(ra[:, :, :, :], ra[:, :, :, :], rb[:, :, :, :], ALU.add).then_inc(rsumd, 1)

                pool.wait_ge(zeroed, 1)
                run(pool, NW, [(0, shift), (1, add), (1, norms)], 4)

            @block.tensor
            def _(pe):
                pe.wait_ge(weights, 32)
                pe.wait_ge(zeroed, 1)

                def product(t, p, j, bank, done):
                    for k in range(KD):
                        mm = pe.matmul(proj_bank[bank][:, :], hs[p][:, k], wqkv[:, k, j * INNER:(j + 1) * INNER],
                                       start=(k == 0), stop=(k == KD - 1))
                    mm.then_inc(done, 1)

                def project_qk(t, p):
                    pe.wait_ge(hsr, t + 1)
                    if past(t, 1):
                        pe.wait_ge(qev, t)
                    product(t, p, 0, 0, projq)
                    if past(t, 1):
                        pe.wait_ge(vev, t)
                    product(t, p, 1, 1, projk)

                def project_v(t, p):
                    pe.wait_ge(kev, t + 1)
                    product(t, p, 2, 1, projv)

                def turn_qk(t, p):
                    pe.wait_ge(qkrd, t + 1)
                    if past(t, 3):
                        pe.wait_ge(oTd, t - 2)
                        pe.wait_ge(res, t - 2)
                    elif t == 2:
                        pe.wait_ge(ptA, 2 * (t - 1))
                        pe.wait_ge(ptV, 2 * (t - 1))
                    elif t == 1:
                        pe.wait_ge(qTd, t)
                        pe.wait_ge(kTd, t)
                    for j, done in ((0, trq), (1, trk)):
                        for c in range(HEADS // 2):
                            mm = pe.transpose(turn_bank[j][:, c * W:(c + 1) * W], qkr[p % 2][:, j, c * P:(c + 1) * P], G.ident[:, :])
                        mm.then_inc(done, 1)

                def scores(t, p):
                    pe.wait_ge(qTd, t + 1)
                    pe.wait_ge(kTd, t + 1)
                    which = 2 if known(t) and t == 0 else p % 2
                    for i, heads in enumerate(QUAD):
                        bank = i % 3
                        if i == 3:
                            pe.wait_ge(ex, 4 * t + 1)
                        elif past(t, 1):
                            pe.wait_ge(ex, 4 * t - 2 + i if i else 4 * t)
                        for a, h in enumerate(heads):
                            r = slice(DH * (h % 2), DH * (h % 2) + DH)
                            out = score_bank[bank][:, a * 2 * W:(a + 1) * 2 * W]
                            pe.matmul(out, qT[p % 2][r, h // 2], kT[r, h // 2].rearrange("p s w -> p (s w)"), start=True, stop=False)
                            mm = pe.matmul(out, identb[:, :], masks[:, which], start=False, stop=True)
                        mm.then_inc(sc, 1)

                def turn_p(t, p):
                    pe.wait_ge(ex, 4 * t + 4)
                    for i in range(4):
                        if i < 2:
                            n = min(t + 2, NW) if known(t) else t + 2
                            pe.wait_ge((qTd, kTd)[i], n)
                            if known(t) and t + 1 >= NW:
                                pe.wait_ge((oTd, res)[i], t - 1)
                        else:
                            pe.wait_ge((ptA, ptV)[i % 2], 2 * t + 1)
                        for a in range(4):
                            h, s = 2 * i + a // 2, a % 2
                            mm = pe.transpose(turn_bank[i % 2][:, a * W:(a + 1) * W], pr[p % 2][:, h, s], G.ident[:, :])
                        mm.then_inc(pt, 1)

                def values(t, p):
                    pe.wait_ge(ptA, 2 * t + 2)
                    pe.wait_ge(ptV, 2 * t + 2)
                    pe.wait_ge(vev, t + 1)
                    if past(t, 1):
                        pe.wait_ge(od, t)
                    for h in range(HEADS):
                        for s in range(2):
                            vw = v[p] if s == p % 2 else v[(p - 1) % 4]
                            mm = pe.matmul(value_bank[:, h * DH:(h + 1) * DH], pT[:, h, s], vw[:, h * DH:(h + 1) * DH], start=(s == 0), stop=(s == 1))
                    mm.then_inc(pv, 1)

                def turn_o(t, p):
                    pe.wait_ge(od, t + 1)
                    pe.wait_ge(ptA, min(2 * t + 4, 2 * NW) if known(t) else 2 * t + 4)
                    for c in range(INNER // P):
                        mm = pe.transpose(turn_bank[0][:, c * W:(c + 1) * W], o[p % 2][:, c * P:(c + 1) * P], G.ident[:, :])
                    mm.then_inc(otr, 1)

                def outproj(t, p):
                    pe.wait_ge(oTd, t + 1)
                    pe.wait_ge(ptV, min(2 * t + 4, 2 * NW) if known(t) else 2 * t + 4)
                    for m in range(KD):
                        for k in range(INNER // P):
                            mm = pe.matmul(turn_bank[1][:, m * W:(m + 1) * W], wo[:, k, m * P:(m + 1) * P], oT[:, k], start=(k == 0), stop=(k == INNER // P - 1))
                    mm.then_inc(wod, 1)

                run(pe, NW, [(4, turn_p), (5, turn_o), (3, scores), (5, outproj), (4, values), (1, project_v), (2, turn_qk), (0, project_qk)], 4)

            @block.scalar
            def _(act):
                def turned_p(t, p):
                    if past(t, 1):
                        act.wait_ge(pv, t)
                    for i in (0, 2):
                        act.wait_ge(pt, 4 * t + i + 1)
                        act.activation(pT[:, 2 * i:2 * i + 2].rearrange("p h s w -> p (h s w)"), turn_bank[0][:, :], ACT.Copy).then_inc(ptA, 1)

                def exponentials(t, p):
                    if past(t, 2):
                        act.wait_ge(pt, 4 * (t - 1))
                        act.wait_ge(rid, t - 1)
                    for i, heads in enumerate(QUAD):
                        act.wait_ge(mx, 4 * t + i + 1)
                        for a, h in enumerate(heads):
                            e = act.activation(pr[p % 2][:, h].rearrange("p s w -> p (s w)"), score_bank[i % 3][:, a * 2 * W:(a + 1) * 2 * W],
                                               ACT.Exp, bias=nmax[p % 2][:, h:h + 1], accum_out=rsum[p % 2][:, h:h + 1])
                        e.then_inc(ex, 1)

                def turned_o(t, p):
                    act.wait_ge(otr, t + 1)
                    if past(t, 1):
                        act.wait_ge(wod, t)
                    act.activation(oT[:, :, :].rearrange("p k w -> p (k w)"), turn_bank[0][:, :], ACT.Copy).then_inc(oTd, 1)

                def turned_q(t, p):
                    act.wait_ge(trq, t + 1)
                    if past(t, 2):
                        act.wait_ge(sc, 4 * (t - 1))
                    act.activation(qT[p % 2][:, :, :].rearrange("p c w -> p (c w)"), turn_bank[0][:, :], ACT.Copy).then_inc(qTd, 1)

                def projected(t, p):
                    if past(t, 2):
                        act.wait_ge(rbm, t - 1)
                        act.wait_ge(ram, t - 1)
                    for j, bank, ready, done in ((0, 0, projq, qev), (1, 1, projk, kev)):
                        act.wait_ge(ready, t + 1)
                        act.activation(qk[p % 2][:, j].rearrange("p h d -> p (h d)"), proj_bank[bank][:, :], ACT.Copy).then_inc(done, 1)
                    act.wait_ge(kev, t + 1)
                    if past(t, 1):
                        act.wait_ge(rnh, t)
                    act.activation(sq[:, :, :, :], qk[p % 2][:, :, :, :], ACT.Square).then_inc(sqd, 1)

                def projected_v(t, p):
                    act.wait_ge(projv, t + 1)
                    if past(t, 4):
                        act.wait_ge(pv, t - 2)
                    act.activation(v[p][:, :], proj_bank[1][:, :], ACT.Copy).then_inc(vev, 1)

                act.wait_ge(zeroed, 1)
                run(act, NW, [(4, turned_p), (5, turned_o), (3, exponentials), (1, projected_v), (2, turned_q), (0, projected)], 4)

            @block.vector
            def _(dve):
                dve.wait_ge(consts, 16 * 7)
                dve.tensor_copy(masks[:, :, :], masks32[:, :, :])
                dve.tensor_copy(identb[:, :], G.ident[:, :])
                dve.memset(half[:, :, :], -0.5)
                dve.memset(kT[:, :, :, :], 0.0)
                dve.memset(v[3][:, :], 0.0)
                dve.memset(Y[:, :, 0:1], 0.0).then_inc(zeroed, 1)

                def turned_p(t, p):
                    if past(t, 1):
                        dve.wait_ge(pv, t)
                    for i in (1, 3):
                        dve.wait_ge(pt, 4 * t + i + 1)
                        dve.tensor_copy(pT[:, 2 * i:2 * i + 2].rearrange("p h s w -> p (h s w)"), turn_bank[1][:, :]).then_inc(ptV, 1)

                def maxima(t, p):
                    for i, heads in enumerate(QUAD):
                        dve.wait_ge(sc, 4 * t + i + 1)
                        dve.tensor_reduce(nmax[p % 2][:, heads[0]:heads[1] + 1:2], score_bank[i % 3][:, :].rearrange("p (h k) -> p h k", h=2),
                                          AX.X, ALU.max, negate=True).then_inc(mx, 1)

                def inverse(t, p):
                    dve.wait_ge(ex, 4 * t + 4)
                    if past(t, 2):
                        dve.wait_ge(od, t - 1)
                    dve.reciprocal(rinv[p % 2][:, :], rsum[p % 2][:, :]).then_inc(rid, 1)

                def normalise(t, p):
                    dve.wait_ge(pv, t + 1)
                    dve.wait_ge(rid, t + 1)
                    if past(t, 2):
                        dve.wait_ge(otr, t - 1)
                    dve.tensor_tensor(o[p % 2][:, :].rearrange("p (h d) -> p h d", h=HEADS), value_bank[:, :].rearrange("p (h d) -> p h d", h=HEADS),
                                      rinv[p % 2][:, :].unsqueeze(2).to_broadcast([P, HEADS, DH]), ALU.mult).then_inc(od, 1)

                def residual(t, p):
                    dve.wait_ge(wod, t + 1)
                    dve.tensor_tensor(Y[:, :, tok(t, 1, W)], turn_bank[1][:, 0:KD * W].rearrange("p (k w) -> p k w", k=KD),
                                      X[:, :, tok(t, 1, W)], ALU.add).then_inc(res, 1)

                def turned_k(t, p):
                    dve.wait_ge(trk, t + 1)
                    if past(t, 1):
                        dve.wait_ge(sc, 4 * t)
                    dve.tensor_copy(kT[:, :, p % 2], turn_bank[1][:, :].rearrange("p (c w) -> p c w", w=W)).then_inc(kTd, 1)

                def squares(t, p):
                    dve.wait_ge(sqd, t + 1)
                    if past(t, 2):
                        dve.wait_ge(rnd, t - 1)
                    dve.tensor_reduce(ss[p % 2][:, :, :], sq[:, :, :, :], AX.X, ALU.add).then_inc(rnh, 1)

                def clip(t, p):
                    dve.wait_ge(rnh, t + 1)
                    dve.tensor_scalar(ss[p % 2][:, :, :], ss[p % 2][:, :, :], 1e-24, None, ALU.max).then_inc(ssd, 1)

                def rotate(t, p):
                    q = qk[p % 2]
                    tab = rots[p % 2]
                    dve.wait_ge(kev, t + 1)
                    dve.wait_ge(rotsc, t + 1)
                    if past(t, 1):
                        dve.wait_ge(qkrd, t)
                    for j in range(2):
                        cos = tab[:, 2 * j].unsqueeze(1).to_broadcast([P, HEADS, DH])
                        i = dve.tensor_tensor(ra[:, j], q[:, j], cos, ALU.mult)
                    i.then_inc(ram, 1)
                    H2 = DH // 2
                    for j in range(2):
                        for a in (0, H2):
                            b = H2 - a
                            sin = tab[:, 2 * j + 1, a:a + H2].unsqueeze(1).to_broadcast([P, HEADS, H2])
                            i = dve.tensor_tensor(rb[:, j, :, a:a + H2], q[:, j, :, b:b + H2], sin, ALU.mult)
                    i.then_inc(rbm, 1)

                def scale(t, p):
                    dve.wait_ge(rsumd, t + 1)
                    dve.wait_ge(rnd, t + 1)
                    if past(t, 2):
                        dve.wait_ge(trk, t - 1)
                    dve.tensor_tensor(qkr[p % 2][:, :, :].rearrange("p j (h d) -> p (j h) d", h=HEADS), ra[:, :, :, :].rearrange("p j h d -> p (j h) d"),
                                      rn[p % 2][:, :, :].rearrange("p j h -> p (j h)").unsqueeze(2).to_broadcast([P, 2 * HEADS, DH]), ALU.mult).then_inc(qkrd, 1)

                run(dve, NW, [(4, turned_p), (3, maxima), (1, squares), (1, rotate), (5, residual), (3, inverse), (4, normalise), (2, turned_k), (1, clip), (1, scale)], 4)
        close()


def gated_mlp_pass(nc, G, l, S, X, finish=None):
    with ExitStack() as ctx:
        sb, sem, close = open_pass(nc, G, ctx)
        w1 = sb("mlp_w1", [P, KD, 2 * HID])
        w2 = sb("mlp_w2", [P, HK, D])
        gel = sb("mlp_gel", [P, 2, TT])
        hid = sb("mlp_hid", [P, 2, HK, TT])
        xin = sb("mlp_x", [P, 2, KD, TT])
        weights, ad, gd, geld, hidd, w2d, res, xl0, xl1, stored, link_s = (
            sem("m_" + n) for n in ("weights", "ad", "gd", "geld", "hidd", "w2d", "res", "xl0", "xl1", "stored", "l"))
        xl = (xl0, xl1)
        up_bank, out_bank = G.bank[0:6], G.bank[6:8]
        b1a, b1g, b2 = G.col(f"f_b1a{l}"), G.col(f"f_b1g{l}"), G.col(f"f_b2{l}")
        size = [P] * (HK - 1) + [HLAST]
        if finish:
            xs, xd = (G.io[n].rearrange("(k p) n -> p k n", p=P) for n in finish[0:2])
        with nc.Block() as block:
            @block.sync
            def _(sp):
                sp.dma_start(w1[:, :, :], G.io["w1"][l].rearrange("(k p) n -> p k n", p=P)).then_inc(weights, 16)
                sp.dma_start(w2[:, 0:HK - 1], G.io["w2"][l, 0:(HK - 1) * P].rearrange("(k p) n -> p k n", p=P)).then_inc(weights, 16)
                sp.dma_start(w2[0:HLAST, HK - 1], G.io["w2"][l, (HK - 1) * P:HID]).then_inc(weights, 16)
                if finish:
                    for t in range(NT + 2):
                        if t >= 2:
                            sp.wait_ge(res, t - 1)
                            sp.dma_start(xd[:, :, tok(t - 2)], xin[:, t % 2]).then_inc(stored, 16)
                            sp.wait_ge(stored, 16 * (t - 1))
                        if t < NT:
                            sp.dma_start(xin[:, t % 2], xs[:, :, tok(t)]).then_inc(xl[t % 2], 16)

            @block.tensor
            def _(pe):
                def up(t, p):
                    if t == 0:
                        pe.wait_ge(weights, 48)
                    for m in range(HK):
                        n = t * HK + m
                        M = size[m]
                        if past(n, 3):
                            pe.wait_ge(hidd, n - 2)
                        for j, done in ((1, gd), (0, ad)):
                            for k in range(KD):
                                mm = pe.matmul(up_bank[2 * (m % 3) + j][0:M, :], w1[:, k, j * HID + m * P:j * HID + m * P + M], S(k, t),
                                               start=(k == 0), stop=(k == KD - 1))
                            mm.then_inc(done, 1)

                def down(t, p):
                    pe.wait_ge(hidd, (t + 1) * HK)
                    if past(t, 1):
                        pe.wait_ge(res, t)
                    for m in range(KD):
                        for k in range(HK):
                            mm = pe.matmul(out_bank[m][:, :], w2[0:size[k], k, m * P:(m + 1) * P], hid[0:size[k], p, k], start=(k == 0), stop=(k == HK - 1))
                    mm.then_inc(w2d, 1)
                run(pe, NT, [(0, up), (1, down)])

            @block.scalar
            def _(act):
                def gelu(t, p):
                    for m in range(HK):
                        n, M = t * HK + m, size[m]
                        act.wait_ge(gd, n + 1)
                        if past(n, 2):
                            act.wait_ge(hidd, n - 1)
                        act.activation(gel[0:M, m % 2], up_bank[2 * (m % 3) + 1][0:M, :], ACT.Gelu, bias=b1g[0:M, m:m + 1]).then_inc(geld, 1)
                run(act, NT, [(0, gelu)])

            @block.vector
            def _(dve):
                link = chain(dve, link_s)

                def gate(t, p):
                    if past(t, 2):
                        dve.wait_ge(w2d, t - 1)
                    for m in range(HK):
                        n, M = t * HK + m, size[m]
                        dve.wait_ge(ad, n + 1)
                        dve.wait_ge(geld, n + 1)
                        dve.scalar_tensor_tensor(hid[0:M, p, m], up_bank[2 * (m % 3)][0:M, :], b1a[0:M, m:m + 1], gel[0:M, m % 2], ALU.add, ALU.mult).then_inc(hidd, 1)

                def residual(t, p):
                    dve.wait_ge(w2d, t + 1)
                    for h in range(KD):
                        i = dve.scalar_tensor_tensor(X(h, t), out_bank[h][:, :], b2[:, h:h + 1], X(h, t), ALU.add, ALU.add)
                        if finish:
                            link(i)
                    if finish:
                        dve.wait_ge(xl[p], 16 * (t // 2 + 1))
                        for h in range(KD):
                            i = dve.scalar_tensor_tensor(xin[:, p, h], X(h, t), finish[2][:, h:h + 1], xin[:, p, h], ALU.mult, ALU.add)
                    i.then_inc(res, 1)
                run(dve, NT, [(0, gate), (1, residual)])
        close()


def local_attention_stage(nc, G, src, dst):
    def plain(Z):
        return lambda k, t: Z[:, k, tok(t, 1)]

    def shifted(Z):
        return lambda k, t: Z[:, k, tok(t, 1 - k)]

    with ExitStack() as ctx:
        A, B = (ctx.enter_context(nc.sbuf_tensor(f"la_{n}", [P, KD, 1 + N], F32)) for n in "ab")
        zero_column(nc, G, "", [A])
        ln_pass(nc, G, "", plain(A), plain(A), G.eps5[:, :], G.mod[:, 0, CB:CB + KD], G.mod[:, 0, SB:SB + KD],
                load=load_x(G, src, A[:, :, 1:1 + N]))
        for l in range(DEPTH):
            attention_pass(nc, G, l, A, B)
            ln_pass(nc, G, "", shifted(B), plain(A), G.eps5[:, :], G.col(f"f_ln_g{l}"), G.col(f"f_ln_b{l}"))
            gated_mlp_pass(nc, G, l, plain(A), plain(B), (src, dst, G.mod[:, 0, GB:GB + KD]) if l == DEPTH - 1 else None)
            A, B = B, A


def s4d_params_pass(nc, G, prm):
    K = NL * HQ
    with ExitStack() as ctx:
        sb, sem, close = open_pass(nc, G, ctx)
        dt, ar, ai, cr, ci = (sb(n, [P, K]) for n in ("dt", "ar", "ai", "cr", "ci"))
        e1, s, c, a, b, q, r, den = (sb(n, [P, K]) for n in ("e1", "s", "c", "a", "b", "q", "r", "den"))
        zeros = sb("zeros", [Q4, HQ, C])
        loaded, cleared, stored, dv, ac = sem("p_loaded"), sem("p_cleared"), sem("p_stored"), sem("p_dv"), sem("p_ac")
        turns, rate, cre, cim, ncre = (x[:, :] for x in prm)
        with nc.Block() as block:
            @block.sync
            def _(sp):
                for n, t in (("s_log_dt", dt), ("s_A_re_log", ar), ("s_A_im", ai), ("s_C_re", cr), ("s_C_im", ci)):
                    sp.dma_start(t[:, :], G.io[n].rearrange("p l q -> p (l q)")).then_inc(loaded, 16)
                sp.wait_ge(cleared, 1)
                sp.dma_start(G.io["taps"][:, :, 0:C].rearrange("q a j -> a q j"), zeros[:, :, :]).then_inc(stored, 16)
                sp.wait_ge(stored, 16)

            @block.scalar
            def _(act):
                act.wait_ge(loaded, 80)
                act.activation(dt[:, :], dt[:, :], ACT.Exp).then_inc(ac, 1)
                act.activation(ar[:, :], ar[:, :], ACT.Exp).then_inc(ac, 1)
                act.wait_ge(dv, 4)
                act.activation(e1[:, :], rate, ACT.Tanh, scale=0.5).then_inc(ac, 1)
                act.wait_ge(dv, 8)
                act.activation(s[:, :], turns, ACT.Sin, scale=PI).then_inc(ac, 1)
                act.activation(c[:, :], a[:, :], ACT.Sin, scale=-PI, bias=G.half_pi[:, :]).then_inc(ac, 1)

            @block.vector
            def _(dve):
                link = chain(dve, dv)
                dve.wait_ge(ac, 2)
                link(dve.tensor_scalar(ar[:, :], ar[:, :], -1.0, None, ALU.mult))
                link(dve.tensor_tensor(rate, ar[:, :], dt[:, :], ALU.mult))
                link(dve.tensor_tensor(b[:, :], ai[:, :], dt[:, :], ALU.mult))
                link(dve.tensor_scalar(b[:, :], b[:, :], 1.0 / 6.283185307179586, None, ALU.mult))
                link(dve.tensor_scalar(q[:, :], b[:, :], MAGIC, None, ALU.add))
                link(dve.tensor_scalar(q[:, :], q[:, :], MAGIC, None, ALU.subtract))
                link(dve.tensor_tensor(turns, b[:, :], q[:, :], ALU.subtract))
                link(dve.scalar_tensor_tensor(a[:, :], turns, -1.0, turns, ALU.mult, ALU.max))
                dve.wait_ge(ac, 3)
                link(dve.tensor_scalar(q[:, :], e1[:, :], -1.0, 1.0, ALU.mult, ALU.add))
                link(dve.reciprocal(q[:, :], q[:, :]))
                link(dve.scalar_tensor_tensor(e1[:, :], e1[:, :], 2.0, q[:, :], ALU.mult, ALU.mult))
                dve.wait_ge(ac, 5)
                link(dve.scalar_tensor_tensor(a[:, :], s[:, :], 2.0, s[:, :], ALU.mult, ALU.mult))
                link(dve.scalar_tensor_tensor(b[:, :], s[:, :], 2.0, c[:, :], ALU.mult, ALU.mult))
                link(dve.tensor_tensor(q[:, :], e1[:, :], a[:, :], ALU.mult))
                link(dve.tensor_tensor(q[:, :], e1[:, :], q[:, :], ALU.subtract))
                link(dve.tensor_tensor(q[:, :], q[:, :], a[:, :], ALU.subtract))
                link(dve.scalar_tensor_tensor(r[:, :], e1[:, :], 1.0, b[:, :], ALU.add, ALU.mult))
                link(dve.tensor_tensor(a[:, :], ar[:, :], ar[:, :], ALU.mult))
                link(dve.tensor_tensor(b[:, :], ai[:, :], ai[:, :], ALU.mult))
                link(dve.tensor_tensor(den[:, :], a[:, :], b[:, :], ALU.add))
                link(dve.reciprocal(den[:, :], den[:, :]))
                link(dve.tensor_tensor(a[:, :], q[:, :], ar[:, :], ALU.mult))
                link(dve.tensor_tensor(b[:, :], r[:, :], ai[:, :], ALU.mult))
                link(dve.tensor_tensor(a[:, :], a[:, :], b[:, :], ALU.add))
                link(dve.tensor_tensor(b[:, :], r[:, :], ar[:, :], ALU.mult))
                link(dve.tensor_tensor(q[:, :], q[:, :], ai[:, :], ALU.mult))
                link(dve.tensor_tensor(b[:, :], b[:, :], q[:, :], ALU.subtract))
                link(dve.scalar_tensor_tensor(a[:, :], a[:, :], 2.0, den[:, :], ALU.mult, ALU.mult))
                link(dve.scalar_tensor_tensor(b[:, :], b[:, :], 2.0, den[:, :], ALU.mult, ALU.mult))
                link(dve.tensor_tensor(q[:, :], cr[:, :], a[:, :], ALU.mult))
                link(dve.tensor_tensor(r[:, :], ci[:, :], b[:, :], ALU.mult))
                link(dve.tensor_tensor(cre, q[:, :], r[:, :], ALU.subtract))
                link(dve.tensor_tensor(q[:, :], cr[:, :], b[:, :], ALU.mult))
                link(dve.tensor_tensor(r[:, :], ci[:, :], a[:, :], ALU.mult))
                link(dve.tensor_tensor(cim, q[:, :], r[:, :], ALU.add))
                link(dve.tensor_scalar(ncre, cre, -1.0, None, ALU.mult))

            @block.gpsimd
            def _(pool):
                pool.memset(zeros[:, :, :], 0.0).then_inc(cleared, 1)
        close()


def to_chunks_pass(nc, G, Z, Zr):
    with ExitStack() as ctx:
        sb, sem, close = open_pass(nc, G, ctx)
        turned, evA, evV = sem("turned"), sem("evA"), sem("evV")
        with nc.Block() as block:
            @block.tensor
            def _(pe):
                for n in range(NC // 2):
                    if n >= 4:
                        pe.wait_ge((evA, evV)[n % 2], (n - 4) // 2 + 1)
                    for a in range(2):
                        for h in range(KD):
                            t0 = (2 * n + a) * C
                            mm = pe.transpose(G.bank[n % 4][:, (KD * a + h) * P:(KD * a + h + 1) * P], Z[:, h, t0:t0 + C], G.ident[:, :])
                    mm.then_inc(turned, 1)

            def evacuate(eng, copy, first, done):
                for n in range(first, NC // 2, 2):
                    eng.wait_ge(turned, n + 1)
                    copy(Zr[:, :, 2 * n:2 * n + 2], G.bank[n % 4][:, :].rearrange("p (c h) -> p h c", c=2)).then_inc(done, 1)

            @block.scalar
            def _(act):
                evacuate(act, lambda o, i: act.activation(o, i, ACT.Copy), 0, evA)

            @block.vector
            def _(dve):
                evacuate(dve, dve.tensor_copy, 1, evV)
        close()


def convolution_pass(nc, G, l, prm, Zr, Yt):
    TW = C + 1 + NC
    S = GQ * NC
    with ExitStack() as ctx:
        sb, sem, close = open_pass(nc, G, ctx)
        ramp, quads = sb("ramp", [P, C + 1]), sb("quads", [P, Q4])
        skip = sb("skip", [Q4, HQ])
        ph, rd = sb("ph", [P, GQ, TW]), sb("rd", [P, GQ, TW])
        g128 = sb("g128", [P, HQ])
        g128r = sb("g128r", [P, HQ])
        r128 = sb("r128", [P, HQ])
        ex, sn, cs = ([sb(f"{n}{i}", [P, GQ, TW]) for i in range(3)] for n in ("ex", "sn", "cs"))
        er = sb("er", [P, 2, GQ, C + 1])
        tv = sb("tv", [P, 2, GQ, C])
        tp = sb("tp", [P, 2, GQ, C])
        gm = [sb(f"gm{i}", [P, 2, GQ, C]) for i in range(3)]
        bt = [sb(f"bt{i}", [P, 2, GQ, P]) for i in range(2)]
        krow = [sb(f"krow{i}", [Q4, GQ, C]) for i in range(2)]
        toep = [sb(f"toep{i}", [P, GC, C]) for i in range(2)]
        w = sb("w", [P, 4, GQ, NC])
        uh = sb("uh", [P, 2, GQ, NC])
        sh = sb("sh", [P, 2, GQ, NC])
        sw = sb("sw", [P, 4, GQ, NC])
        st = [sb(f"st{i}", [P, 2, GQ, Q4, NC]) for i in range(2)]
        names = ("consts", "phd", "exh", "trig", "erd", "gmV", "gmP", "taps", "kr", "ks0", "ks1", "tl0", "tl1", "btr", "btA", "btV",
                 "ud", "uread", "scand", "stV", "stP", "yd", "gel", "lv", "lp", "decd")
        (consts, phd, exh, trig, erd, gmV, gmP, taps, kr, ks0, ks1, tl0, tl1, btr, btA, btV,
         ud, uread, scand, stV, stP, yd, gel, lv, lp, decd) = (sem("c_" + n) for n in names)
        ks, tl = (ks0, ks1), (tl0, tl1)
        turns, rate, cre, cim, ncre = (x[:, l * HQ:(l + 1) * HQ] for x in prm)
        taps_bank, b_bank, u_bank, y_bank = G.bank[0], G.bank[1:3], G.bank[3:5], G.bank[5:7]
        tap_rows = G.io["taps"]
        qs = lambda g: slice(g * GQ, (g + 1) * GQ)
        bc = lambda v, g, n: v[:, qs(g)].unsqueeze(2).to_broadcast([P, GQ, n])
        rc = lambda v, n: v.unsqueeze(1).to_broadcast([P, GQ, n])
        with nc.Block() as block:
            @block.sync
            def _(sp):
                sp.dma_start(ramp[:, :], G.io["ramp"]).then_inc(consts, 16)
                sp.dma_start(quads[:, :], G.io["quads"]).then_inc(consts, 16)
                sp.dma_start(skip[:, :], G.io["s_D"][:, l, :]).then_inc(consts, 16)

                def store(g, p):
                    sp.wait_ge(kr, g + 1)
                    sp.dma_start(tap_rows[qs(g), :, C:2 * C].rearrange("q a j -> a q j"), krow[g % 2][:, :, :]).then_inc(ks[g % 2], 16)

                def load(g, p):
                    sp.wait_ge(ks[g % 2], 16 * (g // 2 + 1))
                    if past(g, 2):
                        sp.wait_ge(yd, g - 1)
                    at = tap_rows[g * GQ:g * GQ + 1, 0:1, 1:2]
                    src = bass.AP(tensor=at.tensor, offset=at.offset, ap=[[1, P], [2 * C, GC], [1, C]])
                    sp.dma_start(toep[g % 2][:, :, :], src).then_inc(tl[g % 2], 16)
                run(sp, NG, [(0, store), (0, load)], 2)

            @block.gpsimd
            def _(pool):
                link = chain(pool, lp)
                pool.wait_ge(consts, 48)
                pool.wait_ge(decd, 1)

                def exponents(g, p):
                    r = g % 3
                    if past(g, 3):
                        pool.wait_ge(stV, g - 2)
                        pool.wait_ge(stP, g - 2)
                    pool.tensor_tensor(ex[r][:, :, 0:C + 1], bc(rate, g, C + 1), rc(ramp[:, :], C + 1), ALU.mult)
                    pool.tensor_copy(ex[r][:, :, C + 1:TW], bc(r128, g, NC)).then_inc(exh, 1)

                def imaginary(g, p):
                    if past(g, 3):
                        pool.wait_ge(yd, g - 2)
                    pool.wait_ge(erd, g + 1)
                    pool.tensor_tensor(tp[:, 0], er[:, 1, :, 0:C], bc(ncre, g, C), ALU.mult)
                    link(pool.tensor_tensor(tp[:, 1], er[:, 0, :, 0:C], bc(cim, g, C), ALU.mult))
                    pool.tensor_tensor(gm[g % 3][:, 1], tp[:, 0], tp[:, 1], ALU.subtract).then_inc(gmP, 1)

                def state_im(g, p):
                    pool.wait_ge(scand, g + 1)
                    if past(g, 2):
                        pool.wait_ge(yd, g - 1)
                    R = slice(C + 1, TW)
                    pool.tensor_tensor(sw[:, 2], cs[g % 3][:, :, R], sh[:, 1], ALU.mult)
                    link(pool.tensor_tensor(sw[:, 3], sn[g % 3][:, :, R], sh[:, 0], ALU.mult))
                    link(pool.tensor_tensor(sw[:, 2], sw[:, 2], sw[:, 3], ALU.add))
                    pool.tensor_tensor(st[g % 2][:, 1], sw[:, 2].unsqueeze(2).to_broadcast([P, GQ, Q4, NC]),
                                       quads[:, :].unsqueeze(1).unsqueeze(3).to_broadcast([P, GQ, Q4, NC]), ALU.mult).then_inc(stP, 1)

                run(pool, NG, [(0, exponents), (1, imaginary), (2, state_im)], 2)

            @block.scalar
            def _(act):
                def trigonometry(g, p):
                    r = g % 3
                    act.wait_ge(phd, g + 1)
                    act.activation(sn[r][:, :, :], sn[r][:, :, :], ACT.Sin, scale=TWO_PI)
                    act.activation(cs[r][:, :, :], cs[r][:, :, :], ACT.Sin, scale=-TWO_PI, bias=G.half_pi[:, :])
                    act.wait_ge(exh, g + 1)
                    act.activation(ex[r][:, :, :], ex[r][:, :, :], ACT.Exp).then_inc(trig, 1)

                def inputs(g, p):
                    act.wait_ge(btr, 2 * g + 1)
                    if past(g, 2):
                        act.wait_ge(ud, g - 1)
                    act.activation(bt[g % 2][:, 0].rearrange("p q m -> p (q m)"), b_bank[0][:, :], ACT.Copy).then_inc(btA, 1)

                def gelu(g, p):
                    act.wait_ge(yd, g + 1)
                    act.activation(Yt[:, :, g * GC:(g + 1) * GC], y_bank[g % 2][:, :].rearrange("p (h c) -> p c h", h=GC), ACT.Gelu_apprx_tanh).then_inc(gel, 1)

                run(act, NG, [(0, trigonometry), (3, gelu), (1, inputs)], 2)

            @block.vector
            def _(dve):
                link = chain(dve, lv)
                dve.wait_ge(consts, 48)
                link(dve.tensor_scalar(g128[:, :], turns, float(C), None, ALU.mult))
                link(dve.tensor_scalar(g128r[:, :], g128[:, :], MAGIC, None, ALU.add))
                link(dve.tensor_scalar(g128r[:, :], g128r[:, :], MAGIC, None, ALU.subtract))
                link(dve.tensor_tensor(g128[:, :], g128[:, :], g128r[:, :], ALU.subtract))
                for x in st:
                    dve.memset(x[:, :, :, :, :], 0.0)
                link(dve.memset(uh[:, :, :, 0:1], 0.0))
                dve.tensor_scalar(r128[:, :], rate, float(C), None, ALU.mult).then_inc(decd, 1)

                def phases(g, p):
                    r = g % 3
                    dve.tensor_tensor(ph[:, :, 0:C + 1], bc(turns, g, C + 1), rc(ramp[:, :], C + 1), ALU.mult)
                    link(dve.tensor_tensor(ph[:, :, C + 1:TW], bc(g128, g, NC), rc(ramp[:, 0:NC], NC), ALU.mult))
                    link(dve.tensor_scalar(rd[:, :, :], ph[:, :, :], MAGIC, None, ALU.add))
                    link(dve.tensor_scalar(rd[:, :, :], rd[:, :, :], MAGIC, None, ALU.subtract))
                    if past(g, 3):
                        dve.wait_ge(stP, g - 2)
                    link(dve.tensor_tensor(sn[r][:, :, :], ph[:, :, :], rd[:, :, :], ALU.subtract))
                    dve.scalar_tensor_tensor(cs[r][:, :, :], sn[r][:, :, :], -1.0, sn[r][:, :, :], ALU.mult, ALU.max).then_inc(phd, 1)

                def bases(g, p):
                    r = g % 3
                    dve.wait_ge(trig, g + 1)
                    if past(g, 1):
                        dve.wait_ge(gmP, g)
                        dve.wait_ge(btr, 2 * g)
                    link(dve.memset(ex[r][:, :, C + 1:C + 2], 0.0))
                    dve.tensor_tensor(er[:, 0], ex[r][:, :, 0:C + 1], cs[r][:, :, 0:C + 1], ALU.mult)
                    dve.tensor_tensor(er[:, 1], ex[r][:, :, 0:C + 1], sn[r][:, :, 0:C + 1], ALU.mult).then_inc(erd, 1)
                    dve.wait_ge(erd, g + 1)
                    if past(g, 3):
                        dve.wait_ge(yd, g - 2)
                    dve.tensor_tensor(tv[:, 0], er[:, 0, :, 0:C], bc(cre, g, C), ALU.mult)
                    link(dve.tensor_tensor(tv[:, 1], er[:, 1, :, 0:C], bc(cim, g, C), ALU.mult))
                    dve.tensor_tensor(gm[g % 3][:, 0], tv[:, 0], tv[:, 1], ALU.subtract).then_inc(gmV, 1)

                def tap_row(g, p):
                    dve.wait_ge(taps, g + 1)
                    if past(g, 2):
                        dve.wait_ge(ks[g % 2], 16 * (g // 2))
                    link(dve.tensor_copy(krow[g % 2][:, :, :].rearrange("p q j -> p (q j)"), taps_bank[0:Q4, :]))
                    dve.tensor_tensor(krow[g % 2][:, :, 0], krow[g % 2][:, :, 0], skip[:, qs(g)], ALU.add).then_inc(kr, 1)
                    dve.wait_ge(btr, 2 * g + 2)
                    if past(g, 2):
                        dve.wait_ge(ud, g - 1)
                    dve.tensor_copy(bt[g % 2][:, 1].rearrange("p q m -> p (q m)"), b_bank[1][:, :]).then_inc(btV, 1)

                def scan(g, p):
                    r = g % 3
                    dve.wait_ge(ud, g + 1)
                    u = u_bank[g % 2][:, 0:2 * S].rearrange("p (r q c) -> p r q c", r=2, q=GQ)
                    R1, R = slice(C + 2, TW), slice(C + 1, TW)
                    for j, (tab, part) in enumerate(((cs, 0), (sn, 1), (cs, 1), (sn, 0))):
                        i = dve.tensor_tensor(w[:, j, :, 1:NC], tab[r][:, :, R1], u[:, part, :, 0:NC - 1], ALU.mult)
                    i.then_inc(uread, 1)
                    dve.wait_ge(uread, g + 1)
                    dve.tensor_tensor(uh[:, 0, :, 1:NC], w[:, 0, :, 1:NC], w[:, 1, :, 1:NC], ALU.add)
                    link(dve.tensor_tensor(uh[:, 1, :, 1:NC], w[:, 2, :, 1:NC], w[:, 3, :, 1:NC], ALU.subtract))
                    if past(g, 1):
                        dve.wait_ge(stP, g)
                    link(dve.tensor_copy(w[:, 0], ex[r][:, :, R]))
                    for part in range(2):
                        i = dve.tensor_tensor_scan(sh[:, part].rearrange("p q c -> p (q c)"), w[:, 0].rearrange("p q c -> p (q c)"),
                                                   uh[:, part].rearrange("p q c -> p (q c)"), 0.0, ALU.mult, ALU.add)
                    i.then_inc(scand, 1)
                    dve.wait_ge(scand, g + 1)
                    if past(g, 2):
                        dve.wait_ge(yd, g - 1)
                    dve.tensor_tensor(sw[:, 0], cs[r][:, :, R], sh[:, 0], ALU.mult)
                    link(dve.tensor_tensor(sw[:, 1], sn[r][:, :, R], sh[:, 1], ALU.mult))
                    for a in range(Q4):
                        R = slice(SN * a, SN * (a + 1))
                        i = dve.tensor_tensor(st[g % 2][R, 0, :, a], sw[R, 0], sw[R, 1], ALU.subtract)
                    i.then_inc(stV, 1)

                run(dve, NG, [(0, phases), (1, bases), (2, scan), (1, tap_row)], 2)

            @block.tensor
            def _(pe):
                pe.wait_ge(consts, 48)

                def tables(g, p):
                    pe.wait_ge(gmV, g + 1)
                    if past(g, 1):
                        pe.wait_ge(kr, g)
                    pe.matmul(taps_bank[0:Q4, :], quads[:, :], gm[g % 3][:, 0].rearrange("p q j -> p (q j)"), start=True, stop=True).then_inc(taps, 1)
                    for part, ev in ((0, btA), (1, btV)):
                        if past(g, 1):
                            pe.wait_ge(ev, g)
                        for q in range(GQ):
                            mm = pe.transpose(b_bank[part][:, q * P:(q + 1) * P], er[:, part, q, 1:C + 1], G.ident[:, :])
                        mm.then_inc(btr, 1)

                def inputs(g, p):
                    pe.wait_ge(btA, g + 1)
                    pe.wait_ge(btV, g + 1)
                    if past(g, 2):
                        pe.wait_ge(uread, g - 1)
                    for q in range(GQ):
                        for a in range(Q4):
                            for part in range(2):
                                mm = pe.matmul(u_bank[g % 2][SN * a:SN * (a + 1), (part * GQ + q) * NC:(part * GQ + q + 1) * NC],
                                               bt[g % 2][:, part, q, SN * a:SN * (a + 1)], Zr[:, (g * GQ + q) * Q4 + a], start=True, stop=True)
                    mm.then_inc(ud, 1)

                def outputs(g, p):
                    pe.wait_ge(tl[g % 2], 16 * (g // 2 + 1))
                    pe.wait_ge(gmP, g + 1)
                    pe.wait_ge(stV, g + 1)
                    pe.wait_ge(stP, g + 1)
                    if past(g, 2):
                        pe.wait_ge(gel, g - 1)
                    for q in range(GQ):
                        four = y_bank[g % 2][:, q * Q4 * NC:(q + 1) * Q4 * NC]
                        for part in range(2):
                            pe.matmul(four, gm[g % 3][:, part, q], st[g % 2][:, part, q].rearrange("p a c -> p (a c)"),
                                      start=(part == 0), stop=False)
                        for a in range(Q4):
                            mm = pe.matmul(y_bank[g % 2][:, (q * Q4 + a) * NC:(q * Q4 + a + 1) * NC], toep[g % 2][:, q * Q4 + a],
                                           Zr[:, (g * GQ + q) * Q4 + a], start=False, stop=(a == Q4 - 1))
                    mm.then_inc(yd, 1)

                run(pe, NG, [(2, inputs), (3, outputs), (1, tables)], 2)
        close()


def s4d_out_pass(nc, G, l, Yt, H, finish=None):
    CT = TT // C
    with ExitStack() as ctx:
        sb, sem, close = open_pass(nc, G, ctx)
        wt = sb("so_w", [P, KD, 2 * D])
        y = sb("so_y", [P, 2, KD, TT])
        th = sb("so_th", [P, 2, KD, TT])
        hb = sb("so_hb", [P, KD])
        xin = sb("so_x", [P, 2, KD, TT])
        weights, tr, yA, yV, od, thd, res, o1r, hbd, xl0, xl1, stored, link_s = (
            sem("so_" + n) for n in ("weights", "tr", "yA", "yV", "od", "thd", "res", "o1r", "hbd", "xl0", "xl1", "stored", "l"))
        xl = (xl0, xl1)
        tr_bank, o_bank = G.bank[0:4], G.bank[4:8]
        b = G.col(f"s_b{l}")
        if finish:
            xs, xd = (G.io[n].rearrange("(k p) n -> p k n", p=P) for n in finish[0:2])
        with nc.Block() as block:
            @block.sync
            def _(sp):
                sp.dma_start(wt[:, :, :], G.io["s_W"][l].rearrange("(k p) n -> p k n", p=P)).then_inc(weights, 16)
                if finish:
                    for t in range(NT + 2):
                        if t >= 2:
                            sp.wait_ge(res, t - 1)
                            sp.dma_start(xd[:, :, tok(t - 2)], xin[:, t % 2]).then_inc(stored, 16)
                            sp.wait_ge(stored, 16 * (t - 1))
                        if t < NT:
                            sp.dma_start(xin[:, t % 2], xs[:, :, tok(t)]).then_inc(xl[t % 2], 16)

            @block.tensor
            def _(pe):
                def turn(t, p):
                    for h, ev in ((0, yA), (1, yV)):
                        if past(t, 2):
                            pe.wait_ge(ev, t - 1)
                        for c in range(CT):
                            mm = pe.transpose(tr_bank[2 * p + h][:, c * C:(c + 1) * C], Yt[:, t * CT + c, h * P:(h + 1) * P], G.ident[:, :])
                        mm.then_inc(tr, 1)

                def project(t, p):
                    if t == 0:
                        pe.wait_ge(weights, 16)
                    pe.wait_ge(yA, t + 1)
                    pe.wait_ge(yV, t + 1)
                    for m in (2, 3, 0, 1):
                        if past(t, 1):
                            pe.wait_ge(thd if m >= 2 else o1r, t)
                        for k in range(KD):
                            mm = pe.matmul(o_bank[m][:, :], wt[:, k, m * P:(m + 1) * P], y[:, p, k], start=(k == 0), stop=(k == KD - 1))
                        if m in (3, 1):
                            mm.then_inc(od, 1)
                run(pe, NT, [(0, turn), (1, project)])

            @block.scalar
            def _(act):
                def evacuate(t, p):
                    act.wait_ge(tr, 2 * t + 1)
                    if past(t, 2):
                        act.wait_ge(od, 2 * (t - 1))
                    act.activation(y[:, p, 0], tr_bank[2 * p][:, :], ACT.Copy).then_inc(yA, 1)

                def sigmoid(t, p):
                    if t == 0:
                        act.wait_ge(hbd, 1)
                    act.wait_ge(od, 2 * t + 1)
                    if past(t, 2):
                        act.wait_ge(res, t - 1)
                    for h in range(KD):
                        i = act.activation(th[:, p, h], o_bank[2 + h][:, :], ACT.Tanh, scale=0.5, bias=hb[:, h:h + 1])
                    i.then_inc(thd, 1)
                run(act, NT, [(0, evacuate), (1, sigmoid)])

            @block.vector
            def _(dve):
                link = chain(dve, link_s)
                dve.tensor_scalar(hb[:, :], b[:, KD:2 * KD], 0.5, None, ALU.mult).then_inc(hbd, 1)

                def evacuate(t, p):
                    dve.wait_ge(tr, 2 * t + 2)
                    if past(t, 2):
                        dve.wait_ge(od, 2 * (t - 1))
                    dve.tensor_copy(y[:, p, 1], tr_bank[2 * p + 1][:, :]).then_inc(yV, 1)

                def residual(t, p):
                    dve.wait_ge(thd, t + 1)
                    link(dve.tensor_scalar(th[:, p], th[:, p], 1.0, 0.5, ALU.add, ALU.mult))
                    dve.wait_ge(od, 2 * t + 2)
                    for h in range(KD):
                        i = dve.scalar_tensor_tensor(th[:, p, h], o_bank[h][:, :], b[:, h:h + 1], th[:, p, h], ALU.add, ALU.mult)
                    i.then_inc(o1r, 1)
                    dve.wait_ge(o1r, t + 1)
                    i = dve.tensor_tensor(H[:, :, tok(t)], H[:, :, tok(t)], th[:, p], ALU.add)
                    if finish:
                        link(i)
                        dve.wait_ge(xl[p], 16 * (t // 2 + 1))
                        for h in range(KD):
                            i = dve.scalar_tensor_tensor(xin[:, p, h], H[:, h, tok(t)], finish[2][:, h:h + 1], xin[:, p, h], ALU.mult, ALU.add)
                    i.then_inc(res, 1)
                run(dve, NT, [(0, evacuate), (1, residual)])
        close()


def s4d_stage(nc, G, src, dst):
    with ExitStack() as ctx:
        sb = lambda n, s: ctx.enter_context(nc.sbuf_tensor(n, s, F32))
        prm = [sb("s_" + n, [P, NL * HQ]) for n in ("turns", "rate", "cre", "cim", "ncre")]
        H = sb("s_h", [P, KD, N])
        Z = sb("s_z", [P, KD, N])
        Zr = sb("s_zr", [P, D, NC])
        Yt = Z[:, :, :].rearrange("p k n -> p (k n)").rearrange("p (c h) -> p c h", h=D)
        Hv = lambda k, t: H[:, k, tok(t)]
        Zv = lambda k, t: Z[:, k, tok(t)].rearrange("p (c j) -> p c j", j=C)[:, :, ::-1]
        s4d_params_pass(nc, G, prm)
        ln_pass(nc, G, "", Hv, Hv, G.eps5[:, :], G.mod[:, 1, CA:CA + KD], G.mod[:, 1, SA:SA + KD], load=load_x(G, src, H))
        for l in range(NL):
            ln_pass(nc, G, "", Hv, Zv, G.eps5[:, :], G.col(f"s_ln_w{l}"), G.col(f"s_ln_b{l}"))
            to_chunks_pass(nc, G, Z, Zr)
            convolution_pass(nc, G, l, prm, Zr, Yt)
            s4d_out_pass(nc, G, l, Yt, H, (src, dst, G.mod[:, 1, GA:GA + KD]) if l == NL - 1 else None)


class FfnWeights:
    PER_STEP = 3
    RAW = 6

    def __init__(self, nc, G, ctx, sb, sem):
        self.G, MF = G, FF // P
        make = lambda n, k, w: ctx.enter_context(nc.sbuf_tensor("ff_" + n, [P, k, w], F32R))
        self.w = {"w1": make("w1", KD, FF), "w2": make("w2", KD, FF), "h1": make("h1", MF, FF), "h2": make("h2", MF, FF), "w3": make("w3", MF, D)}
        self.inexact = ctx.enter_context(nc.sbuf_tensor("ff_inexact", [P, 1], I32))
        self.chunks = [(n, k, 1) for n in ("w1", "w2", "h1", "h2") for k in range(self.w[n].shape[1])] + [("w3", k, FF // D) for k in range(0, MF, FF // D)]

    def open(self, sb, sem):
        self.raw = [sb(f"raw{i}", [P, FF]) for i in range(self.RAW)]
        self.rest = [sb(f"rest{i}", [P, FF]) for i in range(3)]
        self.lost = sb("lost", [P, len(self.chunks)])
        self.any_lost = sb("any_lost", [P, 1])
        self.raw_loaded = [sem(f"raw_loaded{i}") for i in range(self.RAW)]
        self.rounded, self.rest_ready, self.summed, self.any_ready, self.count_ready, self.known = (
            sem("f_" + n) for n in ("rounded", "rest_ready", "summed", "any_ready", "count_ready", "known"))

    def of_step(self, t):
        return [(c, self.chunks[c]) for c in range(t * self.PER_STEP, min((t + 1) * self.PER_STEP, len(self.chunks)))]

    def rows(self, chunk, b):
        name, k, n = chunk
        return b[:, k] if n == 1 else b[:, k:k + n].rearrange("p k n -> p (k n)")

    def load(self, sp, t):
        for c, (name, k, n) in self.of_step(t):
            if c >= self.RAW:
                sp.wait_ge(self.rest_ready, c - self.RAW + 1)
            src = self.G.io["g_" + name].rearrange("(k p) n -> p k n", p=P)[:, k:k + n]
            sp.dma_start(self.raw[c % self.RAW][:, :].rearrange("p (k n) -> p k n", k=n), src).then_inc(self.raw_loaded[c % self.RAW], 16)

    def round(self, act, t):
        for c, chunk in self.of_step(t):
            act.wait_ge(self.raw_loaded[c % self.RAW], 16 * (c // self.RAW + 1))
            act.activation(self.rows(chunk, self.w[chunk[0]]), self.raw[c % self.RAW][:, :], ACT.Copy).then_inc(self.rounded, 1)

    def subtract(self, pool, t):
        for c, chunk in self.of_step(t):
            pool.wait_ge(self.rounded, c + 1)
            if c >= 3:
                pool.wait_ge(self.summed, c - 2)
            pool.tensor_tensor(self.rest[c % 3][:, :], self.raw[c % self.RAW][:, :], self.rows(chunk, self.w[chunk[0]]), ALU.subtract).then_inc(self.rest_ready, 1)

    def sum_rests(self, act, t):
        for c, chunk in self.of_step(t):
            act.wait_ge(self.rest_ready, c + 1)
            act.activation(self.rest[c % 3][:, :], self.rest[c % 3][:, :], ACT.Abs, accum_out=self.lost[:, c:c + 1]).then_inc(self.summed, 1)

    def decide(self, dve):
        dve.wait_ge(self.summed, len(self.chunks))
        dve.tensor_reduce(self.any_lost[:, :], self.lost[:, :], AX.X, ALU.add).then_inc(self.any_ready, 1)
        dve.wait_ge(self.any_ready, 1)
        dve.tensor_scalar(self.any_lost[:, :], self.any_lost[:, :], 0.0, None, ALU.not_equal).then_inc(self.any_ready, 1)
        dve.wait_ge(self.count_ready, 1)
        dve.tensor_scalar(self.inexact[:, :], self.G.bank[4][:, 0:1], 0.0, None, ALU.not_equal).then_inc(self.known, 1)

    def count(self, pe):
        pe.wait_ge(self.any_ready, 2)
        pe.matmul(self.G.bank[4][:, 0:1], self.G.mean_w[:, :], self.any_lost[:, :], start=True, stop=True).then_inc(self.count_ready, 1)


def ffn_pass(nc, G, F, src, dst):
    MF = FF // P
    with ExitStack() as ctx:
        sb, sem, close = open_pass(nc, G, ctx)
        s32 = sb("s32", [P, KD, TT])
        S, U, V = ([sb(f"{n}_{part}", [P, k, TT], F32R) for part in ("hi", "lo")] for n, k in (("s", KD), ("u", MF), ("v", MF)))
        gated = sb("gated", [P, 2, TT])
        whole = sb("whole", [P, 2, TT])
        whole_u = sb("whole_u", [P, 2, TT])
        xin = sb("xin", [P, KD, TT])
        out_scale = sb("out_scale", [P, KD])
        block_buf = [sb(f"weight_block{i}", [P, MF, P]) for i in range(2)]
        w1d, w2d, silud, hid, lod, evac, h1d, h2d, w3d, res, xload, stored, scaled, sload, shi, slo, block_used = (
            sem("f_" + n) for n in ("w1d", "w2d", "silud", "hid", "lod", "evac", "h1d", "h2d", "w3d", "res", "xload", "stored",
                                    "scaled", "sload", "shi", "slo", "block_used"))
        block_loaded = [sem(f"block_loaded{i}") for i in range(2)]
        pair = (G.bank[0:2], G.bank[2:4])
        hidden_bank = G.bank[4:6]
        out_bank = G.bank[6:8]
        gate = G.mod[:, 1, GB:GB + KD]
        s1, s2, sh1, sh2, s3 = (G.col(n) for n in ("w1_s", "w2_s", "h1_s", "h2_s", "w3_s"))
        feat = lambda n: G.io[n].rearrange("(k p) n -> p k n", p=P)
        xs, xd, sd = feat(src), feat(dst), feat("s3")
        blocks = ([(n, m) for m in range(MF) for n in ("w1", "w2")] + [("h1", m) for m in range(MF)]
                  + [("h2", m) for m in range(MF)] + [("w3", m) for m in range(KD)])
        number = {b: i for i, b in enumerate(blocks)}
        parts = 3 * MF
        with nc.Block() as block:
            @block.sync
            def _(sp):
                def load_s(t):
                    if t >= 1:
                        sp.wait_ge(slo, t)
                    sp.dma_start(s32[:, :, :], sd[:, :, tok(t)]).then_inc(sload, 16)

                def tiles(general):
                    load_s(0)
                    for t in range(NT):
                        if t >= 1:
                            sp.wait_ge(stored, 16 * t)
                        sp.dma_start(xin[:, :, :], xs[:, :, tok(t)]).then_inc(xload, 16)
                        if t + 1 < NT:
                            load_s(t + 1)
                        if general:
                            for i, (name, m) in enumerate(blocks):
                                n = t * len(blocks) + i
                                if n >= 2:
                                    sp.wait_ge(block_used, n - 1)
                                K = F.w[name].shape[1]
                                sp.dma_start(block_buf[n % 2][:, 0:K], feat("g_" + name)[:, :, m * P:(m + 1) * P]).then_inc(block_loaded[n % 2], 16)
                        sp.wait_ge(res, t + 1)
                        sp.dma_start(xd[:, :, tok(t)], xin[:, :, :]).then_inc(stored, 16)
                    sp.wait_ge(stored, 16 * NT)

                inexact = sp.value_load(F.inexact[0:1, 0:1], min_val=0, max_val=1)
                with sp.If(inexact == 0):
                    tiles(False)
                with sp.Else():
                    tiles(True)

            @block.tensor
            def _(pe):
                def first_waits(t, m):
                    if m == 0:
                        pe.wait_ge(slo, t + 1)
                    n = t * MF + m
                    if n >= 2:
                        pe.wait_ge(hid, n - 1)

                def free_bank(t, m, layer):
                    n = (2 * t + layer) * MF + m
                    if n >= 2:
                        pe.wait_ge(evac, n - 1)

                def part_ready(t, layer, k):
                    pe.wait_ge(lod, t * parts + layer * MF + k + 1)

                def exact(t):
                    def product(out, name, m, act_parts, ks, K):
                        for k in ks:
                            for j in range(2):
                                mm = pe.matmul(out[:, :], F.w[name][:, k, m * P:(m + 1) * P], act_parts[j][:, k], start=(k == 0 and j == 0), stop=(k == K - 1 and j == 1))
                        return mm

                    for m in range(MF):
                        first_waits(t, m)
                        product(pair[m % 2][0], "w1", m, S, range(KD), KD).then_inc(w1d, 1)
                        product(pair[m % 2][1], "w2", m, S, range(KD), KD).then_inc(w2d, 1)
                    for layer, name, source, done in ((0, "h1", U, h1d), (1, "h2", V, h2d)):
                        for m in range(2):
                            free_bank(t, m, layer)
                            for k in range(MF - 1):
                                if m == 0:
                                    part_ready(t, layer, k)
                                product(hidden_bank[m], name, m, source, [k], MF)
                        part_ready(t, layer, MF - 1)
                        for m in range(2):
                            product(hidden_bank[m], name, m, source, [MF - 1], MF).then_inc(done, 1)
                        for m in range(2, MF):
                            free_bank(t, m, layer)
                            product(hidden_bank[m % 2], name, m, source, range(MF), MF).then_inc(done, 1)
                    if t >= 1:
                        pe.wait_ge(res, t)
                    for m in range(KD):
                        for k in range(MF - 1):
                            if m == 0:
                                part_ready(t, 2, k)
                            product(out_bank[m], "w3", m, U, [k], MF)
                    part_ready(t, 2, MF - 1)
                    for m in range(KD):
                        mm = product(out_bank[m], "w3", m, U, [MF - 1], MF)
                    mm.then_inc(w3d, 1)

                def general(t):
                    def product(out, name, m, act_parts, K):
                        n = t * len(blocks) + number[name, m]
                        pe.wait_ge(block_loaded[n % 2], 16 * (n // 2 + 1))
                        for k in range(K):
                            for j in range(2):
                                mm = pe.matmul(out[:, :], block_buf[n % 2][:, k], act_parts[j][:, k].bitcast(F32), start=(k == 0 and j == 0), stop=(k == K - 1 and j == 1))
                        mm.then_inc(block_used, 1)
                        return n + 1

                    def signal(done, n):
                        pe.wait_ge(block_used, n)
                        pe.sem_inc(done, 1)

                    for m in range(MF):
                        first_waits(t, m)
                        for j, (name, done) in enumerate((("w1", w1d), ("w2", w2d))):
                            signal(done, product(pair[m % 2][j], name, m, S, KD))
                    for layer, name, source, done in ((0, "h1", U, h1d), (1, "h2", V, h2d)):
                        part_ready(t, layer, MF - 1)
                        for m in range(MF):
                            free_bank(t, m, layer)
                            signal(done, product(hidden_bank[m % 2], name, m, source, MF))
                    if t >= 1:
                        pe.wait_ge(res, t)
                    part_ready(t, 2, MF - 1)
                    for m in range(KD):
                        n = product(out_bank[m], "w3", m, U, MF)
                    signal(w3d, n)

                inexact = pe.value_load(F.inexact[0:1, 0:1], min_val=0, max_val=1)
                with pe.If(inexact == 0):
                    for t in range(NT):
                        exact(t)
                with pe.Else():
                    for t in range(NT):
                        general(t)

            @block.scalar
            def _(act):
                for t in range(NT):
                    for m in range(MF):
                        n = t * MF + m
                        act.wait_ge(w1d, n + 1)
                        if n >= 2:
                            act.wait_ge(hid, n - 1)
                        act.activation(gated[:, m % 2], pair[m % 2][0][:, :], ACT.Silu, scale=s1[:, m:m + 1]).then_inc(silud, 1)
                    for layer, done, scale, (hi, _) in ((0, h1d, sh1, V), (1, h2d, sh2, U)):
                        for m in range(MF):
                            n = (2 * t + layer) * MF + m
                            act.wait_ge(done, t * MF + m + 1)
                            act.activation(hi[:, m], hidden_bank[m % 2][:, :], ACT.Gelu, scale=scale[:, m:m + 1])
                            if n >= 2:
                                before = n - 2
                                act.wait_ge(lod, (before // (2 * MF)) * parts + MF + before % (2 * MF) + 1)
                            act.activation(whole[:, m % 2], hidden_bank[m % 2][:, :], ACT.Gelu, scale=scale[:, m:m + 1]).then_inc(evac, 1)

            @block.vector
            def _(dve):
                dve.tensor_tensor(out_scale[:, :], gate, s3, ALU.mult).then_inc(scaled, 1)
                dve.wait_ge(scaled, 1)

                def split_s(t):
                    dve.wait_ge(sload, 16 * (t + 1))
                    if t >= 1:
                        dve.wait_ge(w2d, t * MF)
                    dve.tensor_copy(S[0][:, :, :], s32[:, :, :]).then_inc(shi, 1)
                    dve.wait_ge(shi, t + 1)
                    dve.tensor_tensor(S[1][:, :, :], s32[:, :, :], S[0][:, :, :], ALU.subtract).then_inc(slo, 1)

                split_s(0)
                for t in range(NT):
                    if t >= 1:
                        dve.wait_ge(w3d, t)
                    for m in range(MF + 1):
                        if m < MF:
                            n = t * MF + m
                            dve.wait_ge(silud, n + 1)
                            dve.wait_ge(w2d, n + 1)
                            if n >= 2:
                                dve.wait_ge(lod, ((n - 2) // MF) * parts + (n - 2) % MF + 1)
                            for out in (U[0][:, m], whole_u[:, m % 2]):
                                i = dve.scalar_tensor_tensor(out, pair[m % 2][1][:, :], s2[:, m:m + 1], gated[:, m % 2], ALU.mult, ALU.mult)
                            i.then_inc(hid, 1)
                        if m >= 1:
                            dve.wait_ge(hid, t * MF + m)
                            dve.tensor_tensor(U[1][:, m - 1], whole_u[:, (m - 1) % 2], U[0][:, m - 1], ALU.subtract).then_inc(lod, 1)
                    for layer, (hi, lo) in ((0, V), (1, U)):
                        for m in range(MF):
                            dve.wait_ge(evac, (2 * t + layer) * MF + m + 1)
                            dve.tensor_tensor(lo[:, m], whole[:, m % 2], hi[:, m], ALU.subtract).then_inc(lod, 1)
                        if layer == 0 and t + 1 < NT:
                            split_s(t + 1)
                    dve.wait_ge(w3d, t + 1)
                    dve.wait_ge(xload, 16 * (t + 1))
                    for h in range(KD):
                        i = dve.scalar_tensor_tensor(xin[:, h], out_bank[h][:, :], out_scale[:, h:h + 1], xin[:, h], ALU.mult, ALU.add)
                    i.then_inc(res, 1)
        close()


def ffn_stage(nc, G, src, dst):
    with ExitStack() as ctx:
        F = FfnWeights(nc, G, ctx, None, None)
        with ExitStack() as inner:
            S = inner.enter_context(nc.sbuf_tensor("ff_s", [P, KD, N], F32))
            Sv = lambda k, t: S[:, k, tok(t)]
            ln_pass(nc, G, "", Sv, Sv, G.eps5[:, :], G.mod[:, 1, CB:CB + KD], G.mod[:, 1, SB:SB + KD], load=load_x(G, src, S), also=F, store=(S, "s3"))
        ffn_pass(nc, G, F, src, dst)


def program(nc, io, stages="0123"):
    G = Shared()
    G.io, G.passes = io, 0
    with ExitStack() as ctx:
        sb = lambda name, shape, dt=F32: ctx.enter_context(nc.sbuf_tensor(name, shape, dt))
        G.cols = sb("cols", [P, NCOLS])
        G.ident = sb("ident", [P, P])
        G.mean_w = sb("mean_w", [P, P])
        G.mod = sb("mod", [P, 2, 12])
        G.eps3, G.eps5, G.half_pi = sb("eps3", [P, 1]), sb("eps5", [P, 1]), sb("half_pi", [P, 1])
        G.bank = [ctx.enter_context(nc.psum_tensor(f"bank{i}", [P, TT], F32)) for i in range(8)]
        G.col = lambda name: G.cols[:, COLS[name][0]:COLS[name][0] + COLS[name][1]]
        setup_pass(nc, G, "")
        for s, stage in (("0", rwkv_stage), ("1", local_attention_stage), ("2", s4d_stage), ("3", ffn_stage)):
            if s in stages:
                stage(nc, G, f"x{s}", f"x{int(s) + 1}")


def constants():
    import numpy as np
    c = {"ident": np.eye(P, dtype=np.float32)}
    i, j = np.arange(W)[:, None], np.arange(W)[None, :]
    now, before, never = (np.where(m, 0.0, -1e30) for m in (j <= i, j >= i, np.zeros((W, W), bool)))
    c["masks"] = np.stack([np.concatenate(m, 1) for m in ((now, before), (before, now), (now, never))], 1).astype(np.float32)
    half = np.arange(0, DH, 2, dtype=np.float32)
    inv = (1.0 / np.power(np.float32(10000.0), half / np.float32(DH))).astype(np.float32)
    t = np.arange(N, dtype=np.float32)
    fr = np.tile((t[:, None] * inv[None, :]).astype(np.float32), (1, 2)).astype(np.float64)
    base = (half + 0.4 * DH) / (1.4 * DH)
    sc = np.tile(base[None, :] ** ((t - N // 2) / float(W // 2))[:, None], (1, 2)).astype(np.float64)
    sign = np.where(np.arange(DH) < DH // 2, -1.0, 1.0)[None, :]
    rot = np.stack([np.cos(fr) * sc * 8.0, np.sin(fr) * sc * 8.0 * sign, np.cos(fr) / sc, np.sin(fr) / sc * sign], 1)
    c["rotary"] = np.ascontiguousarray(rot.astype(np.float32).reshape(NW, W, 4, DH))
    c["ramp"] = np.ascontiguousarray(np.broadcast_to(np.arange(C + 1, dtype=np.float32), (P, C + 1)))
    c["quads"] = np.ascontiguousarray((np.arange(P)[:, None] // SN == np.arange(Q4)[None, :]).astype(np.float32))
    return c


def lay_out(inp):
    import numpy as np
    a = {}

    def per_feature(v, n):
        v = np.asarray(v)
        full = np.zeros((n * P,), v.dtype)
        full[:v.shape[0]] = v
        return full.reshape(n, P).T

    vec = {}
    for k in ("ln1_g", "ln1_b", "ln2_g", "ln2_b", "tm_mix_k", "tm_mix_v", "tm_mix_r", "time_decay", "time_first", "cm_mix_k", "cm_mix_r"):
        vec[k] = inp["L0_attn_" + k]
    vec["c0"], vec["c1"] = inp["L0_c"][0], inp["L1_c"][0]
    for l in range(DEPTH):
        vec[f"f_ln_g{l}"], vec[f"f_ln_b{l}"] = inp["L0_ffn_ln_g"][l], inp["L0_ffn_ln_b"][l]
        vec[f"f_b1a{l}"], vec[f"f_b1g{l}"] = inp["L0_ffn_b1"][l][:HID], inp["L0_ffn_b1"][l][HID:]
        vec[f"f_b2{l}"] = inp["L0_ffn_b2"][l]
    for l in range(NL):
        vec[f"s_ln_w{l}"], vec[f"s_ln_b{l}"] = inp["L1_attn_ln_w"][l], inp["L1_attn_ln_b"][l]
        vec[f"s_b{l}"] = inp["L1_attn_b_out"][l]
    for k in ("w1_s", "w2_s", "h1_s", "h2_s", "w3_s"):
        vec[k] = inp["L1_ffn_" + k]
    a["cols"] = np.ascontiguousarray(np.concatenate([per_feature(vec[k], COLS[k][1]) for k in COLS], axis=1))
    a["wmod0"], a["wmod1"] = inp["L0_wmod"], inp["L1_wmod"]
    for k in ("tm_Wk", "tm_Wv", "tm_Wr", "Wo", "cm_Wk", "cm_Wv", "cm_Wr"):
        a[k] = inp["L0_attn_" + k]
    for k in ("wqkv", "q_scale", "k_scale", "wo", "w1", "w2"):
        a[k] = inp["L0_ffn_" + k]

    def by_quads(v, axis_n=True):
        v = np.asarray(v)
        if not axis_n:
            v = np.broadcast_to(v[:, :, None], (NL, D, SN))
        return np.ascontiguousarray(v.reshape(NL, HQ, Q4, SN).transpose(2, 3, 0, 1).reshape(P, NL, HQ))

    a["s_log_dt"] = by_quads(inp["L1_attn_log_dt"], False)
    for k in ("A_re_log", "A_im", "C_re", "C_im"):
        a["s_" + k] = by_quads(inp["L1_attn_" + k])
    a["s_D"] = np.ascontiguousarray(np.asarray(inp["L1_attn_D_skip"]).reshape(NL, HQ, Q4).transpose(2, 0, 1))
    a["s_W"] = np.ascontiguousarray(np.asarray(inp["L1_attn_W_out"]).transpose(0, 2, 1))
    for k in ("w1", "w2", "h1", "h2", "w3"):
        a["g_" + k] = np.ascontiguousarray(np.asarray(inp[f"L1_ffn_{k}_w"]).T)
    a.update(constants())
    return {k: np.ascontiguousarray(v) for k, v in a.items()}


def kernel(**inputs):
    import numpy as np
    import concourse.bacc as bacc
    from concourse.bass_utils import run_bass_kernel_spmd

    nc = bacc.Bacc("TRN2", target_bir_lowering=False, num_devices=1)
    arrays = {"in_" + k: v for k, v in lay_out({k: np.asarray(v) for k, v in inputs.items()}).items()}
    arrays["in_x0"] = np.ascontiguousarray(np.asarray(inputs["L0_attn_inputs"])[0].T)
    io = {k[3:]: nc.dram_tensor(k, v.shape, mybir.dt.from_np(v.dtype), kind="ExternalInput").ap() for k, v in arrays.items()}
    for s in (1, 2, 3):
        io[f"x{s}"] = nc.dram_tensor(f"x{s}", [D, N], F32, kind="Internal").ap()
    io["s3"] = nc.dram_tensor("s3", [D, N], F32, kind="Internal").ap()
    io["taps"] = nc.dram_tensor("taps", [HQ, Q4, 2 * C], F32, kind="Internal").ap()
    io["x4"] = nc.dram_tensor("out_x", [D, N], F32, kind="ExternalOutput").ap()
    program(nc, io)
    r = run_bass_kernel_spmd(nc, [arrays], core_ids=[0])
    return np.ascontiguousarray(r.results[0]["out_x"].T)[None]
```

```python
from contextlib import ExitStack

import concourse.bass as bass
from concourse import mybir

F32 = mybir.dt.float32
F32R = mybir.dt.float32r
I32 = mybir.dt.int32
BF16 = mybir.dt.bfloat16
ALU = mybir.AluOpType
ACT = mybir.ActivationFunctionType
AX = mybir.AxisListType

P = 128
D = 256
KD = D // P
N = 4096
TT = 512
NT = N // TT
W = 128
NW = N // W
HEADS, DH = 8, 64
INNER = HEADS * DH
DEPTH = 2
HID = 682
HK = -(-HID // P)
HLAST = HID - (HK - 1) * P
CM = 4 * D
FF = 1024
NL = 4
SN = 32
Q4 = 4
HQ = D // Q4
C = 128
NC = N // C
GQ = 4
GC = GQ * Q4
NG = HQ // GQ
MAGIC = 1.5 * 2.0 ** 23
TWO_PI = 6.2831850
PI = TWO_PI / 2

COLS = {}


def _cols():
    at = 0
    for name, n in ([(k, KD) for k in (
            "ln1_g", "ln1_b", "ln2_g", "ln2_b", "tm_mix_k", "tm_mix_v", "tm_mix_r",
            "time_decay", "time_first", "cm_mix_k", "cm_mix_r", "c0", "c1")]
            + [(f"f_ln_g{l}", KD) for l in range(DEPTH)] + [(f"f_ln_b{l}", KD) for l in range(DEPTH)]
            + [(f"f_b1a{l}", HK) for l in range(DEPTH)] + [(f"f_b1g{l}", HK) for l in range(DEPTH)]
            + [(f"f_b2{l}", KD) for l in range(DEPTH)]
            + [(f"s_ln_w{l}", KD) for l in range(NL)] + [(f"s_ln_b{l}", KD) for l in range(NL)]
            + [(f"s_b{l}", 2 * KD) for l in range(NL)]
            + [("w1_s", FF // P), ("w2_s", FF // P), ("h1_s", FF // P), ("h2_s", FF // P), ("w3_s", KD)]):
        COLS[name] = (at, n)
        at += n
    return at


NCOLS = _cols()
SA, CA, GA, SB, CB, GB = (KD * j for j in range(6))


class Shared:
    pass


def known(t):
    return isinstance(t, int)


def past(t, k):
    return not known(t) or t >= k


def run(eng, n, steps, width=2):
    deepest = max(lag for lag, _ in steps)
    head = -(-(deepest + width) // width) * width
    loops = (n - head) // width
    if n < 24:
        head, loops = n, 0

    def straight(s):
        for lag, f in steps:
            if 0 <= s - lag < n:
                f(s - lag, (s - lag) % width)

    for s in range(head):
        straight(s)
    if loops:
        with eng.Fori(head // width, head // width + loops) as turn:
            for j in range(width):
                for lag, f in steps:
                    f(turn * width + (j - lag), (j - lag) % width)
    for s in range(head + loops * width, n + deepest):
        straight(s)


def open_pass(nc, G, ctx):
    G.passes += 1
    sems, mark = [], f"_{G.passes}"

    def sb(name, shape, dt=F32):
        return ctx.enter_context(nc.sbuf_tensor(name + mark, shape, dt))

    def sem(name):
        s = nc.alloc_semaphore(name + mark)
        sems.append(s)
        return s

    def close():
        nc.clear_and_free_semaphores(sems)
        nc.all_engine_barrier()

    return sb, sem, close


def chain(eng, sem):
    count = [0]

    def link(ins):
        count[0] += 1
        ins.then_inc(sem, 1)
        eng.wait_ge(sem, count[0])

    return link


def product_of_parts(pe, out, w, x, ks, K):
    for k in ks:
        for i, (a, b) in enumerate(((0, 0), (0, 1), (1, 0))):
            mm = pe.matmul(out, w(a, k), x(b, k), start=(k == 0 and i == 0), stop=(k == K - 1 and i == 2))
    return mm


def tok(t, shift=0, size=TT):
    return bass.ds(t * size + shift, size)


def setup_pass(nc, G):
    with ExitStack() as ctx:
        sb, sem, close = open_pass(nc, G, ctx)
        wmod = sb("wmod", [P, 2, KD, 6 * D])
        silu_c = sb("silu_c", [P, 2, KD])
        sign = sb("sign", [P, 2, 12])
        mag = sb("mag", [P, 2, 12])
        loaded, wloaded = sem("loaded"), sem("wloaded")
        silu_ready, mod_ready, link_s = sem("silu_ready"), sem("mod_ready"), sem("link_s")
        constants_ready = sem("constants_ready")
        G.s4d.open(sb, sem)
        with nc.Block() as block:
            @block.sync
            def _(sp):
                sp.dma_start(G.cols[:, :], G.io["cols"]).then_inc(loaded, 16)
                sp.dma_start(G.ident[:, :], G.io["ident"]).then_inc(loaded, 16)
                for l in range(2):
                    sp.dma_start(wmod[:, l], G.io[f"wmod{l}"].rearrange("(k p) n -> p k n", p=P)).then_inc(wloaded, 16)
                G.s4d.sync(sp)

            @block.scalar
            def _(act):
                act.wait_ge(loaded, 32)
                for l in range(2):
                    act.activation(silu_c[:, l], G.col(f"c{l}"), ACT.Silu).then_inc(silu_ready, 1)
                act.wait_ge(constants_ready, 1)
                G.s4d.scalar(act)

            @block.gpsimd
            def _(pool):
                G.s4d.gpsimd(pool)

            @block.tensor
            def _(pe):
                pe.wait_ge(silu_ready, 2)
                pe.wait_ge(wloaded, 32)
                for l in range(2):
                    for m in range(12):
                        for k in range(KD):
                            mm = pe.matmul(G.bank[l][:, m:m + 1], wmod[:, l, k, m * P:(m + 1) * P],
                                           silu_c[:, l, k:k + 1], start=(k == 0), stop=(k == KD - 1))
                    mm.then_inc(mod_ready, 1)

            @block.vector
            def _(dve):
                link = chain(dve, link_s)
                dve.memset(G.mean_w[:, :], 1.0 / D)
                dve.memset(G.eps3[:, :], 1e-3)
                dve.memset(G.half_pi[:, :], TWO_PI / 4)
                dve.memset(G.eps5[:, :], 1e-5).then_inc(constants_ready, 1)
                G.s4d.vector(dve)
                dve.wait_ge(mod_ready, 2)
                for l in range(2):
                    M = G.mod[:, l, :]
                    link(dve.tensor_copy(M, G.bank[l][:, 0:12]))
                    link(dve.tensor_scalar(sign[:, l], M, 0.0, 2.0, ALU.is_ge, ALU.mult))
                    link(dve.tensor_scalar(sign[:, l], sign[:, l], -1.0, None, ALU.add))
                    link(dve.tensor_tensor(mag[:, l], sign[:, l], M, ALU.mult))
                    link(dve.tensor_scalar(mag[:, l], mag[:, l], 0.25, None, ALU.max))
                    for at in (CA, CB):
                        link(dve.tensor_scalar(M[:, at:at + KD], M[:, at:at + KD], 1.0, None, ALU.add))
                    for at in (GA, GB):
                        link(dve.tensor_tensor(M[:, at:at + KD], mag[:, l, at:at + KD], sign[:, l, at:at + KD], ALU.mult))
        close()


def ln_pass(nc, G, src, dst, eps, gain, bias, load=None, also=None, store=None, turn=None):
    XC = 4
    with ExitStack() as ctx:
        sb, sem, close = open_pass(nc, G, ctx)
        xc = sb("ln_xc", [P, XC, KD, TT])
        sq = sb("ln_sq", [P, 2, KD, TT])
        both = sb("ln_both", [P, 2, TT])
        sq_both = sb("ln_sq_both", [P, 2, TT])
        inv = sb("ln_inv", [P, 2, TT])
        src_loaded = [sem(f"src_loaded{t}") for t in range(NT)] if load is not None else []
        mean_ready, centered = sem("mean_ready"), sem("centered")
        added, sq_added, turned, evA, evV = sem("added"), sem("sq_added"), sem("turned"), sem("evA"), sem("evV")
        squared, var_ready, log_ready = sem("squared"), sem("var_ready"), sem("log_ready")
        inv_ready, normed, affined = sem("inv_ready"), sem("normed"), sem("affined")
        mean_bank, var_bank, turn_bank = G.bank[0:2], G.bank[2:4], G.bank[4:8]
        if also:
            also.open(sb, sem)
            stored = sem("stored")
        with nc.Block() as block:
            if load is not None:
                @block.sync
                def _(sp):
                    load(sp, src_loaded)
                    if also:
                        def store_tile(t, p):
                            sp.wait_ge(affined, t + 1)
                            sp.dma_start(G.io[store[1]].rearrange("(k p) n -> p k n", p=P)[:, :, tok(t)], store[0][:, :, tok(t)]).then_inc(stored, 16)
                        run(sp, NT, [(0, lambda t, p: also.load(sp, t)), (5, store_tile)])
                        sp.wait_ge(stored, 16 * NT)

            @block.gpsimd
            def _(pool):
                def add(t, p):
                    if load is not None:
                        pool.wait_ge(src_loaded[t], 16)
                    if past(t, 2):
                        pool.wait_ge(mean_ready, t - 1)
                    pool.tensor_tensor(both[:, p], src(0, t), src(1, t), ALU.add).then_inc(added, 1)

                def add_squares(t, p):
                    pool.wait_ge(squared, t + 1)
                    if past(t, 2):
                        pool.wait_ge(var_ready, t - 1)
                    pool.tensor_tensor(sq_both[:, p], sq[:, p, 0], sq[:, p, 1], ALU.add).then_inc(sq_added, 1)

                run(pool, NT, [(0, add), (1, add_squares)])

            @block.tensor
            def _(pe):
                def mean(t, p):
                    pe.wait_ge(added, t + 1)
                    if past(t, 2):
                        pe.wait_ge(centered, t - 1)
                    pe.matmul(mean_bank[p][:, :], G.mean_w[:, :], both[:, p], start=True, stop=True).then_inc(mean_ready, 1)

                def var(t, p):
                    pe.wait_ge(sq_added, t + 1)
                    if past(t, 2):
                        pe.wait_ge(log_ready, t - 1)
                    pe.matmul(var_bank[p][:, :], G.mean_w[:, :], sq_both[:, p], start=True, stop=True).then_inc(var_ready, 1)

                def turn_chunks(t, p):
                    pe.wait_ge(affined, t + 1)
                    for n in range(t * TT // C // 2, (t + 1) * TT // C // 2):
                        if n >= 4:
                            pe.wait_ge((evA, evV)[n % 2], (n - 4) // 2 + 1)
                        for a in range(2):
                            for h in range(KD):
                                t0 = (2 * n + a) * C
                                mm = pe.transpose(turn_bank[n % 4][:, (KD * a + h) * P:(KD * a + h + 1) * P], turn[0][:, h, t0:t0 + C], G.ident[:, :])
                        mm.then_inc(turned, 1)

                run(pe, NT, [(0, mean), (1, var)] + ([(3, turn_chunks)] if turn else []))
                if also:
                    also.count(pe)

            @block.vector
            def _(dve):
                def center(t, p):
                    dve.wait_ge(mean_ready, t + 1)
                    if past(t, XC):
                        dve.wait_ge(affined, t - XC + 1)
                    for k in range(KD):
                        i = dve.tensor_tensor(xc[:, t % XC, k], src(k, t), mean_bank[p][:, :], ALU.subtract)
                    i.then_inc(centered, 1)

                def norm(t, p):
                    dve.wait_ge(inv_ready, t + 1)
                    for k in range(KD):
                        i = dve.tensor_tensor(xc[:, t % XC, k], xc[:, t % XC, k], inv[:, p], ALU.mult)
                    i.then_inc(normed, 1)

                def affine(t, p):
                    dve.wait_ge(normed, t + 1)
                    for k in range(KD):
                        out = dst(k, t)
                        x = xc[:, t % XC, k] if len(out.shape) == 2 else xc[:, t % XC, k].rearrange("p (c j) -> p c j", j=out.shape[2])
                        i = dve.tensor_scalar(out, x, gain[:, k:k + 1], bias[:, k:k + 1], ALU.mult, ALU.add)
                    i.then_inc(affined, 1)

                def turned_odd(t, p):
                    n = 2 * t + 1
                    dve.wait_ge(turned, n + 1)
                    dve.tensor_copy(turn[1][:, :, 2 * n:2 * n + 2], turn_bank[n % 4][:, :].rearrange("p (c h) -> p h c", c=2)).then_inc(evV, 1)

                run(dve, NT, [(0, center), (3, affine), (2, norm)] + ([(4, turned_odd)] if turn else [])
                    + ([(5, lambda t, p: also.subtract(dve, t))] if also else []))
                if also:
                    also.decide(dve)

            @block.scalar
            def _(act):
                def square(t, p):
                    act.wait_ge(centered, t + 1)
                    if past(t, 2):
                        act.wait_ge(sq_added, t - 1)
                    act.activation(sq[:, p], xc[:, t % XC], ACT.Square).then_inc(squared, 1)

                def root(t, p):
                    act.wait_ge(var_ready, t + 1)
                    if past(t, 2):
                        act.wait_ge(normed, t - 1)
                    act.activation(inv[:, p], var_bank[p][:, :], ACT.Ln, bias=eps).then_inc(log_ready, 1)
                    act.wait_ge(log_ready, t + 1)
                    act.activation(inv[:, p], inv[:, p], ACT.Exp, scale=-0.5).then_inc(inv_ready, 1)

                act.preload_act_table_set("natural_log_exp_and_others")
                def turned_even(t, p):
                    n = 2 * t
                    act.wait_ge(turned, n + 1)
                    act.activation(turn[1][:, :, 2 * n:2 * n + 2], turn_bank[n % 4][:, :].rearrange("p (c h) -> p h c", c=2), ACT.Copy).then_inc(evA, 1)

                more = [(3, turned_even)] if turn else []
                if also:
                    more += [(5, lambda t, p: also.round(act, t)), (6, lambda t, p: also.sum_rests(act, t))]
                run(act, NT, [(0, square), (1, root)] + more)
        close()


def load_x(G, name, X):
    def load(sp, done):
        for t in range(NT):
            sp.dma_start(X[:, :, t * TT:(t + 1) * TT],
                         G.io[name].rearrange("(k p) n -> p k n", p=P)[:, :, t * TT:(t + 1) * TT]).then_inc(done[t], 16)
    return load


def time_mix_pass(nc, G, H, S):
    with ExitStack() as ctx:
        sb, sem, close = open_pass(nc, G, ctx)
        wkvr = sb("tm_w", [P, 3, KD, D])
        wo = sb("tm_wo", [P, KD, D])
        decay = sb("decay", [P, KD, TT])
        wdec = sb("wdec", [P, KD])
        d = sb("tm_d", [P, 2, KD, TT])
        mix = sb("tm_mix", [P, 3, KD, TT])
        mixr = sb("tm_mixr", [P, KD, TT])
        kvr = sb("tm_kvr", [P, 2, 3, KD, TT])
        pp = sb("tm_pp", [P, 2, KD, 1 + TT])
        ab = sb("tm_ab", [P, 1, 2, KD, 1 + TT])
        ex = sb("tm_ex", [P, 2, 4, KD, TT])
        ev = sb("tm_ev", [P, 1, 2, KD, TT])
        rw = sb("tm_rw", [P, 1, KD, TT])
        names = ("weights", "dif", "mixk", "mixv", "mixr_h", "mixr", "proj", "evac", "args", "exps", "evs", "dend", "logd", "invd", "out", "wod", "res", "dec", "l")
        weights, dif, mixk, mixv, mixr_h, mixr_s, proj, evac, args, exps, evs, dend, logd, invd, out, wod, res, dec, link_s = (sem("tm_" + n) for n in names)
        kvr_bank, wo_bank = G.bank[0:6], G.bank[6:8]
        cols = [G.col(n) for n in ("tm_mix_k", "tm_mix_v", "tm_mix_r")]
        u = G.col("time_first")
        with nc.Block() as block:
            @block.sync
            def _(sp):
                for j, n in enumerate(("tm_Wk", "tm_Wv", "tm_Wr")):
                    sp.dma_start(wkvr[:, j], G.io[n].rearrange("(k p) n -> p k n", p=P)).then_inc(weights, 16)
                sp.dma_start(wo[:, :, :], G.io["Wo"].rearrange("(k p) n -> p k n", p=P)).then_inc(weights, 16)

            @block.gpsimd
            def _(pool):
                def difference(t, p):
                    if past(t, 2):
                        pool.wait_ge(mixv, t - 1)
                        pool.wait_ge(mixr_s, t - 1)
                    pool.tensor_tensor(d[:, p], S[:, :, tok(t, 1)], S[:, :, tok(t)], ALU.subtract).then_inc(dif, 1)

                def mix_r(t, p):
                    pool.wait_ge(dif, t + 1)
                    if past(t, 1):
                        pool.wait_ge(mixr_s, t)
                    for k in range(KD):
                        i = pool.tensor_scalar(mixr[:, k], d[:, p, k], cols[2][:, k:k + 1], None, ALU.mult)
                    i.then_inc(mixr_h, 1)
                    pool.wait_ge(mixr_h, t + 1)
                    if past(t, 1):
                        pool.wait_ge(proj, t)
                    pool.tensor_tensor(mix[:, 2], mixr[:, :], S[:, :, tok(t)], ALU.add).then_inc(mixr_s, 1)

                def weighted(t, p):
                    if past(t, 1):
                        pool.wait_ge(out, t)
                    for j in range(2):
                        pool.wait_ge(exps, 2 * t + j + 1)
                        pool.tensor_tensor(ev[:, 0, j], ex[:, p, 2 * j + 1], kvr[:, p, 1], ALU.mult).then_inc(evs, 1)

                run(pool, NT, [(1, mix_r), (3, weighted), (0, difference)])

            @block.tensor
            def _(pe):
                def project(t, p):
                    if t == 0:
                        pe.wait_ge(weights, 64)
                    pe.wait_ge(mixk, t + 1)
                    pe.wait_ge(mixv, t + 1)
                    pe.wait_ge(mixr_s, t + 1)
                    if t >= 1:
                        pe.wait_ge(evac, t)
                    for j in range(3):
                        for m in range(KD):
                            for k in range(KD):
                                mm = pe.matmul(kvr_bank[2 * j + m][:, :], wkvr[:, j, k, m * P:(m + 1) * P], mix[:, j, k],
                                               start=(k == 0), stop=(k == KD - 1))
                    mm.then_inc(proj, 1)

                def outproj(t, p):
                    pe.wait_ge(out, t + 1)
                    if t >= 1:
                        pe.wait_ge(res, t)
                    for m in range(KD):
                        for k in range(KD):
                            mm = pe.matmul(wo_bank[m][:, :], wo[:, k, m * P:(m + 1) * P], rw[:, 0, k], start=(k == 0), stop=(k == KD - 1))
                    mm.then_inc(wod, 1)

                run(pe, NT, [(1, project), (3, outproj)])

            @block.scalar
            def _(act):
                act.activation(wdec[:, :], G.col("time_decay"), ACT.Exp).then_inc(dec, 1)

                def evacuate(t, p):
                    act.wait_ge(proj, t + 1)
                    if t >= 2:
                        act.wait_ge(out, t - 1)
                    for j in range(3):
                        for m in range(KD):
                            i = act.activation(kvr[:, p, j, m], kvr_bank[2 * j + m][:, :], ACT.Tanh if j == 2 else ACT.Copy,
                                               scale=0.5 if j == 2 else 1.0)
                    i.then_inc(evac, 1)

                def inverse(t, p):
                    act.wait_ge(dend, t + 1)
                    act.preload_act_table_set("natural_log_exp_and_others")
                    act.activation(ex[:, p, 1], ex[:, p, 1], ACT.Ln).then_inc(logd, 1)
                    act.wait_ge(logd, t + 1)
                    act.activation(ex[:, p, 1], ex[:, p, 1], ACT.Exp, scale=-1.0).then_inc(invd, 1)

                def exponents(t, p):
                    act.wait_ge(args, t + 1)
                    for j in (0, 2):
                        act.activation(ex[:, p, j:j + 2], ex[:, p, j:j + 2], ACT.Exp).then_inc(exps, 1)

                run(act, NT, [(3, inverse), (2, exponents), (1, evacuate)])

            @block.vector
            def _(dve):
                link = chain(dve, link_s)
                dve.wait_ge(dec, 1)
                link(dve.tensor_scalar(wdec[:, :], wdec[:, :], -1.0, None, ALU.mult))
                link(dve.memset(decay[:, :, :], 0.0))
                for k in range(KD):
                    link(dve.tensor_scalar(decay[:, k], decay[:, k], wdec[:, k:k + 1], None, ALU.add))
                dve.memset(pp[:, 0, :, 0:1], -1e38)
                link(dve.memset(ab[:, 0, :, :, 0:1], 0.0))

                def mixes(t, p):
                    dve.wait_ge(dif, t + 1)
                    if t >= 1:
                        dve.wait_ge(proj, t)
                    for j, s in ((0, mixk), (1, mixv)):
                        for k in range(KD):
                            i = dve.scalar_tensor_tensor(mix[:, j, k], d[:, p, k], cols[j][:, k:k + 1], S[:, k, tok(t)], ALU.mult, ALU.add)
                        i.then_inc(s, 1)

                def arguments(t, p):
                    dve.wait_ge(evac, t + 1)
                    if t >= 2:
                        dve.wait_ge(out, t - 1)
                    if t >= 1:
                        link(dve.tensor_copy(pp[:, p, :, 0:1], pp[:, 1 - p, :, TT:TT + 1]))
                    K = kvr[:, p, 0]
                    for h in range(KD):
                        i = dve.tensor_tensor_scan(pp[:, p, h, 1:1 + TT], decay[:, h], K[:, h], pp[:, p, h, 0:1], ALU.add, ALU.max)
                    link(i)
                    prev, cur = pp[:, p, :, 0:TT], pp[:, p, :, 1:1 + TT]
                    for h in range(KD):
                        dve.scalar_tensor_tensor(ex[:, p, 0, h], prev[:, h], wdec[:, h:h + 1], cur[:, h], ALU.add, ALU.subtract)
                        dve.scalar_tensor_tensor(ex[:, p, 2, h], K[:, h], u[:, h:h + 1], prev[:, h], ALU.add, ALU.max)
                    link(dve.tensor_tensor(ex[:, p, 1], K, cur, ALU.subtract))
                    for h in range(KD):
                        i = dve.scalar_tensor_tensor(ex[:, p, 3, h], K[:, h], u[:, h:h + 1], ex[:, p, 2, h], ALU.add, ALU.subtract)
                    link(i)
                    dve.tensor_tensor(ex[:, p, 2], prev, ex[:, p, 2], ALU.subtract).then_inc(args, 1)

                def sums(t, p):
                    dve.wait_ge(exps, 2 * t + 2)
                    if t >= 1:
                        link(dve.tensor_copy(ab[:, 0, :, :, 0:1], ab[:, 0, :, :, TT:TT + 1]))
                    for h in range(KD):
                        dve.tensor_tensor_scan(ab[:, 0, 1, h, 1:1 + TT], ex[:, p, 0, h], ex[:, p, 1, h], ab[:, 0, 1, h, 0:1], ALU.mult, ALU.add)
                    dve.wait_ge(evs, 2 * t + 1)
                    for h in range(KD):
                        i = dve.tensor_tensor_scan(ab[:, 0, 0, h, 1:1 + TT], ex[:, p, 0, h], ev[:, 0, 0, h], ab[:, 0, 0, h, 0:1], ALU.mult, ALU.add)
                    link(i)
                    num, den = ex[:, p, 0], ex[:, p, 1]
                    dve.tensor_tensor(den, ex[:, p, 2], ab[:, 0, 1, :, 0:TT], ALU.mult)
                    link(dve.tensor_tensor(num, ex[:, p, 2], ab[:, 0, 0, :, 0:TT], ALU.mult))
                    dve.wait_ge(evs, 2 * t + 2)
                    dve.tensor_tensor(den, den, ex[:, p, 3], ALU.add).then_inc(dend, 1)
                    link(dve.tensor_tensor(num, num, ev[:, 0, 1], ALU.add))

                def quotient(t, p):
                    dve.wait_ge(invd, t + 1)
                    num, den = ex[:, p, 0], ex[:, p, 1]
                    link(dve.tensor_tensor(num, num, den, ALU.mult))
                    if t >= 1:
                        dve.wait_ge(wod, t)
                    dve.scalar_tensor_tensor(rw[:, 0], kvr[:, p, 2], 1.0, num, ALU.add, ALU.mult).then_inc(out, 1)

                def residual(t, p):
                    dve.wait_ge(wod, t + 1)
                    for h in range(KD):
                        i = dve.scalar_tensor_tensor(H[:, h, tok(t)], wo_bank[h][:, :], 0.5, H[:, h, tok(t)], ALU.mult, ALU.add)
                    i.then_inc(res, 1)

                run(dve, NT, [(1, mixes), (3, sums), (2, arguments), (4, residual), (3, quotient)])
        close()


def channel_mix_pass(nc, G, H, S, src, dst):
    MF = CM // P
    with ExitStack() as ctx:
        sb, sem, close = open_pass(nc, G, ctx)
        parts = lambda n, shape: [sb(f"cm_{n}_{part}", shape, F32R) for part in ("hi", "lo")]
        wr, wk, wv = parts("wr", [P, KD, D]), parts("wk", [P, KD, CM]), parts("wv", [P, MF, D])
        d = sb("cm_d", [P, KD, TT])
        whole_mix = sb("cm_whole_mix", [P, 2, KD, TT])
        mix = parts("mix", [P, 2, KD, TT])
        relu = sb("cm_relu", [P, 2, TT])
        whole = sb("cm_whole", [P, 2, TT])
        th = sb("cm_th", [P, 2, KD, TT])
        xin = sb("cm_x", [P, 2, KD, TT])
        with ExitStack() as early:
            raw = [early.enter_context(nc.sbuf_tensor(f"cm_raw_{n}", shape, F32)) for n, shape in (("r", [P, KD, D]), ("k", [P, KD, CM]), ("v", [P, MF, D]))]
        kc = parts("kc", [P, MF, TT])
        weights = [sem(f"cm_weights{i}") for i in range(3)]
        whi, wlo, dif, mixed, mhi, mlo, krdy, relud, squared, khi, klo, rrdy, tanhed, vrdy, res, xload, stored, link_s = (
            sem("cm_" + n) for n in ("whi", "wlo", "dif", "mixed", "mhi", "mlo", "krdy", "relud", "squared", "khi", "klo", "rrdy", "tanhed", "vrdy", "res",
                                     "xload", "stored", "l"))
        xld = [xload, sem("cm_xload1")]
        k_bank, r_bank, v_bank = G.bank[0:4], G.bank[4:6], G.bank[6:8]
        mk, mr = G.col("cm_mix_k"), G.col("cm_mix_r")
        gate = G.mod[:, 0, GA:GA + KD]
        xs = G.io[src].rearrange("(k p) n -> p k n", p=P)
        xd = G.io[dst].rearrange("(k p) n -> p k n", p=P)
        pairs = list(enumerate(zip(raw, (wr, wk, wv))))
        with nc.Block() as block:
            @block.sync
            def _(sp):
                for i, n in enumerate(("cm_Wr", "cm_Wk", "cm_Wv")):
                    sp.dma_start(raw[i][:, :, :], G.io[n].rearrange("(k p) n -> p k n", p=P)).then_inc(weights[i], 16)
                for t in range(NT):
                    if t >= 2:
                        sp.wait_ge(res, t - 1)
                        sp.dma_start(xd[:, :, tok(t - 2)], xin[:, t % 2]).then_inc(stored, 16)
                        sp.wait_ge(stored, 16 * (t - 1))
                    sp.dma_start(xin[:, t % 2], xs[:, :, tok(t)]).then_inc(xld[t % 2], 16)
                for t in range(NT, NT + 2):
                    sp.wait_ge(res, t - 1)
                    sp.dma_start(xd[:, :, tok(t - 2)], xin[:, t % 2]).then_inc(stored, 16)
                sp.wait_ge(stored, 16 * NT)

            @block.gpsimd
            def _(pool):
                def difference(t, p):
                    if t >= 1:
                        pool.wait_ge(mixed, t)
                    pool.tensor_tensor(d[:, :], S[:, :, tok(t, 1)], S[:, :, tok(t)], ALU.subtract).then_inc(dif, 1)

                def mix_low(t, p):
                    pool.wait_ge(mhi, t + 1)
                    pool.tensor_tensor(mix[1][:, :, :, :], whole_mix[:, :, :, :], mix[0][:, :, :, :], ALU.subtract).then_inc(mlo, 1)
                run(pool, NT, [(0, difference), (0, mix_low)])

            @block.tensor
            def _(pe):
                def front(t, p):
                    if t == 0:
                        pe.wait_ge(wlo, 2)
                    pe.wait_ge(mlo, t + 1)
                    if t >= 1:
                        pe.wait_ge(tanhed, t)
                    for m in range(KD):
                        mm = product_of_parts(pe, r_bank[m][:, :], lambda a, k: wr[a][:, k, m * P:(m + 1) * P], lambda b, k: mix[b][:, 1, k], range(KD), KD)
                    mm.then_inc(rrdy, 1)
                    for m in range(MF):
                        n = t * MF + m
                        if n >= 4:
                            pe.wait_ge(relud, n - 3)
                        product_of_parts(pe, k_bank[m % 4][:, :], lambda a, k: wk[a][:, k, m * P:(m + 1) * P], lambda b, k: mix[b][:, 0, k],
                                         range(KD), KD).then_inc(krdy, 1)

                def back(t, p):
                    if t == 0:
                        pe.wait_ge(wlo, 3)
                    if t >= 1:
                        pe.wait_ge(res, t)
                    for k in range(MF):
                        pe.wait_ge(klo, t * MF + k + 1)
                        for m in range(KD):
                            mm = product_of_parts(pe, v_bank[m][:, :], lambda a, k: wv[a][:, k, m * P:(m + 1) * P], lambda b, k: kc[b][:, k], [k], MF)
                    mm.then_inc(vrdy, 1)

                run(pe, NT, [(1, front), (1, back)])

            @block.scalar
            def _(act):
                def weights_high(which):
                    for i, (w32, w) in which:
                        act.wait_ge(weights[i], 16)
                        act.activation(w[0][:, :, :], w32[:, :, :], ACT.Copy).then_inc(whi, 1)

                def value_weights(t, p):
                    if t == 0:
                        weights_high(pairs[2:])
                weights_high(pairs[:2])

                def mix_high(t, p):
                    act.wait_ge(mixed, t + 1)
                    if t >= 1:
                        act.wait_ge(krdy, t * MF)
                    act.activation(mix[0][:, :, :, :], whole_mix[:, :, :, :], ACT.Copy).then_inc(mhi, 1)

                def gate_r(t, p):
                    act.wait_ge(rrdy, t + 1)
                    if t >= 2:
                        act.wait_ge(res, t - 1)
                    for m in range(KD):
                        i = act.activation(th[:, p, m], r_bank[m][:, :], ACT.Tanh, scale=0.5)
                    i.then_inc(tanhed, 1)

                def square_high(t, p):
                    if t >= 1:
                        act.wait_ge(vrdy, t)
                    for m in range(MF + 1):
                        n = t * MF + m
                        if m < MF:
                            act.wait_ge(krdy, n + 1)
                            if n >= 2:
                                act.wait_ge(squared, n - 1)
                                act.wait_ge(khi, n - 1)
                            act.activation(relu[:, m % 2], k_bank[m % 4][:, :], ACT.Relu).then_inc(relud, 1)
                        if m >= 1:
                            act.wait_ge(relud, n)
                            act.activation(kc[0][:, m - 1], relu[:, (m - 1) % 2], ACT.Square).then_inc(khi, 1)

                run(act, NT, [(1, gate_r), (1, square_high), (0, mix_high), (0, value_weights)])

            @block.vector
            def _(dve):
                link = chain(dve, link_s)
                def weights_low(t, p):
                    if t == 0:
                        for i, (w32, w) in pairs:
                            dve.wait_ge(whi, i + 1)
                            dve.tensor_tensor(w[1][:, :, :], w32[:, :, :], w[0][:, :, :], ALU.subtract).then_inc(wlo, 1)

                def mixes(t, p):
                    dve.wait_ge(dif, t + 1)
                    if t >= 1:
                        dve.wait_ge(mlo, t)
                    for j, col in ((0, mk), (1, mr)):
                        for k in range(KD):
                            i = dve.scalar_tensor_tensor(whole_mix[:, j, k], d[:, k], col[:, k:k + 1], S[:, k, tok(t)], ALU.mult, ALU.add)
                    i.then_inc(mixed, 1)

                def square(t, p):
                    for m in range(MF + 1):
                        n = t * MF + m
                        if m < MF:
                            dve.wait_ge(relud, n + 1)
                            if n >= 2:
                                dve.wait_ge(klo, n - 1)
                            dve.tensor_tensor(whole[:, m % 2], relu[:, m % 2], relu[:, m % 2], ALU.mult).then_inc(squared, 1)
                        if m >= 1:
                            dve.wait_ge(squared, n)
                            dve.wait_ge(khi, n)
                            dve.tensor_tensor(kc[1][:, m - 1], whole[:, (m - 1) % 2], kc[0][:, m - 1], ALU.subtract).then_inc(klo, 1)

                def residual(t, p):
                    dve.wait_ge(tanhed, t + 1)
                    dve.wait_ge(vrdy, t + 1)
                    dve.wait_ge(xld[p], 16 * (t // 2 + 1))
                    for h in range(KD):
                        i = dve.scalar_tensor_tensor(th[:, p, h], th[:, p, h], 1.0, v_bank[h][:, :], ALU.add, ALU.mult)
                    link(i)
                    for h in range(KD):
                        i = dve.scalar_tensor_tensor(H[:, h, tok(t)], th[:, p, h], 0.5, H[:, h, tok(t)], ALU.mult, ALU.add)
                    link(i)
                    for h in range(KD):
                        i = dve.scalar_tensor_tensor(xin[:, p, h], H[:, h, tok(t)], gate[:, h:h + 1], xin[:, p, h], ALU.mult, ALU.add)
                    i.then_inc(res, 1)

                run(dve, NT, [(2, residual), (0, mixes), (0, weights_low), (1, square)])
        close()


def zero_column(nc, bufs):
    with nc.Block() as block:
        @block.vector
        def _(dve):
            for b in bufs:
                dve.memset(b[:, :, 0:1], 0.0)


def rwkv_stage(nc, G, src, dst):
    with ExitStack() as ctx:
        H = ctx.enter_context(nc.sbuf_tensor("rw_h", [P, KD, N], F32))
        S = ctx.enter_context(nc.sbuf_tensor("rw_s", [P, KD, 1 + N], F32))
        Sv = lambda k, t: S[:, k, tok(t, 1)]
        Hv = lambda k, t: H[:, k, tok(t)]
        zero_column(nc, [S])
        ln_pass(nc, G, Hv, Hv, G.eps5[:, :], G.mod[:, 0, CA:CA + KD], G.mod[:, 0, SA:SA + KD], load=load_x(G, src, H))
        ln_pass(nc, G, Hv, Sv, G.eps3[:, :], G.col("ln1_g"), G.col("ln1_b"))
        time_mix_pass(nc, G, H, S)
        ln_pass(nc, G, Hv, Sv, G.eps3[:, :], G.col("ln2_g"), G.col("ln2_b"))
        channel_mix_pass(nc, G, H, S, src, dst)


def attention_pass(nc, G, l, X, Y):
    with ExitStack() as ctx:
        sb, sem, close = open_pass(nc, G, ctx)
        wqkv = [sb(f"wqkv_{n}", [P, KD, 3 * INNER], F32R) for n in ("hi", "lo")]
        wo = sb("wo", [P, INNER // P, D])
        masks = sb("masks", [P, 3, 2 * W], BF16)
        masks32 = sb("masks32", [P, 3, 2 * W])
        identb = sb("identb", [P, P], BF16)
        scales = sb("scales", [P, 4, DH])
        rot = [sb(f"rot{i}", [P, 4, DH]) for i in range(2)]
        rots = [sb(f"rots{i}", [P, 4, DH]) for i in range(2)]
        hs = [[sb(f"hs{i}_{n}", [P, KD, W], F32R) for n in ("hi", "lo")] for i in range(4)]
        qk = [sb(f"qk{i}", [P, 2, HEADS, DH]) for i in range(2)]
        v = [sb(f"v{i}", [P, INNER]) for i in range(4)]
        sq = sb("sq", [P, 2, HEADS, DH])
        ss = [sb(f"ss{i}", [P, 2, HEADS]) for i in range(2)]
        rn = [sb(f"rn{i}", [P, 2, HEADS]) for i in range(2)]
        half = sb("half", [P, 2, HEADS])
        ra = sb("ra", [P, 2, HEADS, DH])
        rb = sb("rb", [P, 2, HEADS, DH])
        qkr = [sb(f"qkr{i}", [P, 2, INNER]) for i in range(2)]
        qT = [sb(f"qT{i}", [P, HEADS // 2, W]) for i in range(2)]
        kT = sb("kT", [P, HEADS // 2, 2, W])
        nmax = [sb(f"nmax{i}", [P, HEADS]) for i in range(2)]
        rsum = [sb(f"rsum{i}", [P, HEADS]) for i in range(2)]
        rinv = [sb(f"rinv{i}", [P, HEADS]) for i in range(2)]
        with ExitStack() as early:
            raw = early.enter_context(nc.sbuf_tensor(f"wqkv_raw{l}", [P, KD, 3 * INNER], F32))
        pr = [sb(f"pr{i}", [P, HEADS, 2, W]) for i in range(2)]
        pT = sb("pT", [P, HEADS, 2, W])
        o = [sb(f"o{i}", [P, INNER]) for i in range(2)]
        oT = sb("oT", [P, INNER // P, W])
        names = ("whi", "wlo", "hsh", "weights", "consts", "scal", "rotld0", "rotld1", "rotsc", "hsr", "projq", "projk", "projv", "qev", "kev", "vev",
                 "sqd", "ssd", "rnh", "rnd", "ram", "rbm", "rsumd", "qkrd", "trq", "trk", "qTd", "kTd", "sc", "mx", "ex",
                 "pt", "ptA", "ptV", "pv", "rid", "od", "otr", "oTd", "wod", "res", "zeroed")
        (whi, wlo, hsh, weights, consts, scal, rotld0, rotld1, rotsc, hsr, projq, projk, projv, qev, kev, vev,
         sqd, ssd, rnh, rnd, ram, rbm, rsumd, qkrd, trq, trk, qTd, kTd, sc, mx, ex,
         pt, ptA, ptV, pv, rid, od, otr, oTd, wod, res, zeroed) = (sem("a_" + n) for n in names)
        rotld = (rotld0, rotld1)
        rawld = [sem(f"a_rawld{j}") for j in range(3)]
        proj_bank, turn_bank, score_bank, value_bank = G.bank[0:2], G.bank[2:4], G.bank[4:7], G.bank[7]
        QUAD = ((0, 2), (1, 3), (4, 6), (5, 7))
        qs, ks = G.io["q_scale"], G.io["k_scale"]
        part = lambda w, j: w[:, :, j * INNER:(j + 1) * INNER]
        with nc.Block() as block:
            @block.sync
            def _(sp):
                sp.dma_start(masks32[:, :, :], G.io["masks"]).then_inc(consts, 16)
                for j, s in ((0, qs), (2, ks)):
                    row = s[l:l + 1, :]
                    sp.dma_start(scales[:, j], row.to_broadcast([P, DH])).then_inc(consts, 16)
                    for a in (0, DH // 2):
                        b = DH // 2 - a
                        sp.dma_start(scales[:, j + 1, a:a + DH // 2], row[:, b:b + DH // 2].to_broadcast([P, DH // 2])).then_inc(consts, 16)

                for j in range(3):
                    sp.dma_start(part(raw, j), part(G.io["wqkv"][l].rearrange("(k p) n -> p k n", p=P), j)).then_inc(rawld[j], 16)
                sp.dma_start(wo[:, :, :], G.io["wo"][l].rearrange("(k p) n -> p k n", p=P)).then_inc(weights, 16)

                def table(t, p):
                    if past(t, 2):
                        sp.wait_ge(rotsc, t - 1)
                    sp.dma_start(rot[p % 2][:, :, :], G.io["rotary"][t] if known(t) else G.io["rotary"][bass.ds(t, 1)].rearrange("a p j d -> p (a j) d")).then_inc(rotld[p % 2], 16)
                run(sp, NW, [(0, table)], 4)

            @block.gpsimd
            def _(pool):
                pool.wait_ge(consts, 16 * 7)

                def shift(t, p):
                    if past(t, 4):
                        pool.wait_ge(projv, t - 3)
                    pool.tensor_copy(hs[p][0][:, 0], X[:, 0, tok(t, 1, W)])
                    pool.tensor_copy(hs[p][0][:, 1], X[:, 1, tok(t, 0, W)]).then_inc(hsh, 1)

                def table(t, p):
                    pool.wait_ge(rotld[p % 2], 16 * (t // 2 + 1) if known(t) else (t - p % 2) * 8 + 16)
                    if past(t, 2):
                        pool.wait_ge(rbm, t - 1)
                    pool.tensor_tensor(rots[p % 2][:, :, :], rot[p % 2][:, :, :], scales[:, :, :], ALU.mult).then_inc(rotsc, 1)

                def norms(t, p):
                    pool.wait_ge(ssd, t + 1)
                    if past(t, 2):
                        pool.wait_ge(qkrd, t - 1)
                    pool.tensor_tensor(rn[p % 2][:, :, :], ss[p % 2][:, :, :], half[:, :, :], ALU.pow).then_inc(rnd, 1)

                def add(t, p):
                    pool.wait_ge(ram, t + 1)
                    pool.wait_ge(rbm, t + 1)
                    pool.tensor_tensor(ra[:, :, :, :], ra[:, :, :, :], rb[:, :, :, :], ALU.add).then_inc(rsumd, 1)

                pool.wait_ge(zeroed, 1)
                run(pool, NW, [(0, shift), (1, table), (2, add), (2, norms)], 4)

            @block.tensor
            def _(pe):
                pe.wait_ge(weights, 16)
                pe.wait_ge(zeroed, 1)

                def product(t, p, j, bank, done):
                    if known(t) and t == 0:
                        pe.wait_ge(wlo, j + 1)
                    product_of_parts(pe, proj_bank[bank][:, :], lambda a, k: hs[p][a][:, k], lambda b, k: wqkv[b][:, k, j * INNER:(j + 1) * INNER],
                                     range(KD), KD).then_inc(done, 1)

                def project_q(t, p):
                    pe.wait_ge(hsr, t + 1)
                    if past(t, 1):
                        pe.wait_ge(qev, t)
                    product(t, p, 0, 0, projq)

                def project_k(t, p):
                    if past(t, 1):
                        pe.wait_ge(vev, t)
                    product(t, p, 1, 1, projk)

                def project_v(t, p):
                    pe.wait_ge(kev, t + 1)
                    product(t, p, 2, 1, projv)

                def turn_qk(t, p):
                    pe.wait_ge(qkrd, t + 1)
                    if past(t, 3):
                        pe.wait_ge(oTd, t - 2)
                        pe.wait_ge(res, t - 2)
                    elif t == 2:
                        pe.wait_ge(ptA, 2 * (t - 1))
                        pe.wait_ge(ptV, 2 * (t - 1))
                    elif t == 1:
                        pe.wait_ge(qTd, t)
                        pe.wait_ge(kTd, t)
                    for j, done in ((0, trq), (1, trk)):
                        for c in range(HEADS // 2):
                            mm = pe.transpose(turn_bank[j][:, c * W:(c + 1) * W], qkr[p % 2][:, j, c * P:(c + 1) * P], G.ident[:, :])
                        mm.then_inc(done, 1)

                def scores(t, p):
                    pe.wait_ge(qTd, t + 1)
                    pe.wait_ge(kTd, t + 1)
                    which = 2 if known(t) and t == 0 else p % 2
                    for i, heads in enumerate(QUAD):
                        bank = i % 3
                        if i == 3:
                            pe.wait_ge(ex, 4 * t + 1)
                        elif past(t, 1):
                            pe.wait_ge(ex, 4 * t - 2 + i if i else 4 * t)
                        for a, h in enumerate(heads):
                            r = slice(DH * (h % 2), DH * (h % 2) + DH)
                            out = score_bank[bank][:, a * 2 * W:(a + 1) * 2 * W]
                            pe.matmul(out, qT[p % 2][r, h // 2], kT[r, h // 2].rearrange("p s w -> p (s w)"), start=True, stop=False)
                            mm = pe.matmul(out, identb[:, :], masks[:, which], start=False, stop=True)
                        mm.then_inc(sc, 1)

                def turn_p(halves):
                    def turn(t, p):
                        pe.wait_ge(ex, 4 * t + 4)
                        for i in halves:
                            if i < 2:
                                n = min(t + 2, NW) if known(t) else t + 2
                                pe.wait_ge((qTd, kTd)[i], n)
                                if known(t) and t + 1 >= NW:
                                    pe.wait_ge((oTd, res)[i], t - 1)
                            else:
                                pe.wait_ge((ptA, ptV)[i % 2], 2 * t + 1)
                            for a in range(4):
                                h, s = 2 * i + a // 2, a % 2
                                mm = pe.transpose(turn_bank[i % 2][:, a * W:(a + 1) * W], pr[p % 2][:, h, s], G.ident[:, :])
                            mm.then_inc(pt, 1)
                    return turn

                def values(t, p):
                    pe.wait_ge(ptA, 2 * t + 2)
                    pe.wait_ge(ptV, 2 * t + 2)
                    pe.wait_ge(vev, t + 1)
                    if past(t, 1):
                        pe.wait_ge(od, t)
                    for h in range(HEADS):
                        for s in range(2):
                            vw = v[p] if s == p % 2 else v[(p - 1) % 4]
                            mm = pe.matmul(value_bank[:, h * DH:(h + 1) * DH], pT[:, h, s], vw[:, h * DH:(h + 1) * DH], start=(s == 0), stop=(s == 1))
                    mm.then_inc(pv, 1)

                def turn_o(t, p):
                    pe.wait_ge(od, t + 1)
                    pe.wait_ge(ptA, min(2 * t + 4, 2 * NW) if known(t) else 2 * t + 4)
                    for c in range(INNER // P):
                        mm = pe.transpose(turn_bank[0][:, c * W:(c + 1) * W], o[p % 2][:, c * P:(c + 1) * P], G.ident[:, :])
                    mm.then_inc(otr, 1)

                def outproj(t, p):
                    pe.wait_ge(oTd, t + 1)
                    pe.wait_ge(ptV, min(2 * t + 4, 2 * NW) if known(t) else 2 * t + 4)
                    for m in range(KD):
                        for k in range(INNER // P):
                            mm = pe.matmul(turn_bank[1][:, m * W:(m + 1) * W], wo[:, k, m * P:(m + 1) * P], oT[:, k], start=(k == 0), stop=(k == INNER // P - 1))
                    mm.then_inc(wod, 1)

                run(pe, NW, [(5, turn_p((0, 1))), (2, project_v), (5, turn_p((2, 3))), (1, project_q), (6, turn_o), (4, scores), (6, outproj), (5, values),
                             (3, turn_qk), (1, project_k)], 4)

            @block.scalar
            def _(act):
                def turned_p(t, p):
                    if past(t, 1):
                        act.wait_ge(pv, t)
                    for i in (0, 2):
                        act.wait_ge(pt, 4 * t + i + 1)
                        act.activation(pT[:, 2 * i:2 * i + 2].rearrange("p h s w -> p (h s w)"), turn_bank[0][:, :], ACT.Copy).then_inc(ptA, 1)

                def exponentials(t, p):
                    if past(t, 2):
                        act.wait_ge(pt, 4 * (t - 1))
                        act.wait_ge(rid, t - 1)
                    for i, heads in enumerate(QUAD):
                        act.wait_ge(mx, 4 * t + i + 1)
                        for a, h in enumerate(heads):
                            e = act.activation(pr[p % 2][:, h].rearrange("p s w -> p (s w)"), score_bank[i % 3][:, a * 2 * W:(a + 1) * 2 * W],
                                               ACT.Exp, bias=nmax[p % 2][:, h:h + 1], accum_out=rsum[p % 2][:, h:h + 1])
                        e.then_inc(ex, 1)

                def turned_o(t, p):
                    act.wait_ge(otr, t + 1)
                    if past(t, 1):
                        act.wait_ge(wod, t)
                    act.activation(oT[:, :, :].rearrange("p k w -> p (k w)"), turn_bank[0][:, :], ACT.Copy).then_inc(oTd, 1)

                def turned_q(t, p):
                    act.wait_ge(trq, t + 1)
                    if past(t, 2):
                        act.wait_ge(sc, 4 * (t - 1))
                    act.activation(qT[p % 2][:, :, :].rearrange("p c w -> p (c w)"), turn_bank[0][:, :], ACT.Copy).then_inc(qTd, 1)

                def projected_q(t, p):
                    if past(t, 2):
                        act.wait_ge(rbm, t - 1)
                        act.wait_ge(ram, t - 1)
                    act.wait_ge(projq, t + 1)
                    act.activation(qk[p % 2][:, 0].rearrange("p h d -> p (h d)"), proj_bank[0][:, :], ACT.Copy).then_inc(qev, 1)

                def projected_k(t, p):
                    act.wait_ge(projk, t + 1)
                    act.activation(qk[p % 2][:, 1].rearrange("p h d -> p (h d)"), proj_bank[1][:, :], ACT.Copy).then_inc(kev, 1)

                def square(t, p):
                    act.wait_ge(kev, t + 1)
                    if past(t, 1):
                        act.wait_ge(rnh, t)
                    act.activation(sq[:, :, :, :], qk[p % 2][:, :, :, :], ACT.Square).then_inc(sqd, 1)

                def projected_v(t, p):
                    act.wait_ge(projv, t + 1)
                    if past(t, 3):
                        act.wait_ge(pv, t - 2)
                    act.activation(v[p][:, :], proj_bank[1][:, :], ACT.Copy).then_inc(vev, 1)

                for j in range(3):
                    act.wait_ge(rawld[j], 16)
                    act.activation(part(wqkv[0], j), part(raw, j), ACT.Copy).then_inc(whi, 1)
                act.wait_ge(zeroed, 1)
                run(act, NW, [(5, turned_p), (1, projected_q), (2, square), (6, turned_o), (4, exponentials), (2, projected_v), (3, turned_q), (1, projected_k)], 4)

            @block.vector
            def _(dve):
                dve.wait_ge(consts, 16 * 7)
                dve.tensor_copy(masks[:, :, :], masks32[:, :, :])
                dve.tensor_copy(identb[:, :], G.ident[:, :])
                dve.memset(half[:, :, :], -0.5)
                dve.memset(kT[:, :, :, :], 0.0)
                dve.memset(v[3][:, :], 0.0)
                dve.memset(Y[:, :, 0:1], 0.0).then_inc(zeroed, 1)

                def weights_low(t, p):
                    if known(t) and t == 0:
                        for j in range(3):
                            dve.wait_ge(whi, j + 1)
                            dve.tensor_tensor(part(wqkv[1], j), part(raw, j), part(wqkv[0], j), ALU.subtract).then_inc(wlo, 1)

                def turned_p(t, p):
                    if past(t, 1):
                        dve.wait_ge(pv, t)
                    for i in (1, 3):
                        dve.wait_ge(pt, 4 * t + i + 1)
                        dve.tensor_copy(pT[:, 2 * i:2 * i + 2].rearrange("p h s w -> p (h s w)"), turn_bank[1][:, :]).then_inc(ptV, 1)

                def maxima(t, p):
                    for i, heads in enumerate(QUAD):
                        dve.wait_ge(sc, 4 * t + i + 1)
                        dve.tensor_reduce(nmax[p % 2][:, heads[0]:heads[1] + 1:2], score_bank[i % 3][:, :].rearrange("p (h k) -> p h k", h=2),
                                          AX.X, ALU.max, negate=True).then_inc(mx, 1)

                def inverse(t, p):
                    dve.wait_ge(ex, 4 * t + 4)
                    if past(t, 2):
                        dve.wait_ge(od, t - 1)
                    dve.reciprocal(rinv[p % 2][:, :], rsum[p % 2][:, :]).then_inc(rid, 1)

                def normalise(t, p):
                    dve.wait_ge(pv, t + 1)
                    dve.wait_ge(rid, t + 1)
                    if past(t, 2):
                        dve.wait_ge(otr, t - 1)
                    dve.tensor_tensor(o[p % 2][:, :].rearrange("p (h d) -> p h d", h=HEADS), value_bank[:, :].rearrange("p (h d) -> p h d", h=HEADS),
                                      rinv[p % 2][:, :].unsqueeze(2).to_broadcast([P, HEADS, DH]), ALU.mult).then_inc(od, 1)

                def residual(t, p):
                    dve.wait_ge(wod, t + 1)
                    dve.tensor_tensor(Y[:, :, tok(t, 1, W)], turn_bank[1][:, 0:KD * W].rearrange("p (k w) -> p k w", k=KD),
                                      X[:, :, tok(t, 1, W)], ALU.add).then_inc(res, 1)

                def turned_k(t, p):
                    dve.wait_ge(trk, t + 1)
                    if past(t, 1):
                        dve.wait_ge(sc, 4 * t)
                    dve.tensor_copy(kT[:, :, p % 2], turn_bank[1][:, :].rearrange("p (c w) -> p c w", w=W)).then_inc(kTd, 1)

                def shifted_low(t, p):
                    dve.wait_ge(hsh, t + 1)
                    if past(t, 4):
                        dve.wait_ge(projv, t - 3)
                    dve.tensor_tensor(hs[p][1][:, 0], X[:, 0, tok(t, 1, W)], hs[p][0][:, 0], ALU.subtract)
                    dve.tensor_tensor(hs[p][1][:, 1], X[:, 1, tok(t, 0, W)], hs[p][0][:, 1], ALU.subtract).then_inc(hsr, 1)

                def squares(t, p):
                    dve.wait_ge(sqd, t + 1)
                    if past(t, 2):
                        dve.wait_ge(rnd, t - 1)
                    dve.tensor_reduce(ss[p % 2][:, :, :], sq[:, :, :, :], AX.X, ALU.add).then_inc(rnh, 1)

                def clip(t, p):
                    dve.wait_ge(rnh, t + 1)
                    dve.tensor_scalar(ss[p % 2][:, :, :], ss[p % 2][:, :, :], 1e-24, None, ALU.max).then_inc(ssd, 1)

                def rotate(t, p):
                    q = qk[p % 2]
                    tab = rots[p % 2]
                    dve.wait_ge(kev, t + 1)
                    dve.wait_ge(rotsc, t + 1)
                    if past(t, 1):
                        dve.wait_ge(qkrd, t)
                    for j in range(2):
                        cos = tab[:, 2 * j].unsqueeze(1).to_broadcast([P, HEADS, DH])
                        i = dve.tensor_tensor(ra[:, j], q[:, j], cos, ALU.mult)
                    i.then_inc(ram, 1)
                    H2 = DH // 2
                    for j in range(2):
                        for a in (0, H2):
                            b = H2 - a
                            sin = tab[:, 2 * j + 1, a:a + H2].unsqueeze(1).to_broadcast([P, HEADS, H2])
                            i = dve.tensor_tensor(rb[:, j, :, a:a + H2], q[:, j, :, b:b + H2], sin, ALU.mult)
                    i.then_inc(rbm, 1)

                def scale(t, p):
                    dve.wait_ge(rsumd, t + 1)
                    dve.wait_ge(rnd, t + 1)
                    if past(t, 2):
                        dve.wait_ge(trk, t - 1)
                    dve.tensor_tensor(qkr[p % 2][:, :, :].rearrange("p j (h d) -> p (j h) d", h=HEADS), ra[:, :, :, :].rearrange("p j h d -> p (j h) d"),
                                      rn[p % 2][:, :, :].rearrange("p j h -> p (j h)").unsqueeze(2).to_broadcast([P, 2 * HEADS, DH]), ALU.mult).then_inc(qkrd, 1)

                run(dve, NW, [(5, turned_p), (4, maxima), (3, scale), (2, squares), (6, residual), (2, rotate), (4, inverse), (5, normalise), (3, turned_k), (0, shifted_low), (0, weights_low), (2, clip)], 4)
        close()


def gated_mlp_pass(nc, G, l, S, X, finish=None):
    HP = HK * P
    with ExitStack() as ctx:
        sb, sem, close = open_pass(nc, G, ctx)
        w1 = [sb(f"mlp_w1_{n}", [P, KD, 2, HP], F32R) for n in ("hi", "lo")]
        w2 = [sb(f"mlp_w2_{n}", [P, HK, D], F32R) for n in ("hi", "lo")]
        s = [sb(f"mlp_s_{n}", [P, 2, KD, TT], F32R) for n in ("hi", "lo")]
        gel = sb("mlp_gel", [P, 2, TT])
        whole = sb("mlp_whole", [P, 2, TT])
        xin = sb("mlp_x", [P, 2, KD, TT])
        with ExitStack() as early:
            raw1 = early.enter_context(nc.sbuf_tensor(f"mlp_raw1_{l}", [P, KD, 2, HP], F32))
            raw2 = early.enter_context(nc.sbuf_tensor(f"mlp_raw2_{l}", [P, HK, D], F32))
        hid = [sb(f"mlp_hid_{n}", [P, 2, HK, TT], F32R) for n in ("hi", "lo")]
        cleared, weights1, weights2, whi, wlo, shi, slo, ad, gd, geld, wholed, hidd, w2d, res, xl0, xl1, stored, link_s = (
            sem("m_" + n) for n in ("cleared", "weights1", "weights2", "whi", "wlo", "shi", "slo", "ad", "gd", "geld", "wholed", "hidd", "w2d", "res",
                                    "xl0", "xl1", "stored", "l"))
        xl = (xl0, xl1)
        up_bank, out_bank = G.bank[0:6], G.bank[6:8]
        b1a, b1g, b2 = G.col(f"f_b1a{l}"), G.col(f"f_b1g{l}"), G.col(f"f_b2{l}")
        size = [P] * (HK - 1) + [HLAST]
        if finish:
            xs, xd = (G.io[n].rearrange("(k p) n -> p k n", p=P) for n in finish[0:2])
        with nc.Block() as block:
            @block.sync
            def _(sp):
                sp.wait_ge(cleared, 1)
                for j in range(2):
                    sp.dma_start(raw1[:, :, j, 0:HID], G.io["w1"][l, :, j * HID:(j + 1) * HID].rearrange("(k p) n -> p k n", p=P)).then_inc(weights1, 16)
                sp.wait_ge(cleared, 2)
                sp.dma_start(raw2[:, 0:HK - 1], G.io["w2"][l, 0:(HK - 1) * P].rearrange("(k p) n -> p k n", p=P)).then_inc(weights2, 16)
                sp.dma_start(raw2[0:HLAST, HK - 1], G.io["w2"][l, (HK - 1) * P:HID]).then_inc(weights2, 16)
                if finish:
                    for t in range(NT + 2):
                        if t >= 2:
                            sp.wait_ge(res, t - 1)
                            sp.dma_start(xd[:, :, tok(t - 2)], xin[:, t % 2]).then_inc(stored, 16)
                            sp.wait_ge(stored, 16 * (t - 1))
                        if t < NT:
                            sp.dma_start(xin[:, t % 2], xs[:, :, tok(t)]).then_inc(xl[t % 2], 16)

            @block.gpsimd
            def _(pool):
                pool.memset(raw1[:, :, :, HID:HP], 0.0).then_inc(cleared, 1)
                pool.memset(raw2[:, HK - 1], 0.0).then_inc(cleared, 1)

                def split(t, p):
                    if past(t, 2):
                        pool.wait_ge(ad, (t - 1) * HK)
                    for k in range(KD):
                        i = pool.tensor_copy(s[0][:, p, k], S(k, t))
                    i.then_inc(shi, 1)
                    pool.wait_ge(shi, t + 1)
                    for k in range(KD):
                        i = pool.tensor_tensor(s[1][:, p, k], S(k, t), s[0][:, p, k], ALU.subtract)
                    i.then_inc(slo, 1)
                run(pool, NT, [(0, split)])

            @block.tensor
            def _(pe):
                def up(t, p):
                    if t == 0:
                        pe.wait_ge(wlo, 1)
                    pe.wait_ge(slo, t + 1)
                    for m in range(HK):
                        n = t * HK + m
                        if past(n, 3):
                            pe.wait_ge(wholed, n - 2)
                        for j, done in ((1, gd), (0, ad)):
                            product_of_parts(pe, up_bank[2 * (m % 3) + j][:, :], lambda a, k: w1[a][:, k, j, m * P:(m + 1) * P],
                                             lambda b, k: s[b][:, p, k], range(KD), KD).then_inc(done, 1)

                def down(t, p):
                    if t == 0:
                        pe.wait_ge(wlo, 2)
                    pe.wait_ge(hidd, (t + 1) * HK)
                    if past(t, 1):
                        pe.wait_ge(res, t)
                    for m in range(KD):
                        mm = product_of_parts(pe, out_bank[m][:, :], lambda a, k: w2[a][0:size[k], k, m * P:(m + 1) * P],
                                              lambda b, k: hid[b][0:size[k], p, k], range(HK), HK)
                    mm.then_inc(w2d, 1)
                run(pe, NT, [(0, up), (1, down)])

            @block.scalar
            def _(act):
                for raw, w, loaded in ((raw1, w1, weights1), (raw2, w2, weights2)):
                    act.wait_ge(loaded, 32)
                    act.activation(w[0][:], raw[:], ACT.Copy).then_inc(whi, 1)

                def gelu(t, p):
                    for m in range(HK):
                        n = t * HK + m
                        act.wait_ge(gd, n + 1)
                        if past(n, 2):
                            act.wait_ge(wholed, n - 1)
                        act.activation(gel[:, m % 2], up_bank[2 * (m % 3) + 1][:, :], ACT.Gelu, bias=b1g[:, m:m + 1]).then_inc(geld, 1)
                run(act, NT, [(0, gelu)])

            @block.vector
            def _(dve):
                link = chain(dve, link_s)
                for i, (raw, w) in enumerate(((raw1, w1), (raw2, w2))):
                    dve.wait_ge(whi, i + 1)
                    dve.tensor_tensor(w[1][:], raw[:], w[0][:], ALU.subtract).then_inc(wlo, 1)

                def gate(t, p):
                    if past(t, 2):
                        dve.wait_ge(w2d, t - 1)
                    elif t == 0:
                        dve.wait_ge(wlo, 2)
                    for m in range(HK + 1):
                        n = t * HK + m
                        if m < HK:
                            dve.wait_ge(ad, n + 1)
                            dve.wait_ge(geld, n + 1)
                            if past(n, 2):
                                dve.wait_ge(hidd, n - 1)
                            for out in (hid[0][:, p, m], whole[:, m % 2]):
                                i = dve.scalar_tensor_tensor(out, up_bank[2 * (m % 3)][:, :], b1a[:, m:m + 1], gel[:, m % 2], ALU.add, ALU.mult)
                            i.then_inc(wholed, 1)
                        if m >= 1:
                            dve.wait_ge(wholed, n)
                            dve.tensor_tensor(hid[1][:, p, m - 1], whole[:, (m - 1) % 2], hid[0][:, p, m - 1], ALU.subtract).then_inc(hidd, 1)

                def residual(t, p):
                    dve.wait_ge(w2d, t + 1)
                    for h in range(KD):
                        i = dve.scalar_tensor_tensor(X(h, t), out_bank[h][:, :], b2[:, h:h + 1], X(h, t), ALU.add, ALU.add)
                        if finish:
                            link(i)
                    if finish:
                        dve.wait_ge(xl[p], 16 * (t // 2 + 1))
                        for h in range(KD):
                            i = dve.scalar_tensor_tensor(xin[:, p, h], X(h, t), finish[2][:, h:h + 1], xin[:, p, h], ALU.mult, ALU.add)
                    i.then_inc(res, 1)
                run(dve, NT, [(0, gate), (1, residual)])
        close()


def local_attention_stage(nc, G, src, dst):
    def plain(Z):
        return lambda k, t: Z[:, k, tok(t, 1)]

    def shifted(Z):
        return lambda k, t: Z[:, k, tok(t, 1 - k)]

    with ExitStack() as ctx:
        A, B = (ctx.enter_context(nc.sbuf_tensor(f"la_{n}", [P, KD, 1 + N], F32)) for n in "ab")
        zero_column(nc, [A])
        ln_pass(nc, G, plain(A), plain(A), G.eps5[:, :], G.mod[:, 0, CB:CB + KD], G.mod[:, 0, SB:SB + KD],
                load=load_x(G, src, A[:, :, 1:1 + N]))
        for l in range(DEPTH):
            attention_pass(nc, G, l, A, B)
            ln_pass(nc, G, shifted(B), plain(A), G.eps5[:, :], G.col(f"f_ln_g{l}"), G.col(f"f_ln_b{l}"))
            gated_mlp_pass(nc, G, l, plain(A), plain(B), (src, dst, G.mod[:, 0, GB:GB + KD]) if l == DEPTH - 1 else None)
            A, B = B, A


class S4dParams:
    K = NL * HQ

    def __init__(self, nc, G, ctx):
        self.G = G
        self.prm = [ctx.enter_context(nc.sbuf_tensor("s_" + n, [P, self.K], F32)) for n in ("turns", "rate", "cre", "cim", "ncre")]

    def open(self, sb, sem):
        names = ("dt", "ar", "ai", "cr", "ci", "e1", "s", "c", "a", "b", "q", "r", "den")
        self.buf = [sb(n, [P, self.K]) for n in names]
        self.zeros = sb("zeros", [Q4, HQ, C])
        self.sems = [sem("p_" + n) for n in ("loaded", "cleared", "stored", "dv", "ac")]

    def sync(self, sp):
        G = self.G
        dt, ar, ai, cr, ci = self.buf[0:5]
        zeros, (loaded, cleared, stored) = self.zeros, self.sems[0:3]
        for n, t in (("s_log_dt", dt), ("s_A_re_log", ar), ("s_A_im", ai), ("s_C_re", cr), ("s_C_im", ci)):
            sp.dma_start(t[:, :], G.io[n].rearrange("p l q -> p (l q)")).then_inc(loaded, 16)
        sp.wait_ge(cleared, 1)
        sp.dma_start(G.io["taps"][:, :, 0:C].rearrange("q a j -> a q j"), zeros[:, :, :]).then_inc(stored, 16)
        sp.wait_ge(stored, 16)

    def scalar(self, act):
        G = self.G
        dt, ar, ai, cr, ci, e1, s, c, a, b, q, r, den = self.buf
        loaded, cleared, stored, dv, ac = self.sems
        turns, rate, cre, cim, ncre = (x[:, :] for x in self.prm)
        act.wait_ge(loaded, 80)
        act.activation(dt[:, :], dt[:, :], ACT.Exp).then_inc(ac, 1)
        act.activation(ar[:, :], ar[:, :], ACT.Exp).then_inc(ac, 1)
        act.wait_ge(dv, 4)
        act.activation(e1[:, :], rate, ACT.Tanh, scale=0.5).then_inc(ac, 1)
        act.wait_ge(dv, 8)
        act.activation(s[:, :], turns, ACT.Sin, scale=PI).then_inc(ac, 1)
        act.activation(c[:, :], a[:, :], ACT.Sin, scale=-PI, bias=G.half_pi[:, :]).then_inc(ac, 1)

    def vector(self, dve):
        dt, ar, ai, cr, ci, e1, s, c, a, b, q, r, den = self.buf
        loaded, cleared, stored, dv, ac = self.sems
        turns, rate, cre, cim, ncre = (x[:, :] for x in self.prm)
        link = chain(dve, dv)
        dve.wait_ge(ac, 2)
        link(dve.tensor_scalar(ar[:, :], ar[:, :], -1.0, None, ALU.mult))
        link(dve.tensor_tensor(rate, ar[:, :], dt[:, :], ALU.mult))
        link(dve.tensor_tensor(b[:, :], ai[:, :], dt[:, :], ALU.mult))
        link(dve.tensor_scalar(b[:, :], b[:, :], 1.0 / 6.283185307179586, None, ALU.mult))
        link(dve.tensor_scalar(q[:, :], b[:, :], MAGIC, None, ALU.add))
        link(dve.tensor_scalar(q[:, :], q[:, :], MAGIC, None, ALU.subtract))
        link(dve.tensor_tensor(turns, b[:, :], q[:, :], ALU.subtract))
        link(dve.scalar_tensor_tensor(a[:, :], turns, -1.0, turns, ALU.mult, ALU.max))
        dve.wait_ge(ac, 3)
        link(dve.tensor_scalar(q[:, :], e1[:, :], -1.0, 1.0, ALU.mult, ALU.add))
        link(dve.reciprocal(q[:, :], q[:, :]))
        link(dve.scalar_tensor_tensor(e1[:, :], e1[:, :], 2.0, q[:, :], ALU.mult, ALU.mult))
        dve.wait_ge(ac, 5)
        link(dve.scalar_tensor_tensor(a[:, :], s[:, :], 2.0, s[:, :], ALU.mult, ALU.mult))
        link(dve.scalar_tensor_tensor(b[:, :], s[:, :], 2.0, c[:, :], ALU.mult, ALU.mult))
        link(dve.tensor_tensor(q[:, :], e1[:, :], a[:, :], ALU.mult))
        link(dve.tensor_tensor(q[:, :], e1[:, :], q[:, :], ALU.subtract))
        link(dve.tensor_tensor(q[:, :], q[:, :], a[:, :], ALU.subtract))
        link(dve.scalar_tensor_tensor(r[:, :], e1[:, :], 1.0, b[:, :], ALU.add, ALU.mult))
        link(dve.tensor_tensor(a[:, :], ar[:, :], ar[:, :], ALU.mult))
        link(dve.tensor_tensor(b[:, :], ai[:, :], ai[:, :], ALU.mult))
        link(dve.tensor_tensor(den[:, :], a[:, :], b[:, :], ALU.add))
        link(dve.reciprocal(den[:, :], den[:, :]))
        link(dve.tensor_tensor(a[:, :], q[:, :], ar[:, :], ALU.mult))
        link(dve.tensor_tensor(b[:, :], r[:, :], ai[:, :], ALU.mult))
        link(dve.tensor_tensor(a[:, :], a[:, :], b[:, :], ALU.add))
        link(dve.tensor_tensor(b[:, :], r[:, :], ar[:, :], ALU.mult))
        link(dve.tensor_tensor(q[:, :], q[:, :], ai[:, :], ALU.mult))
        link(dve.tensor_tensor(b[:, :], b[:, :], q[:, :], ALU.subtract))
        link(dve.scalar_tensor_tensor(a[:, :], a[:, :], 2.0, den[:, :], ALU.mult, ALU.mult))
        link(dve.scalar_tensor_tensor(b[:, :], b[:, :], 2.0, den[:, :], ALU.mult, ALU.mult))
        link(dve.tensor_tensor(q[:, :], cr[:, :], a[:, :], ALU.mult))
        link(dve.tensor_tensor(r[:, :], ci[:, :], b[:, :], ALU.mult))
        link(dve.tensor_tensor(cre, q[:, :], r[:, :], ALU.subtract))
        link(dve.tensor_tensor(q[:, :], cr[:, :], b[:, :], ALU.mult))
        link(dve.tensor_tensor(r[:, :], ci[:, :], a[:, :], ALU.mult))
        link(dve.tensor_tensor(cim, q[:, :], r[:, :], ALU.add))
        link(dve.tensor_scalar(ncre, cre, -1.0, None, ALU.mult))

    def gpsimd(self, pool):
        zeros, cleared = self.zeros, self.sems[1]
        pool.memset(zeros[:, :, :], 0.0).then_inc(cleared, 1)


def convolution_pass(nc, G, l, prm, Zr, Y):
    TW = C + 1 + NC
    S = GQ * NC
    with ExitStack() as ctx:
        sb, sem, close = open_pass(nc, G, ctx)
        ramp, quads = sb("ramp", [P, C + 1]), sb("quads", [P, Q4])
        skip = sb("skip", [Q4, HQ])
        ph, rd = sb("ph", [P, GQ, TW]), sb("rd", [P, GQ, TW])
        g128 = sb("g128", [P, HQ])
        g128r = sb("g128r", [P, HQ])
        r128 = sb("r128", [P, HQ])
        ex, sn, cs = ([sb(f"{n}{i}", [P, GQ, TW]) for i in range(3)] for n in ("ex", "sn", "cs"))
        er = sb("er", [P, 2, GQ, C + 1])
        tv = sb("tv", [P, 2, GQ, C])
        tp = sb("tp", [P, 2, GQ, C])
        gm = [sb(f"gm{i}", [P, 2, GQ, C]) for i in range(3)]
        bt = [sb(f"bt{i}", [P, 2, GQ, P]) for i in range(2)]
        krow = [sb(f"krow{i}", [Q4, GQ, C]) for i in range(2)]
        toep = [sb(f"toep{i}", [P, GC, C]) for i in range(2)]
        w = sb("w", [P, 4, GQ, NC])
        uh = sb("uh", [P, 2, GQ, NC])
        sh = sb("sh", [P, 2, GQ, NC])
        sw = sb("sw", [P, 4, GQ, NC])
        yst = [sb(f"yst{i}", [P, GQ, C]) for i in range(2)]
        st = [sb(f"st{i}", [P, 2, GQ, Q4, NC]) for i in range(2)]
        names = ("consts", "phd", "absd", "kcopied", "exh", "trig", "erd", "gmV", "gmP", "taps", "kr", "ks0", "ks1", "tl0", "tl1", "btr", "btA", "btV",
                 "ud", "uread", "scand", "stV", "stP", "yd", "gel", "out0", "out1", "lv", "lp", "decd")
        (consts, phd, absd, kcopied, exh, trig, erd, gmV, gmP, taps, kr, ks0, ks1, tl0, tl1, btr, btA, btV,
         ud, uread, scand, stV, stP, yd, gel, out0, out1, lv, lp, decd) = (sem("c_" + n) for n in names)
        ks, tl, out = (ks0, ks1), (tl0, tl1), (out0, out1)
        turns, rate, cre, cim, ncre = (x[:, l * HQ:(l + 1) * HQ] for x in prm)
        taps_bank, b_bank, u_bank, y_bank = G.bank[0], G.bank[1:3], G.bank[3:5], G.bank[5:7]
        tap_rows = G.io["taps"]
        qs = lambda g: slice(g * GQ, (g + 1) * GQ)
        bc = lambda v, g, n: v[:, qs(g)].unsqueeze(2).to_broadcast([P, GQ, n])
        rc = lambda v, n: v.unsqueeze(1).to_broadcast([P, GQ, n])
        with nc.Block() as block:
            @block.sync
            def _(sp):
                sp.dma_start(ramp[:, :], G.io["ramp"]).then_inc(consts, 16)
                sp.dma_start(quads[:, :], G.io["quads"]).then_inc(consts, 16)
                sp.dma_start(skip[:, :], G.io["s_D"][:, l, :]).then_inc(consts, 16)

                def store(g, p):
                    sp.wait_ge(kr, g + 1)
                    sp.dma_start(tap_rows[qs(g), :, C:2 * C].rearrange("q a j -> a q j"), krow[g % 2][:, :, :]).then_inc(ks[g % 2], 16)

                def load(g, p):
                    sp.wait_ge(ks[g % 2], 16 * (g // 2 + 1))
                    if past(g, 2):
                        sp.wait_ge(yd, g - 1)
                    at = tap_rows[g * GQ:g * GQ + 1, 0:1, 1:2]
                    src = bass.AP(tensor=at.tensor, offset=at.offset, ap=[[1, P], [2 * C, GC], [1, C]])
                    sp.dma_start(toep[g % 2][:, :, :], src).then_inc(tl[g % 2], 16)

                def place(g, p):
                    sp.wait_ge(gel, g + 1)
                    for q in range(GQ):
                        h = (g * GQ + q) * Q4
                        sp.dma_start(Y[h % P:h % P + Q4, h // P].rearrange("a (c j) -> a c j", j=C), yst[g % 2][:, q]).then_inc(out[g % 2], 16)
                run(sp, NG, [(0, store), (0, load), (2, place)], 2)
                for i in range(2):
                    sp.wait_ge(out[i], 16 * GQ * (NG // 2))

            @block.gpsimd
            def _(pool):
                link = chain(pool, lp)
                pool.wait_ge(consts, 48)
                pool.wait_ge(decd, 1)

                def exponents(g, p):
                    r = g % 3
                    if past(g, 3):
                        pool.wait_ge(stV, g - 2)
                        pool.wait_ge(stP, g - 2)
                    pool.tensor_tensor(ex[r][:, :, 0:C + 1], bc(rate, g, C + 1), rc(ramp[:, :], C + 1), ALU.mult)
                    pool.tensor_copy(ex[r][:, :, C + 1:TW], bc(r128, g, NC)).then_inc(exh, 1)

                def imaginary(g, p):
                    if past(g, 3):
                        pool.wait_ge(yd, g - 2)
                    pool.wait_ge(erd, g + 1)
                    pool.tensor_tensor(tp[:, 0], er[:, 1, :, 0:C], bc(ncre, g, C), ALU.mult)
                    link(pool.tensor_tensor(tp[:, 1], er[:, 0, :, 0:C], bc(cim, g, C), ALU.mult))
                    pool.tensor_tensor(gm[g % 3][:, 1], tp[:, 0], tp[:, 1], ALU.subtract).then_inc(gmP, 1)

                def state_im(g, p):
                    pool.wait_ge(scand, g + 1)
                    if past(g, 2):
                        pool.wait_ge(yd, g - 1)
                    R = slice(C + 1, TW)
                    pool.tensor_tensor(sw[:, 2], cs[g % 3][:, :, R], sh[:, 1], ALU.mult)
                    link(pool.tensor_tensor(sw[:, 3], sn[g % 3][:, :, R], sh[:, 0], ALU.mult))
                    link(pool.tensor_tensor(sw[:, 2], sw[:, 2], sw[:, 3], ALU.add))
                    pool.tensor_tensor(st[g % 2][:, 1], sw[:, 2].unsqueeze(2).to_broadcast([P, GQ, Q4, NC]),
                                       quads[:, :].unsqueeze(1).unsqueeze(3).to_broadcast([P, GQ, Q4, NC]), ALU.mult).then_inc(stP, 1)

                run(pool, NG, [(0, exponents), (1, imaginary), (2, state_im)], 2)

            @block.scalar
            def _(act):
                def trigonometry(g, p):
                    r = g % 3
                    act.wait_ge(phd, g + 1)
                    if past(g, 3):
                        act.wait_ge(stP, g - 2)
                    act.activation(cs[r][:, :, :], sn[r][:, :, :], ACT.Abs).then_inc(absd, 1)
                    act.wait_ge(absd, g + 1)
                    act.activation(sn[r][:, :, :], sn[r][:, :, :], ACT.Sin, scale=TWO_PI)
                    act.activation(cs[r][:, :, :], cs[r][:, :, :], ACT.Sin, scale=-TWO_PI, bias=G.half_pi[:, :])
                    act.wait_ge(exh, g + 1)
                    act.activation(ex[r][:, :, :], ex[r][:, :, :], ACT.Exp).then_inc(trig, 1)

                def inputs(g, p):
                    act.wait_ge(taps, g + 1)
                    if past(g, 2):
                        act.wait_ge(ks[g % 2], 16 * (g // 2))
                    act.activation(krow[g % 2][:, :, :].rearrange("p q j -> p (q j)"), taps_bank[0:Q4, :], ACT.Copy).then_inc(kcopied, 1)
                    act.wait_ge(btr, 2 * g + 1)
                    if past(g, 2):
                        act.wait_ge(ud, g - 1)
                    act.activation(bt[g % 2][:, 0].rearrange("p q m -> p (q m)"), b_bank[0][:, :], ACT.Copy).then_inc(btA, 1)
                    act.wait_ge(btr, 2 * g + 2)
                    act.activation(bt[g % 2][:, 1].rearrange("p q m -> p (q m)"), b_bank[1][:, :], ACT.Copy).then_inc(btV, 1)

                def gelu(g, p):
                    act.wait_ge(yd, g + 1)
                    if past(g, 2):
                        act.wait_ge(out[g % 2], 16 * GQ * (g // 2))
                    act.activation(yst[g % 2][:, :, :].rearrange("p q j -> p (q j)"), y_bank[g % 2][:, :], ACT.Gelu_apprx_tanh).then_inc(gel, 1)

                run(act, NG, [(0, trigonometry), (3, gelu), (1, inputs)], 2)

            @block.vector
            def _(dve):
                link = chain(dve, lv)
                dve.wait_ge(consts, 48)
                link(dve.tensor_scalar(g128[:, :], turns, float(C), None, ALU.mult))
                link(dve.tensor_scalar(g128r[:, :], g128[:, :], MAGIC, None, ALU.add))
                link(dve.tensor_scalar(g128r[:, :], g128r[:, :], MAGIC, None, ALU.subtract))
                link(dve.tensor_tensor(g128[:, :], g128[:, :], g128r[:, :], ALU.subtract))
                for x in st:
                    dve.memset(x[:, :, :, :, :], 0.0)
                link(dve.memset(uh[:, :, :, 0:1], 0.0))
                dve.tensor_scalar(r128[:, :], rate, float(C), None, ALU.mult).then_inc(decd, 1)

                def phases(g, p):
                    r = g % 3
                    if past(g, 1):
                        dve.wait_ge(phd, g)
                    dve.tensor_tensor(ph[:, :, 0:C + 1], bc(turns, g, C + 1), rc(ramp[:, :], C + 1), ALU.mult)
                    link(dve.tensor_tensor(ph[:, :, C + 1:TW], bc(g128, g, NC), rc(ramp[:, 0:NC], NC), ALU.mult))
                    link(dve.tensor_scalar(rd[:, :, :], ph[:, :, :], MAGIC, MAGIC, ALU.add, ALU.subtract))
                    if past(g, 3):
                        dve.wait_ge(stP, g - 2)
                    dve.tensor_tensor(sn[r][:, :, :], ph[:, :, :], rd[:, :, :], ALU.subtract).then_inc(phd, 1)

                def bases(g, p):
                    r = g % 3
                    dve.wait_ge(trig, g + 1)
                    if past(g, 1):
                        dve.wait_ge(gmP, g)
                        dve.wait_ge(btr, 2 * g)
                    link(dve.memset(ex[r][:, :, C + 1:C + 2], 0.0))
                    dve.tensor_tensor(er[:, 0], ex[r][:, :, 0:C + 1], cs[r][:, :, 0:C + 1], ALU.mult)
                    dve.tensor_tensor(er[:, 1], ex[r][:, :, 0:C + 1], sn[r][:, :, 0:C + 1], ALU.mult).then_inc(erd, 1)
                    dve.wait_ge(erd, g + 1)
                    if past(g, 3):
                        dve.wait_ge(yd, g - 2)
                    dve.tensor_tensor(tv[:, 0], er[:, 0, :, 0:C], bc(cre, g, C), ALU.mult)
                    link(dve.tensor_tensor(tv[:, 1], er[:, 1, :, 0:C], bc(cim, g, C), ALU.mult))
                    dve.tensor_tensor(gm[g % 3][:, 0], tv[:, 0], tv[:, 1], ALU.subtract).then_inc(gmV, 1)

                def tap_row(g, p):
                    dve.wait_ge(kcopied, g + 1)
                    dve.tensor_tensor(krow[g % 2][:, :, 0], krow[g % 2][:, :, 0], skip[:, qs(g)], ALU.add).then_inc(kr, 1)

                def scan(g, p):
                    r = g % 3
                    dve.wait_ge(ud, g + 1)
                    u = u_bank[g % 2][:, 0:2 * S].rearrange("p (r q c) -> p r q c", r=2, q=GQ)
                    R1, R = slice(C + 2, TW), slice(C + 1, TW)
                    for j, (tab, part) in enumerate(((cs, 0), (sn, 1), (cs, 1), (sn, 0))):
                        i = dve.tensor_tensor(w[:, j, :, 1:NC], tab[r][:, :, R1], u[:, part, :, 0:NC - 1], ALU.mult)
                    i.then_inc(uread, 1)
                    dve.wait_ge(uread, g + 1)
                    dve.tensor_tensor(uh[:, 0, :, 1:NC], w[:, 0, :, 1:NC], w[:, 1, :, 1:NC], ALU.add)
                    link(dve.tensor_tensor(uh[:, 1, :, 1:NC], w[:, 2, :, 1:NC], w[:, 3, :, 1:NC], ALU.subtract))
                    if past(g, 1):
                        dve.wait_ge(stP, g)
                    link(dve.tensor_copy(w[:, 0], ex[r][:, :, R]))
                    for part in range(2):
                        i = dve.tensor_tensor_scan(sh[:, part].rearrange("p q c -> p (q c)"), w[:, 0].rearrange("p q c -> p (q c)"),
                                                   uh[:, part].rearrange("p q c -> p (q c)"), 0.0, ALU.mult, ALU.add)
                    i.then_inc(scand, 1)
                    dve.wait_ge(scand, g + 1)
                    if past(g, 2):
                        dve.wait_ge(yd, g - 1)
                    dve.tensor_tensor(sw[:, 0], cs[r][:, :, R], sh[:, 0], ALU.mult)
                    link(dve.tensor_tensor(sw[:, 1], sn[r][:, :, R], sh[:, 1], ALU.mult))
                    for a in range(Q4):
                        R = slice(SN * a, SN * (a + 1))
                        i = dve.tensor_tensor(st[g % 2][R, 0, :, a], sw[R, 0], sw[R, 1], ALU.subtract)
                    i.then_inc(stV, 1)

                run(dve, NG, [(0, phases), (2, tap_row), (1, bases), (2, scan)], 2)

            @block.tensor
            def _(pe):
                pe.wait_ge(consts, 48)

                def tables(g, p):
                    pe.wait_ge(gmV, g + 1)
                    if past(g, 1):
                        pe.wait_ge(kcopied, g)
                    pe.matmul(taps_bank[0:Q4, :], quads[:, :], gm[g % 3][:, 0].rearrange("p q j -> p (q j)"), start=True, stop=True).then_inc(taps, 1)
                    for part, ev in ((0, btA), (1, btV)):
                        if past(g, 1):
                            pe.wait_ge(ev, g)
                        for q in range(GQ):
                            mm = pe.transpose(b_bank[part][:, q * P:(q + 1) * P], er[:, part, q, 1:C + 1], G.ident[:, :])
                        mm.then_inc(btr, 1)

                def inputs(g, p):
                    pe.wait_ge(btA, g + 1)
                    pe.wait_ge(btV, g + 1)
                    if past(g, 2):
                        pe.wait_ge(uread, g - 1)
                    for q in range(GQ):
                        for a in range(Q4):
                            for part in range(2):
                                mm = pe.matmul(u_bank[g % 2][SN * a:SN * (a + 1), (part * GQ + q) * NC:(part * GQ + q + 1) * NC],
                                               bt[g % 2][:, part, q, SN * a:SN * (a + 1)], Zr[:, (g * GQ + q) * Q4 + a], start=True, stop=True)
                    mm.then_inc(ud, 1)

                def outputs(g, p):
                    pe.wait_ge(tl[g % 2], 16 * (g // 2 + 1))
                    pe.wait_ge(gmP, g + 1)
                    pe.wait_ge(stV, g + 1)
                    pe.wait_ge(stP, g + 1)
                    if past(g, 2):
                        pe.wait_ge(gel, g - 1)
                    for q in range(GQ):
                        four = y_bank[g % 2][:, q * C:(q + 1) * C]
                        for part in range(2):
                            pe.matmul(four, st[g % 2][:, part, q].rearrange("p a c -> p (a c)"), gm[g % 3][:, part, q],
                                      start=(part == 0), stop=False)
                        for a in range(Q4):
                            mm = pe.matmul(four[NC * a:NC * (a + 1), :], Zr[:, (g * GQ + q) * Q4 + a], toep[g % 2][:, q * Q4 + a],
                                           start=False, stop=True)
                    mm.then_inc(yd, 1)

                run(pe, NG, [(2, inputs), (3, outputs), (1, tables)], 2)
        close()


def s4d_out_pass(nc, G, l, Y, H, finish=None):
    with ExitStack() as ctx:
        sb, sem, close = open_pass(nc, G, ctx)
        raw = sb("so_raw", [P, KD, 2 * D])
        wt = [sb(f"so_w_{n}", [P, KD, 2 * D], F32R) for n in ("hi", "lo")]
        y = [sb(f"so_y_{n}", [P, 2, KD, TT], F32R) for n in ("hi", "lo")]
        th = sb("so_th", [P, 2, KD, TT])
        hb = sb("so_hb", [P, KD])
        xin = sb("so_x", [P, 2, KD, TT])
        weights, whi, wlo, yhi, ylo, od, thd, res, o1r, hbd, xl0, xl1, stored, link_s = (
            sem("so_" + n) for n in ("weights", "whi", "wlo", "yhi", "ylo", "od", "thd", "res", "o1r", "hbd", "xl0", "xl1", "stored", "l"))
        xl = (xl0, xl1)
        o_bank = (G.bank[0:4], G.bank[4:8])
        b = G.col(f"s_b{l}")
        if finish:
            xs, xd = (G.io[n].rearrange("(k p) n -> p k n", p=P) for n in finish[0:2])
        with nc.Block() as block:
            @block.sync
            def _(sp):
                sp.dma_start(raw[:, :, :], G.io["s_W"][l].rearrange("(k p) n -> p k n", p=P)).then_inc(weights, 16)
                if finish:
                    for t in range(NT + 2):
                        if t >= 2:
                            sp.wait_ge(res, t - 1)
                            sp.dma_start(xd[:, :, tok(t - 2)], xin[:, t % 2]).then_inc(stored, 16)
                            sp.wait_ge(stored, 16 * (t - 1))
                        if t < NT:
                            sp.dma_start(xin[:, t % 2], xs[:, :, tok(t)]).then_inc(xl[t % 2], 16)

            @block.gpsimd
            def _(pool):
                def low(t, p):
                    pool.wait_ge(yhi, t + 1)
                    pool.tensor_tensor(y[1][:, p], Y[:, :, tok(t)], y[0][:, p], ALU.subtract).then_inc(ylo, 1)
                run(pool, NT, [(0, low)])

            @block.tensor
            def _(pe):
                def project(t, p):
                    if t == 0:
                        pe.wait_ge(wlo, 1)
                    pe.wait_ge(ylo, t + 1)
                    for m in (2, 3, 0, 1):
                        if past(t, 2):
                            pe.wait_ge(thd if m >= 2 else o1r, t - 1)
                        mm = product_of_parts(pe, o_bank[p][m][:, :], lambda a, k: wt[a][:, k, m * P:(m + 1) * P], lambda b, k: y[b][:, p, k], range(KD), KD)
                        if m in (3, 1):
                            mm.then_inc(od, 1)
                run(pe, NT, [(0, project)])

            @block.scalar
            def _(act):
                def high(t, p):
                    if past(t, 2):
                        act.wait_ge(od, 2 * (t - 1))
                    act.activation(y[0][:, p], Y[:, :, tok(t)], ACT.Copy).then_inc(yhi, 1)

                def weights_high(t, p):
                    if t == 0:
                        act.wait_ge(weights, 16)
                        act.activation(wt[0][:, :, :], raw[:, :, :], ACT.Copy).then_inc(whi, 1)

                def sigmoid(t, p):
                    if t == 0:
                        act.wait_ge(hbd, 1)
                    act.wait_ge(od, 2 * t + 1)
                    if past(t, 2):
                        act.wait_ge(res, t - 1)
                    for h in range(KD):
                        i = act.activation(th[:, p, h], o_bank[p][2 + h][:, :], ACT.Tanh, scale=0.5, bias=hb[:, h:h + 1])
                    i.then_inc(thd, 1)
                run(act, NT, [(0, high), (0, weights_high), (1, sigmoid)])

            @block.vector
            def _(dve):
                link = chain(dve, link_s)
                dve.tensor_scalar(hb[:, :], b[:, KD:2 * KD], 0.5, None, ALU.mult).then_inc(hbd, 1)
                dve.wait_ge(whi, 1)
                dve.tensor_tensor(wt[1][:, :, :], raw[:, :, :], wt[0][:, :, :], ALU.subtract).then_inc(wlo, 1)

                def residual(t, p):
                    dve.wait_ge(thd, t + 1)
                    link(dve.tensor_scalar(th[:, p], th[:, p], 1.0, 0.5, ALU.add, ALU.mult))
                    dve.wait_ge(od, 2 * t + 2)
                    for h in range(KD):
                        i = dve.scalar_tensor_tensor(th[:, p, h], o_bank[p][h][:, :], b[:, h:h + 1], th[:, p, h], ALU.add, ALU.mult)
                    i.then_inc(o1r, 1)
                    dve.wait_ge(o1r, t + 1)
                    i = dve.tensor_tensor(H[:, :, tok(t)], H[:, :, tok(t)], th[:, p], ALU.add)
                    if finish:
                        link(i)
                        dve.wait_ge(xl[p], 16 * (t // 2 + 1))
                        for h in range(KD):
                            i = dve.scalar_tensor_tensor(xin[:, p, h], H[:, h, tok(t)], finish[2][:, h:h + 1], xin[:, p, h], ALU.mult, ALU.add)
                    i.then_inc(res, 1)
                run(dve, NT, [(0, residual)])
        close()


def s4d_stage(nc, G, src, dst):
    with ExitStack() as ctx:
        sb = lambda n, s: ctx.enter_context(nc.sbuf_tensor(n, s, F32))
        H = sb("s_h", [P, KD, N])
        Z = sb("s_z", [P, KD, N])
        Zr = sb("s_zr", [P, D, NC])
        Hv = lambda k, t: H[:, k, tok(t)]
        Zv = lambda k, t: Z[:, k, tok(t)].rearrange("p (c j) -> p c j", j=C)[:, :, ::-1]
        ln_pass(nc, G, Hv, Hv, G.eps5[:, :], G.mod[:, 1, CA:CA + KD], G.mod[:, 1, SA:SA + KD], load=load_x(G, src, H))
        for l in range(NL):
            ln_pass(nc, G, Hv, Zv, G.eps5[:, :], G.col(f"s_ln_w{l}"), G.col(f"s_ln_b{l}"), turn=(Z, Zr))
            convolution_pass(nc, G, l, G.s4d.prm, Zr, Z)
            s4d_out_pass(nc, G, l, Z, H, (src, dst, G.mod[:, 1, GA:GA + KD]) if l == NL - 1 else None)


class FfnWeights:
    PER_STEP = 3
    RAW = 6

    def __init__(self, nc, G, ctx):
        self.G, MF = G, FF // P
        make = lambda n, k, w: ctx.enter_context(nc.sbuf_tensor("ff_" + n, [P, k, w], F32R))
        self.w = {"w1": make("w1", KD, FF), "w2": make("w2", KD, FF), "h1": make("h1", MF, FF), "h2": make("h2", MF, FF), "w3": make("w3", MF, D)}
        self.inexact = ctx.enter_context(nc.sbuf_tensor("ff_inexact", [P, 1], I32))
        self.chunks = [(n, k, 1) for n in ("w1", "w2", "h1", "h2") for k in range(self.w[n].shape[1])] + [("w3", k, FF // D) for k in range(0, MF, FF // D)]

    def open(self, sb, sem):
        self.raw = [sb(f"raw{i}", [P, FF]) for i in range(self.RAW)]
        self.rest = [sb(f"rest{i}", [P, FF]) for i in range(3)]
        self.lost = sb("lost", [P, len(self.chunks)])
        self.any_lost = sb("any_lost", [P, 1])
        self.raw_loaded = [sem(f"raw_loaded{i}") for i in range(self.RAW)]
        self.rounded, self.rest_ready, self.summed, self.any_ready, self.count_ready, self.known = (
            sem("f_" + n) for n in ("rounded", "rest_ready", "summed", "any_ready", "count_ready", "known"))

    def of_step(self, t):
        return [(c, self.chunks[c]) for c in range(t * self.PER_STEP, min((t + 1) * self.PER_STEP, len(self.chunks)))]

    def rows(self, chunk, b):
        name, k, n = chunk
        return b[:, k] if n == 1 else b[:, k:k + n].rearrange("p k n -> p (k n)")

    def load(self, sp, t):
        for c, (name, k, n) in self.of_step(t):
            if c >= self.RAW:
                sp.wait_ge(self.rest_ready, c - self.RAW + 1)
            src = self.G.io["g_" + name].rearrange("(k p) n -> p k n", p=P)[:, k:k + n]
            sp.dma_start(self.raw[c % self.RAW][:, :].rearrange("p (k n) -> p k n", k=n), src).then_inc(self.raw_loaded[c % self.RAW], 16)

    def round(self, act, t):
        for c, chunk in self.of_step(t):
            act.wait_ge(self.raw_loaded[c % self.RAW], 16 * (c // self.RAW + 1))
            act.activation(self.rows(chunk, self.w[chunk[0]]), self.raw[c % self.RAW][:, :], ACT.Copy).then_inc(self.rounded, 1)

    def subtract(self, dve, t):
        for c, chunk in self.of_step(t):
            dve.wait_ge(self.rounded, c + 1)
            if c >= 3:
                dve.wait_ge(self.summed, c - 2)
            dve.tensor_tensor(self.rest[c % 3][:, :], self.raw[c % self.RAW][:, :], self.rows(chunk, self.w[chunk[0]]), ALU.subtract).then_inc(self.rest_ready, 1)

    def sum_rests(self, act, t):
        for c, chunk in self.of_step(t):
            act.wait_ge(self.rest_ready, c + 1)
            act.activation(self.rest[c % 3][:, :], self.rest[c % 3][:, :], ACT.Abs, accum_out=self.lost[:, c:c + 1]).then_inc(self.summed, 1)

    def decide(self, dve):
        dve.wait_ge(self.summed, len(self.chunks))
        dve.tensor_reduce(self.any_lost[:, :], self.lost[:, :], AX.X, ALU.add).then_inc(self.any_ready, 1)
        dve.wait_ge(self.any_ready, 1)
        dve.tensor_scalar(self.any_lost[:, :], self.any_lost[:, :], 0.0, None, ALU.not_equal).then_inc(self.any_ready, 1)
        dve.wait_ge(self.count_ready, 1)
        dve.tensor_scalar(self.inexact[:, :], self.G.bank[4][:, 0:1], 0.0, None, ALU.not_equal).then_inc(self.known, 1)

    def count(self, pe):
        pe.wait_ge(self.any_ready, 2)
        pe.matmul(self.G.bank[4][:, 0:1], self.G.mean_w[:, :], self.any_lost[:, :], start=True, stop=True).then_inc(self.count_ready, 1)


def ffn_pass(nc, G, F, src, dst):
    MF = FF // P
    with ExitStack() as ctx:
        sb, sem, close = open_pass(nc, G, ctx)
        s32 = sb("s32", [P, KD, TT])
        S, U, V = ([sb(f"{n}_{part}", [P, k, TT], F32R) for part in ("hi", "lo")] for n, k in (("s", KD), ("u", MF), ("v", MF)))
        gated = sb("gated", [P, 2, TT])
        whole = sb("whole", [P, 2, TT])
        whole_u = sb("whole_u", [P, 2, TT])
        xin = sb("xin", [P, KD, TT])
        out_scale = sb("out_scale", [P, KD])
        block_buf = [sb(f"weight_block{i}", [P, MF, P]) for i in range(2)]
        w1d, w2d, silud, hid, lod, evac, h1d, h2d, w3d, res, xload, stored, scaled, sload, shi, slo, block_used = (
            sem("f_" + n) for n in ("w1d", "w2d", "silud", "hid", "lod", "evac", "h1d", "h2d", "w3d", "res", "xload", "stored",
                                    "scaled", "sload", "shi", "slo", "block_used"))
        block_loaded = [sem(f"block_loaded{i}") for i in range(2)]
        pair = (G.bank[0:2], G.bank[2:4])
        hidden_bank = G.bank[4:6] + G.bank[2:4]
        out_bank = G.bank[6:8]
        gate = G.mod[:, 1, GB:GB + KD]
        s1, s2, sh1, sh2, s3 = (G.col(n) for n in ("w1_s", "w2_s", "h1_s", "h2_s", "w3_s"))
        feat = lambda n: G.io[n].rearrange("(k p) n -> p k n", p=P)
        xs, xd, sd = feat(src), feat(dst), feat("s3")
        blocks = ([(n, m) for m in range(MF) for n in ("w1", "w2")] + [("h1", m) for m in range(MF)]
                  + [("h2", m) for m in range(MF)] + [("w3", m) for m in range(KD)])
        number = {b: i for i, b in enumerate(blocks)}
        parts = 3 * MF
        with nc.Block() as block:
            @block.sync
            def _(sp):
                def load_s(t):
                    if t >= 1:
                        sp.wait_ge(slo, t)
                    sp.dma_start(s32[:, :, :], sd[:, :, tok(t)]).then_inc(sload, 16)

                def tiles(general):
                    load_s(0)
                    for t in range(NT):
                        if t >= 1:
                            sp.wait_ge(stored, 16 * t)
                        sp.dma_start(xin[:, :, :], xs[:, :, tok(t)]).then_inc(xload, 16)
                        if t + 1 < NT:
                            load_s(t + 1)
                        if general:
                            for i, (name, m) in enumerate(blocks):
                                n = t * len(blocks) + i
                                if n >= 2:
                                    sp.wait_ge(block_used, n - 1)
                                K = F.w[name].shape[1]
                                sp.dma_start(block_buf[n % 2][:, 0:K], feat("g_" + name)[:, :, m * P:(m + 1) * P]).then_inc(block_loaded[n % 2], 16)
                        sp.wait_ge(res, t + 1)
                        sp.dma_start(xd[:, :, tok(t)], xin[:, :, :]).then_inc(stored, 16)
                    sp.wait_ge(stored, 16 * NT)

                inexact = sp.value_load(F.inexact[0:1, 0:1], min_val=0, max_val=1)
                with sp.If(inexact == 0):
                    tiles(False)
                with sp.Else():
                    tiles(True)

            @block.tensor
            def _(pe):
                def first_waits(t, m):
                    if m == 0:
                        pe.wait_ge(slo, t + 1)
                    n = t * MF + m
                    if t >= 1 and m == 1:
                        pe.wait_ge(evac, 2 * t * MF)
                    if n >= 2:
                        pe.wait_ge(hid, n - 1)

                def free_bank(t, m, layer):
                    n = (2 * t + layer) * MF + m
                    if n >= 4:
                        pe.wait_ge(evac, n - 3)

                def part_ready(t, layer, k):
                    pe.wait_ge(lod, t * parts + layer * MF + k + 1)

                def exact(t):
                    def product(out, name, m, act_parts, ks, K):
                        for k in ks:
                            for j in range(2):
                                mm = pe.matmul(out[:, :], F.w[name][:, k, m * P:(m + 1) * P], act_parts[j][:, k], start=(k == 0 and j == 0), stop=(k == K - 1 and j == 1))
                        return mm

                    for m in range(MF):
                        first_waits(t, m)
                        product(pair[m % 2][0], "w1", m, S, range(KD), KD).then_inc(w1d, 1)
                        product(pair[m % 2][1], "w2", m, S, range(KD), KD).then_inc(w2d, 1)
                    for layer, name, source, done in ((0, "h1", U, h1d), (1, "h2", V, h2d)):
                        for m in range(2):
                            free_bank(t, m, layer)
                            for k in range(MF - 1):
                                if m == 0:
                                    part_ready(t, layer, k)
                                product(hidden_bank[m], name, m, source, [k], MF)
                        part_ready(t, layer, MF - 1)
                        for m in range(2):
                            product(hidden_bank[m], name, m, source, [MF - 1], MF).then_inc(done, 1)
                        for m in range(2, MF):
                            free_bank(t, m, layer)
                            product(hidden_bank[m % 4], name, m, source, range(MF), MF).then_inc(done, 1)
                    if t >= 1:
                        pe.wait_ge(res, t)
                    for m in range(KD):
                        for k in range(MF - 1):
                            if m == 0:
                                part_ready(t, 2, k)
                            product(out_bank[m], "w3", m, U, [k], MF)
                    part_ready(t, 2, MF - 1)
                    for m in range(KD):
                        mm = product(out_bank[m], "w3", m, U, [MF - 1], MF)
                    mm.then_inc(w3d, 1)

                def general(t):
                    def product(out, name, m, act_parts, K):
                        n = t * len(blocks) + number[name, m]
                        pe.wait_ge(block_loaded[n % 2], 16 * (n // 2 + 1))
                        for k in range(K):
                            for j in range(2):
                                mm = pe.matmul(out[:, :], block_buf[n % 2][:, k], act_parts[j][:, k].bitcast(F32), start=(k == 0 and j == 0), stop=(k == K - 1 and j == 1))
                        mm.then_inc(block_used, 1)
                        return n + 1

                    def signal(done, n):
                        pe.wait_ge(block_used, n)
                        pe.sem_inc(done, 1)

                    for m in range(MF):
                        first_waits(t, m)
                        for j, (name, done) in enumerate((("w1", w1d), ("w2", w2d))):
                            signal(done, product(pair[m % 2][j], name, m, S, KD))
                    for layer, name, source, done in ((0, "h1", U, h1d), (1, "h2", V, h2d)):
                        part_ready(t, layer, MF - 1)
                        for m in range(MF):
                            free_bank(t, m, layer)
                            signal(done, product(hidden_bank[m % 4], name, m, source, MF))
                    if t >= 1:
                        pe.wait_ge(res, t)
                    part_ready(t, 2, MF - 1)
                    for m in range(KD):
                        n = product(out_bank[m], "w3", m, U, MF)
                    signal(w3d, n)

                inexact = pe.value_load(F.inexact[0:1, 0:1], min_val=0, max_val=1)
                with pe.If(inexact == 0):
                    for t in range(NT):
                        exact(t)
                with pe.Else():
                    for t in range(NT):
                        general(t)

            @block.scalar
            def _(act):
                for t in range(NT):
                    for m in range(MF):
                        n = t * MF + m
                        act.wait_ge(w1d, n + 1)
                        if n >= 2:
                            act.wait_ge(hid, n - 1)
                        act.activation(gated[:, m % 2], pair[m % 2][0][:, :], ACT.Silu, scale=s1[:, m:m + 1]).then_inc(silud, 1)
                    for layer, done, scale, (hi, _) in ((0, h1d, sh1, V), (1, h2d, sh2, U)):
                        for m in range(MF):
                            n = (2 * t + layer) * MF + m
                            act.wait_ge(done, t * MF + m + 1)
                            act.activation(hi[:, m], hidden_bank[m % 4][:, :], ACT.Gelu, scale=scale[:, m:m + 1])
                            if n >= 2:
                                before = n - 2
                                act.wait_ge(lod, (before // (2 * MF)) * parts + MF + before % (2 * MF) + 1)
                            act.activation(whole[:, m % 2], hidden_bank[m % 4][:, :], ACT.Gelu, scale=scale[:, m:m + 1]).then_inc(evac, 1)

            @block.vector
            def _(dve):
                dve.tensor_tensor(out_scale[:, :], gate, s3, ALU.mult).then_inc(scaled, 1)
                dve.wait_ge(scaled, 1)

                def split_s(t):
                    dve.wait_ge(sload, 16 * (t + 1))
                    if t >= 1:
                        dve.wait_ge(w2d, t * MF)
                    dve.tensor_copy(S[0][:, :, :], s32[:, :, :]).then_inc(shi, 1)
                    dve.wait_ge(shi, t + 1)
                    dve.tensor_tensor(S[1][:, :, :], s32[:, :, :], S[0][:, :, :], ALU.subtract).then_inc(slo, 1)

                split_s(0)
                for t in range(NT):
                    if t >= 1:
                        dve.wait_ge(w3d, t)
                    for m in range(MF + 1):
                        if m < MF:
                            n = t * MF + m
                            dve.wait_ge(silud, n + 1)
                            dve.wait_ge(w2d, n + 1)
                            if n >= 2:
                                dve.wait_ge(lod, ((n - 2) // MF) * parts + (n - 2) % MF + 1)
                            for out in (U[0][:, m], whole_u[:, m % 2]):
                                i = dve.scalar_tensor_tensor(out, pair[m % 2][1][:, :], s2[:, m:m + 1], gated[:, m % 2], ALU.mult, ALU.mult)
                            i.then_inc(hid, 1)
                        if m >= 1:
                            dve.wait_ge(hid, t * MF + m)
                            dve.tensor_tensor(U[1][:, m - 1], whole_u[:, (m - 1) % 2], U[0][:, m - 1], ALU.subtract).then_inc(lod, 1)
                    for layer, (hi, lo) in ((0, V), (1, U)):
                        for m in range(MF):
                            dve.wait_ge(evac, (2 * t + layer) * MF + m + 1)
                            dve.tensor_tensor(lo[:, m], whole[:, m % 2], hi[:, m], ALU.subtract).then_inc(lod, 1)
                        if layer == 0 and t + 1 < NT:
                            split_s(t + 1)
                    dve.wait_ge(w3d, t + 1)
                    dve.wait_ge(xload, 16 * (t + 1))
                    for h in range(KD):
                        i = dve.scalar_tensor_tensor(xin[:, h], out_bank[h][:, :], out_scale[:, h:h + 1], xin[:, h], ALU.mult, ALU.add)
                    i.then_inc(res, 1)
        close()


def ffn_stage(nc, G, src, dst):
    with ExitStack() as ctx:
        F = FfnWeights(nc, G, ctx)
        with ExitStack() as inner:
            S = inner.enter_context(nc.sbuf_tensor("ff_s", [P, KD, N], F32))
            Sv = lambda k, t: S[:, k, tok(t)]
            ln_pass(nc, G, Sv, Sv, G.eps5[:, :], G.mod[:, 1, CB:CB + KD], G.mod[:, 1, SB:SB + KD], load=load_x(G, src, S), also=F, store=(S, "s3"))
        ffn_pass(nc, G, F, src, dst)


def program(nc, io, stages="0123"):
    G = Shared()
    G.io, G.passes = io, 0
    with ExitStack() as ctx:
        sb = lambda name, shape, dt=F32: ctx.enter_context(nc.sbuf_tensor(name, shape, dt))
        G.cols = sb("cols", [P, NCOLS])
        G.ident = sb("ident", [P, P])
        G.mean_w = sb("mean_w", [P, P])
        G.mod = sb("mod", [P, 2, 12])
        G.eps3, G.eps5, G.half_pi = sb("eps3", [P, 1]), sb("eps5", [P, 1]), sb("half_pi", [P, 1])
        G.bank = [ctx.enter_context(nc.psum_tensor(f"bank{i}", [P, TT], F32)) for i in range(8)]
        G.col = lambda name: G.cols[:, COLS[name][0]:COLS[name][0] + COLS[name][1]]
        G.s4d = S4dParams(nc, G, ctx)
        setup_pass(nc, G)
        for s, stage in (("0", rwkv_stage), ("1", local_attention_stage), ("2", s4d_stage), ("3", ffn_stage)):
            if s in stages:
                stage(nc, G, f"x{s}", f"x{int(s) + 1}")


def constants():
    import numpy as np
    c = {"ident": np.eye(P, dtype=np.float32)}
    i, j = np.arange(W)[:, None], np.arange(W)[None, :]
    now, before, never = (np.where(m, 0.0, -1e30) for m in (j <= i, j >= i, np.zeros((W, W), bool)))
    c["masks"] = np.stack([np.concatenate(m, 1) for m in ((now, before), (before, now), (now, never))], 1).astype(np.float32)
    half = np.arange(0, DH, 2, dtype=np.float32)
    inv = (1.0 / np.power(np.float32(10000.0), half / np.float32(DH))).astype(np.float32)
    t = np.arange(N, dtype=np.float32)
    fr = np.tile((t[:, None] * inv[None, :]).astype(np.float32), (1, 2)).astype(np.float64)
    base = (half + 0.4 * DH) / (1.4 * DH)
    sc = np.tile(base[None, :] ** ((t - N // 2) / float(W // 2))[:, None], (1, 2)).astype(np.float64)
    sign = np.where(np.arange(DH) < DH // 2, -1.0, 1.0)[None, :]
    rot = np.stack([np.cos(fr) * sc * 8.0, np.sin(fr) * sc * 8.0 * sign, np.cos(fr) / sc, np.sin(fr) / sc * sign], 1)
    c["rotary"] = np.ascontiguousarray(rot.astype(np.float32).reshape(NW, W, 4, DH))
    c["ramp"] = np.ascontiguousarray(np.broadcast_to(np.arange(C + 1, dtype=np.float32), (P, C + 1)))
    c["quads"] = np.ascontiguousarray((np.arange(P)[:, None] // SN == np.arange(Q4)[None, :]).astype(np.float32))
    return c


def lay_out(inp):
    import numpy as np
    a = {}

    def per_feature(v, n):
        v = np.asarray(v)
        full = np.zeros((n * P,), v.dtype)
        full[:v.shape[0]] = v
        return full.reshape(n, P).T

    vec = {}
    for k in ("ln1_g", "ln1_b", "ln2_g", "ln2_b", "tm_mix_k", "tm_mix_v", "tm_mix_r", "time_decay", "time_first", "cm_mix_k", "cm_mix_r"):
        vec[k] = inp["L0_attn_" + k]
    vec["c0"], vec["c1"] = inp["L0_c"][0], inp["L1_c"][0]
    for l in range(DEPTH):
        vec[f"f_ln_g{l}"], vec[f"f_ln_b{l}"] = inp["L0_ffn_ln_g"][l], inp["L0_ffn_ln_b"][l]
        vec[f"f_b1a{l}"], vec[f"f_b1g{l}"] = inp["L0_ffn_b1"][l][:HID], inp["L0_ffn_b1"][l][HID:]
        vec[f"f_b2{l}"] = inp["L0_ffn_b2"][l]
    for l in range(NL):
        vec[f"s_ln_w{l}"], vec[f"s_ln_b{l}"] = inp["L1_attn_ln_w"][l], inp["L1_attn_ln_b"][l]
        vec[f"s_b{l}"] = inp["L1_attn_b_out"][l]
    for k in ("w1_s", "w2_s", "h1_s", "h2_s", "w3_s"):
        vec[k] = inp["L1_ffn_" + k]
    a["cols"] = np.ascontiguousarray(np.concatenate([per_feature(vec[k], COLS[k][1]) for k in COLS], axis=1))
    a["wmod0"], a["wmod1"] = inp["L0_wmod"], inp["L1_wmod"]
    for k in ("tm_Wk", "tm_Wv", "tm_Wr", "Wo", "cm_Wk", "cm_Wv", "cm_Wr"):
        a[k] = inp["L0_attn_" + k]
    for k in ("wqkv", "q_scale", "k_scale", "wo", "w1", "w2"):
        a[k] = inp["L0_ffn_" + k]

    def by_quads(v, axis_n=True):
        v = np.asarray(v)
        if not axis_n:
            v = np.broadcast_to(v[:, :, None], (NL, D, SN))
        return np.ascontiguousarray(v.reshape(NL, HQ, Q4, SN).transpose(2, 3, 0, 1).reshape(P, NL, HQ))

    a["s_log_dt"] = by_quads(inp["L1_attn_log_dt"], False)
    for k in ("A_re_log", "A_im", "C_re", "C_im"):
        a["s_" + k] = by_quads(inp["L1_attn_" + k])
    a["s_D"] = np.ascontiguousarray(np.asarray(inp["L1_attn_D_skip"]).reshape(NL, HQ, Q4).transpose(2, 0, 1))
    a["s_W"] = np.ascontiguousarray(np.asarray(inp["L1_attn_W_out"]).transpose(0, 2, 1))
    for k in ("w1", "w2", "h1", "h2", "w3"):
        a["g_" + k] = np.ascontiguousarray(np.asarray(inp[f"L1_ffn_{k}_w"]).T)
    a.update(constants())
    return {k: np.ascontiguousarray(v) for k, v in a.items()}


def kernel(**inputs):
    import numpy as np
    import concourse.bacc as bacc
    from concourse.bass_utils import run_bass_kernel_spmd

    nc = bacc.Bacc("TRN2", target_bir_lowering=False, num_devices=1)
    arrays = {"in_" + k: v for k, v in lay_out({k: np.asarray(v) for k, v in inputs.items()}).items()}
    arrays["in_x0"] = np.ascontiguousarray(np.asarray(inputs["L0_attn_inputs"])[0].T)
    io = {k[3:]: nc.dram_tensor(k, v.shape, mybir.dt.from_np(v.dtype), kind="ExternalInput").ap() for k, v in arrays.items()}
    for s in (1, 2, 3):
        io[f"x{s}"] = nc.dram_tensor(f"x{s}", [D, N], F32, kind="Internal").ap()
    io["s3"] = nc.dram_tensor("s3", [D, N], F32, kind="Internal").ap()
    io["taps"] = nc.dram_tensor("taps", [HQ, Q4, 2 * C], F32, kind="Internal").ap()
    io["x4"] = nc.dram_tensor("out_x", [D, N], F32, kind="ExternalOutput").ap()
    program(nc, io)
    r = run_bass_kernel_spmd(nc, [arrays], core_ids=[0])
    return np.ascontiguousarray(r.results[0]["out_x"].T)[None]
```
